# Optimizing a Trainium2 kernel written in Bass

```python
import numpy as np
import jax
import jax.numpy as jnp

def _softmax(x, axis=-1):
    return jax.nn.softmax(x, axis=axis)

def _gelu(x):
    return jax.nn.gelu(x, approximate=True)

def _silu(x):
    return jax.nn.silu(x)

def _sigmoid(x):
    return jax.nn.sigmoid(x)

def _layernorm(x, axis=-1, eps=1e-05):
    m = jnp.mean(x, axis=axis, keepdims=True)
    v = jnp.var(x, axis=axis, keepdims=True)
    return (x - m) / jnp.sqrt(v + eps)

def _scatter_add(tgt, idx, src, axis=0):
    return tgt.at[idx].add(src)

def _segment_sum(src, seg, n):
    return jax.ops.segment_sum(src, seg, n)
kernel_name = 'mk_adj_ffn_d4_adj_r2_dc709f'

def setup_inputs(seed: int=0):
    np.random.seed(seed)
    _w = jnp.asarray

    def _rec_inputs():
        import jax
        import jax.numpy as jnp
        _gk = jax.random.key(seed)
        x = -0.0005207 + 1.001 * jax.random.normal(jax.random.fold_in(_gk, 1), (128, 64, 128), jnp.float32)
        _w = (1.0 + jnp.arange(64, dtype=jnp.float32)) ** (-0.5)
        _w = _w / _w.mean()
        _pij = jnp.clip(0.0625 * _w[:, None] * _w[None, :], 0.0, 1.0)
        _a = jax.random.uniform(jax.random.fold_in(_gk, 2), (128, 64, 64)) < _pij
        _a = jnp.logical_or(_a, jnp.eye(64, dtype=bool))
        _af = _a.astype(jnp.float32)
        _af = _af * jax.random.uniform(jax.random.fold_in(_gk, 3), (128, 64, 64), jnp.float32, 0.05, 1)
        adj = _af
        _nm = jnp.ones((128, 64), dtype=bool)
        nodemask = jnp.where(_nm, 1.0, 0.0).astype(jnp.float32)
        return (x, adj, nodemask)
    x, adj, nodemask = _rec_inputs()

    def _L0_gnn_setup():
        import math
        import jax, jax.numpy as jnp
        import numpy as np
        HIDDEN = 128
        HEADS = 8
        HEAD_DIM = HIDDEN // HEADS
        key = jax.random.key(seed)
        ks = jax.random.split(key, 8)
        b, n = (2, 2048)
        node_state = jax.random.normal(ks[0], (b, n, HIDDEN), dtype=jnp.float32)
        adjacency = jax.random.uniform(ks[1], (b, n, n), dtype=jnp.float32)
        s = 1.0 / math.sqrt(HIDDEN)
        Wq = jax.random.uniform(ks[2], (HIDDEN, HIDDEN), jnp.float32, -s, s)
        Wk = jax.random.uniform(ks[3], (HIDDEN, HIDDEN), jnp.float32, -s, s)
        Wv = jax.random.uniform(ks[4], (HIDDEN, HIDDEN), jnp.float32, -s, s)
        Wo = jax.random.uniform(ks[5], (HIDDEN, HIDDEN), jnp.float32, -s, s)
        bo = jax.random.uniform(ks[6], (HIDDEN,), jnp.float32, -s, s)
        return {'node_state': node_state, 'adjacency': adjacency, 'Wq': Wq, 'Wk': Wk, 'Wv': Wv, 'Wo': Wo, 'bo': bo}
    _L0_gnn_all = _L0_gnn_setup()
    _L0_gnn_in = {k: v for k, v in _L0_gnn_all.items() if k in ('Wq', 'Wk', 'Wv', 'Wo', 'bo')}
    del _L0_gnn_all

    def _L0_ffn_setup():
        import math
        import jax, jax.numpy as jnp
        import numpy as np
        CAPACITY_FACTOR = 1.25
        key = jax.random.key(seed)
        ks = jax.random.split(key, 5)
        B, L, D, F, E = (8, 4096, 128, 512, 8)
        h = jax.random.normal(ks[0], (B, L, D), dtype=jnp.float32)
        gate_w = jax.random.normal(ks[1], (D, E), dtype=jnp.float32) * 0.02
        gate_b = jnp.zeros((E,), dtype=jnp.float32)
        w1 = jax.random.normal(ks[2], (E, D, F), dtype=jnp.float32) * (1.0 / math.sqrt(D))
        b1 = jnp.zeros((E, F), dtype=jnp.float32)
        w2 = jax.random.normal(ks[3], (E, F, D), dtype=jnp.float32) * (1.0 / math.sqrt(F))
        b2 = jnp.zeros((E, D), dtype=jnp.float32)
        return {'h': h, 'gate_w': gate_w, 'gate_b': gate_b, 'w1': w1, 'b1': b1, 'w2': w2, 'b2': b2}
    _L0_ffn_all = _L0_ffn_setup()
    _L0_ffn_in = {k: v for k, v in _L0_ffn_all.items() if k in ('gate_w', 'gate_b', 'w1', 'b1', 'w2', 'b2')}
    del _L0_ffn_all

    def _L1_gnn_setup():
        import jax, jax.numpy as jnp
        import numpy as np
        GROUPS = [list(range(25)), [0, 1, 2, 3, 4, 5, 6, 7, 8], [0, 9, 10, 11, 12, 13, 14], [6, 7, 8, 12, 13, 14], [3, 4, 5, 9, 10, 11]]
        B, N, D_IN, D_HID = (4096, 25, 128, 256)

        def _graph_conv(x, adj, W, b):
            n = adj.shape[-1]
            A = adj + jnp.eye(n, dtype=adj.dtype)
            deg = jnp.sum(A, axis=-1)
            deg_safe = jnp.where(deg == 0, 1.0, deg)
            dinv = jnp.where(deg == 0, 0.0, deg_safe ** (-0.5))
            norm_adj = dinv[:, :, None] * A * dinv[:, None, :]
            support = jnp.einsum('bnd,de->bne', x, W)
            out = jnp.einsum('bnm,bme->bne', norm_adj, support) + b
            return jax.nn.relu(out)
        key = jax.random.key(seed)
        ks = jax.random.split(key, 7)
        s1 = float(np.sqrt(6.0 / (D_IN + D_HID)))
        s2 = float(np.sqrt(6.0 / (D_HID + D_IN)))
        return {'x': jax.random.normal(ks[0], (B, N, D_IN), dtype=jnp.float32), 'adj': jax.random.uniform(ks[1], (B, N, N), dtype=jnp.float32), 'W1': jax.random.uniform(ks[2], (5, D_IN, D_HID), jnp.float32, -s1, s1), 'b1': jnp.zeros((5, D_HID), dtype=jnp.float32), 'W2': jax.random.uniform(ks[3], (5, D_HID, D_IN), jnp.float32, -s2, s2), 'b2': jnp.zeros((5, D_IN), dtype=jnp.float32), 'fusion_w': jnp.ones((5,), dtype=jnp.float32)}
    _L1_gnn_all = _L1_gnn_setup()
    _L1_gnn_in = {k: v for k, v in _L1_gnn_all.items() if k in ('W1', 'b1', 'W2', 'b2', 'fusion_w')}
    del _L1_gnn_all

    def _L1_ffn_setup():
        import jax, jax.numpy as jnp
        import numpy as np
        B, T, IN_DIM = (64, 128, 128)
        HID, OUT_DIM = (256, 128)
        N_LAYERS, N_EXPERTS, N_SHARED = (2, 16, 1)
        key = jax.random.key(seed)
        ks = jax.random.split(key, 10)
        s = 0.02
        x = jax.random.normal(ks[0], (B, T, IN_DIM), dtype=jnp.float32)
        route_id = jax.random.randint(ks[1], (B,), 0, N_EXPERTS)
        Wi = jax.random.normal(ks[2], (HID, IN_DIM), dtype=jnp.float32) * s
        bi = jnp.zeros((HID,), dtype=jnp.float32)
        Wr = jax.random.normal(ks[3], (N_LAYERS, N_EXPERTS, HID, HID), dtype=jnp.float32) * s
        br = jax.random.normal(ks[4], (N_LAYERS, N_EXPERTS, HID), dtype=jnp.float32) * s
        Ws = jax.random.normal(ks[5], (N_LAYERS, N_SHARED, HID, HID), dtype=jnp.float32) * s
        bs = jax.random.normal(ks[6], (N_LAYERS, N_SHARED, HID), dtype=jnp.float32) * s
        Wo = jax.random.normal(ks[7], (OUT_DIM, HID), dtype=jnp.float32) * s
        bo = jnp.zeros((OUT_DIM,), dtype=jnp.float32)
        return {'x': x, 'route_id': route_id, 'Wi': Wi, 'bi': bi, 'Wr': Wr, 'br': br, 'Ws': Ws, 'bs': bs, 'Wo': Wo, 'bo': bo}
    _L1_ffn_all = _L1_ffn_setup()
    _L1_ffn_in = {k: v for k, v in _L1_ffn_all.items() if k in ('route_id', 'Wi', 'bi', 'Wr', 'br', 'Ws', 'bs', 'Wo', 'bo')}
    del _L1_ffn_all

    def _L2_gnn_setup():
        import jax, jax.numpy as jnp
        import numpy as np
        ALPHA = 0.2
        NEG_INF = -9000000000000000.0
        key = jax.random.key(seed)
        kw, ka, k1, k2, k3 = jax.random.split(key, 5)
        B, N1, N2, F, O = (4, 1024, 1024, 128, 128)
        word = jax.random.normal(kw, (B, N2, F), dtype=jnp.float32)
        adj = jax.random.randint(ka, (B, N1, N2), 0, 2).astype(jnp.float32)
        stdv = 1.0 / np.sqrt(O)
        W1 = jax.random.uniform(k1, (F, O), jnp.float32, -stdv, stdv)
        W2 = jax.random.uniform(k2, (F, O), jnp.float32, -stdv, stdv)
        w3 = jax.random.uniform(k3, (2 * O, 1), jnp.float32, -stdv, stdv)
        return {'word': word, 'adj': adj, 'W1': W1, 'W2': W2, 'w3': w3}
    _L2_gnn_all = _L2_gnn_setup()
    _L2_gnn_in = {k: v for k, v in _L2_gnn_all.items() if k in ('W1', 'W2', 'w3')}
    del _L2_gnn_all

    def _L2_ffn_setup():
        import jax, jax.numpy as jnp
        import numpy as np
        N_EXPERTS = 8
        TOP_K = 2
        key = jax.random.key(seed)
        ks = jax.random.split(key, 5)
        B, T, C, E, H = (8, 1024, 128, 8, 341)
        scale = 1.0 / np.sqrt(C)
        return {'x': jax.random.normal(ks[0], (B, T, C), dtype=jnp.float32), 'router_w': jax.random.normal(ks[1], (E, C), dtype=jnp.float32) * scale, 'w1': jax.random.normal(ks[2], (E, H, C), dtype=jnp.float32) * scale, 'w2': jax.random.normal(ks[3], (E, C, H), dtype=jnp.float32) * (1.0 / np.sqrt(H)), 'w3': jax.random.normal(ks[4], (E, H, C), dtype=jnp.float32) * scale}
    _L2_ffn_all = _L2_ffn_setup()
    _L2_ffn_in = {k: v for k, v in _L2_ffn_all.items() if k in ('router_w', 'w1', 'w2', 'w3')}
    del _L2_ffn_all

    def _L3_gnn_setup():
        import jax, jax.numpy as jnp
        import numpy as np
        EPS = 1e-08
        key = jax.random.key(seed)
        kH, kA, kW = jax.random.split(key, 3)
        B, N, IN, OUT = (32, 256, 128, 128)
        H = jax.random.normal(kH, (B, N, IN), dtype=jnp.float32)
        A = jax.random.uniform(kA, (B, N, N), dtype=jnp.float32)
        mask = jnp.ones((B, N), dtype=jnp.float32)
        W = jax.random.normal(kW, (OUT, IN), dtype=jnp.float32) * (1.0 / np.sqrt(IN))
        b = jnp.zeros((OUT,), dtype=jnp.float32)
        return {'H': H, 'A': A, 'mask': mask, 'W': W, 'b': b}
    _L3_gnn_all = _L3_gnn_setup()
    _L3_gnn_in = {k: v for k, v in _L3_gnn_all.items() if k in ('W', 'b')}
    del _L3_gnn_all

    def _L3_ffn_setup():
        import jax, jax.numpy as jnp
        import numpy as np
        E = 8
        K = 2
        D = 128
        H = 256
        DOUT = 128
        EPS = 1e-05
        key = jax.random.key(seed)
        ks = jax.random.split(key, 9)
        s = 0.02
        return {'x': jax.random.normal(ks[0], (4, 4096, D), jnp.float32), 'gamma': 1.0 + 0.05 * jax.random.normal(ks[1], (D,), jnp.float32), 'beta': 0.05 * jax.random.normal(ks[2], (D,), jnp.float32), 'Wr': 0.01 * jax.random.normal(ks[3], (D, E), jnp.float32), 'br': jnp.zeros((E,), jnp.float32), 'W1': s * jax.random.normal(ks[4], (E, D, H), jnp.float32), 'b1': s * jax.random.normal(ks[5], (E, H), jnp.float32), 'W2': s * jax.random.normal(ks[6], (E, H, DOUT), jnp.float32), 'b2': s * jax.random.normal(ks[7], (E, DOUT), jnp.float32)}
    _L3_ffn_all = _L3_ffn_setup()
    _L3_ffn_in = {k: v for k, v in _L3_ffn_all.items() if k in ('gamma', 'beta', 'Wr', 'br', 'W1', 'b1', 'W2', 'b2')}
    del _L3_ffn_all
    return {'x': x, 'adj': adj, 'nodemask': nodemask, 'L0_gnn_Wq': _L0_gnn_in['Wq'], 'L0_gnn_Wk': _L0_gnn_in['Wk'], 'L0_gnn_Wv': _L0_gnn_in['Wv'], 'L0_gnn_Wo': _L0_gnn_in['Wo'], 'L0_gnn_bo': _L0_gnn_in['bo'], 'L0_ffn_gate_w': _L0_ffn_in['gate_w'], 'L0_ffn_gate_b': _L0_ffn_in['gate_b'], 'L0_ffn_w1': _L0_ffn_in['w1'], 'L0_ffn_b1': _L0_ffn_in['b1'], 'L0_ffn_w2': _L0_ffn_in['w2'], 'L0_ffn_b2': _L0_ffn_in['b2'], 'L1_gnn_W1': _L1_gnn_in['W1'], 'L1_gnn_b1': _L1_gnn_in['b1'], 'L1_gnn_W2': _L1_gnn_in['W2'], 'L1_gnn_b2': _L1_gnn_in['b2'], 'L1_gnn_fusion_w': _L1_gnn_in['fusion_w'], 'L1_ffn_route_id': _L1_ffn_in['route_id'], 'L1_ffn_Wi': _L1_ffn_in['Wi'], 'L1_ffn_bi': _L1_ffn_in['bi'], 'L1_ffn_Wr': _L1_ffn_in['Wr'], 'L1_ffn_br': _L1_ffn_in['br'], 'L1_ffn_Ws': _L1_ffn_in['Ws'], 'L1_ffn_bs': _L1_ffn_in['bs'], 'L1_ffn_Wo': _L1_ffn_in['Wo'], 'L1_ffn_bo': _L1_ffn_in['bo'], 'L2_gnn_W1': _L2_gnn_in['W1'], 'L2_gnn_W2': _L2_gnn_in['W2'], 'L2_gnn_w3': _L2_gnn_in['w3'], 'L2_ffn_router_w': _L2_ffn_in['router_w'], 'L2_ffn_w1': _L2_ffn_in['w1'], 'L2_ffn_w2': _L2_ffn_in['w2'], 'L2_ffn_w3': _L2_ffn_in['w3'], 'L3_gnn_W': _L3_gnn_in['W'], 'L3_gnn_b': _L3_gnn_in['b'], 'L3_ffn_gamma': _L3_ffn_in['gamma'], 'L3_ffn_beta': _L3_ffn_in['beta'], 'L3_ffn_Wr': _L3_ffn_in['Wr'], 'L3_ffn_br': _L3_ffn_in['br'], 'L3_ffn_W1': _L3_ffn_in['W1'], 'L3_ffn_b1': _L3_ffn_in['b1'], 'L3_ffn_W2': _L3_ffn_in['W2'], 'L3_ffn_b2': _L3_ffn_in['b2']}

def reference(x, adj, nodemask, L0_gnn_Wq, L0_gnn_Wk, L0_gnn_Wv, L0_gnn_Wo, L0_gnn_bo, L0_ffn_gate_w, L0_ffn_gate_b, L0_ffn_w1, L0_ffn_b1, L0_ffn_w2, L0_ffn_b2, L1_gnn_W1, L1_gnn_b1, L1_gnn_W2, L1_gnn_b2, L1_gnn_fusion_w, L1_ffn_route_id, L1_ffn_Wi, L1_ffn_bi, L1_ffn_Wr, L1_ffn_br, L1_ffn_Ws, L1_ffn_bs, L1_ffn_Wo, L1_ffn_bo, L2_gnn_W1, L2_gnn_W2, L2_gnn_w3, L2_ffn_router_w, L2_ffn_w1, L2_ffn_w2, L2_ffn_w3, L3_gnn_W, L3_gnn_b, L3_ffn_gamma, L3_ffn_beta, L3_ffn_Wr, L3_ffn_br, L3_ffn_W1, L3_ffn_b1, L3_ffn_W2, L3_ffn_b2):
    import jax
    import jax.numpy as jnp

    def _L0_gnn_ref(node_state, adjacency, Wq, Wk, Wv, Wo, bo):
        import math
        import jax, jax.numpy as jnp
        import numpy as np
        HIDDEN = 128
        HEADS = 8
        HEAD_DIM = HIDDEN // HEADS
        b, n, _ = node_state.shape

        def split_heads(x):
            return x.reshape(b, n, HEADS, HEAD_DIM).transpose(0, 2, 1, 3)
        q = split_heads(node_state @ Wq.T)
        k = split_heads(node_state @ Wk.T)
        v = split_heads(node_state @ Wv.T)
        scores = jnp.einsum('bhqd,bhkd->bhqk', q, k) / math.sqrt(HEAD_DIM)
        log_adj = jnp.log(adjacency + 1e-06)
        scores = scores + log_adj[:, None, :, :]
        attn = jax.nn.softmax(scores, axis=-1)
        out = jnp.einsum('bhqk,bhkd->bhqd', attn, v)
        out = out.transpose(0, 2, 1, 3).reshape(b, n, HIDDEN)
        return out @ Wo.T + bo

    def _L0_ffn_ref(h, gate_w, gate_b, w1, b1, w2, b2):
        import math
        import jax, jax.numpy as jnp
        import numpy as np
        CAPACITY_FACTOR = 1.25
        B, L, D = h.shape
        E = gate_w.shape[1]
        T = B * L
        C = max(1, math.ceil(CAPACITY_FACTOR * T / E))
        x = h.reshape(T, D)
        logits = x @ gate_w + gate_b
        probs = jax.nn.softmax(logits, axis=-1)
        idx = jnp.argmax(probs, axis=-1)
        prb = jnp.take_along_axis(probs, idx[:, None], axis=1)[:, 0]
        one_hot = jax.nn.one_hot(idx, E, dtype=jnp.float32)
        pos = (jnp.cumsum(one_hot, axis=0) * one_hot).sum(-1).astype(jnp.int32) - 1
        kept = pos < C
        pos_safe = jnp.where(kept, pos, C)
        buf = jnp.zeros((E, C, D), dtype=h.dtype).at[idx, pos_safe].set(x, mode='drop')
        hmid = jax.nn.relu(jnp.einsum('ecd,edf->ecf', buf, w1) + b1[:, None, :])
        ybuf = jnp.einsum('ecf,efd->ecd', hmid, w2) + b2[:, None, :]
        pos_g = jnp.minimum(pos, C - 1)
        y_tok = ybuf[idx, pos_g] * (prb * kept)[:, None]
        y = y_tok.reshape(B, L, D)
        y = jnp.nan_to_num(y, nan=0.0, posinf=10000.0, neginf=-10000.0)
        return y

    def _L1_gnn_ref(x, adj, W1, b1, W2, b2, fusion_w):
        import jax, jax.numpy as jnp
        import numpy as np
        GROUPS = [list(range(25)), [0, 1, 2, 3, 4, 5, 6, 7, 8], [0, 9, 10, 11, 12, 13, 14], [6, 7, 8, 12, 13, 14], [3, 4, 5, 9, 10, 11]]
        B, N, D_IN, D_HID = (4096, 25, 128, 256)

        def _graph_conv(x, adj, W, b):
            n = adj.shape[-1]
            A = adj + jnp.eye(n, dtype=adj.dtype)
            deg = jnp.sum(A, axis=-1)
            deg_safe = jnp.where(deg == 0, 1.0, deg)
            dinv = jnp.where(deg == 0, 0.0, deg_safe ** (-0.5))
            norm_adj = dinv[:, :, None] * A * dinv[:, None, :]
            support = jnp.einsum('bnd,de->bne', x, W)
            out = jnp.einsum('bnm,bme->bne', norm_adj, support) + b
            return jax.nn.relu(out)
        norm_w = jax.nn.softmax(fusion_w)
        fused = jnp.zeros_like(x)
        for g, idx_list in enumerate(GROUPS):
            idx = jnp.asarray(idx_list)
            x_g = x[:, idx, :]
            adj_g = adj[:, idx][:, :, idx]
            h = _graph_conv(x_g, adj_g, W1[g], b1[g])
            out_g = _graph_conv(h, adj_g, W2[g], b2[g])
            fused = fused.at[:, idx, :].add(norm_w[g] * out_g)
        return fused

    def _L1_ffn_ref(x, route_id, Wi, bi, Wr, br, Ws, bs, Wo, bo):
        import jax, jax.numpy as jnp
        import numpy as np
        B, T, IN_DIM = (64, 128, 128)
        HID, OUT_DIM = (256, 128)
        N_LAYERS, N_EXPERTS, N_SHARED = (2, 16, 1)
        flat = x.reshape(-1, x.shape[-1])
        n_tok = flat.shape[0]
        route = jnp.repeat(route_id, n_tok // route_id.shape[0])
        h = jax.nn.relu(flat @ Wi.T + bi)
        n_layers, n_experts = (Wr.shape[0], Wr.shape[1])
        for l in range(n_layers):
            shared = (jnp.einsum('nd,shd->snh', h, Ws[l]) + bs[l][:, None, :]).mean(axis=0)
            routed = jnp.zeros_like(h)
            for e in range(n_experts):
                ye = h @ Wr[l, e].T + br[l, e]
                routed = routed + jnp.where((route == e)[:, None], ye, 0.0)
            h = jax.nn.relu(shared + routed + h)
        out = h @ Wo.T + bo
        return out.reshape(*x.shape[:-1], out.shape[-1])

    def _L2_gnn_ref(word, adj, W1, W2, w3):
        import jax, jax.numpy as jnp
        import numpy as np
        ALPHA = 0.2
        NEG_INF = -9000000000000000.0
        O = W1.shape[1]
        deg = jnp.sum(adj, axis=-1, keepdims=True)
        deg = jnp.where(deg > 0, deg, jnp.ones_like(deg))
        mp = jnp.matmul(adj / deg, word)
        w3a = w3[:O, 0]
        w3b = w3[O:, 0]
        s1 = jnp.einsum('bnf,fo,o->bn', word, W1, w3a)
        s2 = jnp.einsum('bnf,fo,o->bn', mp, W2, w3b)
        pre = adj * (s2[:, :, None] + s1[:, None, :])
        alpha = jnp.exp(jax.nn.leaky_relu(pre, ALPHA))
        attention = jnp.where(adj > 0, alpha, NEG_INF)
        attention_edge = jax.nn.softmax(attention, axis=2)
        edge = jnp.matmul(attention_edge, word)
        return edge

    def _L2_ffn_ref(x, router_w, w1, w2, w3):
        import jax, jax.numpy as jnp
        import numpy as np
        N_EXPERTS = 8
        TOP_K = 2
        B, T, C = x.shape
        flat = x.reshape(-1, C)
        logits = flat @ router_w.T
        probs = jax.nn.softmax(logits, axis=-1)
        topk_probs, topk_idx = jax.lax.top_k(probs, TOP_K)
        topk_probs = topk_probs / (jnp.sum(topk_probs, axis=-1, keepdims=True) + 1e-09)
        onehot = jax.nn.one_hot(topk_idx, N_EXPERTS, dtype=flat.dtype)
        gates = jnp.einsum('nk,nke->ne', topk_probs, onehot)
        h1 = jnp.einsum('nc,ehc->neh', flat, w1)
        h3 = jnp.einsum('nc,ehc->neh', flat, w3)
        h = jax.nn.silu(h1) * h3
        y = jnp.einsum('neh,ech->nec', h, w2)
        out = jnp.einsum('ne,nec->nc', gates, y)
        return out.reshape(B, T, C)

    def _L3_gnn_ref(H, A, mask, W, b):
        import jax, jax.numpy as jnp
        import numpy as np
        EPS = 1e-08
        N = A.shape[-1]
        A_hat = A + jnp.eye(N, dtype=A.dtype)
        deg = A_hat.sum(axis=-1)
        dis = (deg + EPS) ** (-0.5)
        A_norm = dis[:, :, None] * A_hat * dis[:, None, :]
        H_lin = jnp.einsum('bni,oi->bno', H, W) + b
        out = jnp.einsum('bnm,bmo->bno', A_norm, H_lin)
        out = out * mask[:, :, None]
        return jax.nn.relu(out)

    def _L3_ffn_ref(x, gamma, beta, Wr, br, W1, b1, W2, b2):
        import jax, jax.numpy as jnp
        import numpy as np
        E = 8
        K = 2
        D = 128
        H = 256
        DOUT = 128
        EPS = 1e-05
        mu = jnp.mean(x, axis=-1, keepdims=True)
        var = jnp.mean(jnp.square(x - mu), axis=-1, keepdims=True)
        xn = (x - mu) * jax.lax.rsqrt(var + EPS) * gamma + beta
        logits = jnp.einsum('bsd,de->bse', xn, Wr) + br
        top_vals, top_idx = jax.lax.top_k(logits, K)
        w = jax.nn.softmax(top_vals, axis=-1)
        w_full = jnp.einsum('bsk,bske->bse', w, jax.nn.one_hot(top_idx, E, dtype=w.dtype))
        y = jnp.zeros(x.shape[:-1] + (DOUT,), x.dtype)
        for e in range(E):
            h = jax.nn.gelu(jnp.einsum('bsd,dh->bsh', xn, W1[e]) + b1[e], approximate=False)
            y_e = jnp.einsum('bsh,hd->bsd', h, W2[e]) + b2[e]
            y = y + y_e * w_full[..., e, None]
        return y
    x = x + _L0_gnn_ref(_layernorm(x, axis=-1), adj, L0_gnn_Wq, L0_gnn_Wk, L0_gnn_Wv, L0_gnn_Wo, L0_gnn_bo)
    x = x + _L0_ffn_ref(_layernorm(x, axis=-1), L0_ffn_gate_w, L0_ffn_gate_b, L0_ffn_w1, L0_ffn_b1, L0_ffn_w2, L0_ffn_b2)
    x = x + _L1_gnn_ref(_layernorm(x, axis=-1), adj, L1_gnn_W1, L1_gnn_b1, L1_gnn_W2, L1_gnn_b2, L1_gnn_fusion_w)
    x = x + _L1_ffn_ref(_layernorm(x, axis=-1), L1_ffn_route_id, L1_ffn_Wi, L1_ffn_bi, L1_ffn_Wr, L1_ffn_br, L1_ffn_Ws, L1_ffn_bs, L1_ffn_Wo, L1_ffn_bo)
    x = x + _L2_gnn_ref(_layernorm(x, axis=-1), adj, L2_gnn_W1, L2_gnn_W2, L2_gnn_w3)
    x = x + _L2_ffn_ref(_layernorm(x, axis=-1), L2_ffn_router_w, L2_ffn_w1, L2_ffn_w2, L2_ffn_w3)
    x = x + _L3_gnn_ref(_layernorm(x, axis=-1), adj, nodemask, L3_gnn_W, L3_gnn_b)
    x = x + _L3_ffn_ref(_layernorm(x, axis=-1), L3_ffn_gamma, L3_ffn_beta, L3_ffn_Wr, L3_ffn_br, L3_ffn_W1, L3_ffn_b1, L3_ffn_W2, L3_ffn_b2)
    return x

_drawn_inputs = setup_inputs


def setup_inputs(seed=0):
    import zlib

    import numpy as np

    out = dict(_drawn_inputs(seed))
    spreads = {'L0_ffn_gate_b': (0.0, 0.1),
     'L0_ffn_b1': (0.0, 0.318),
     'L0_ffn_b2': (0.0, 0.1),
     'L1_gnn_b1': (0.0, 0.314),
     'L1_gnn_b2': (0.0, 0.1),
     'L1_gnn_fusion_w': (1.0, 0.6),
     'L1_ffn_bi': (0.0, 0.1),
     'L1_ffn_bo': (0.0, 0.1),
     'L3_gnn_b': (0.0, 0.1),
     'L3_ffn_br': (0.0, 0.459)}
    factors = {'L1_ffn_bs': 2.885,
     'L3_ffn_gamma': 8.0,
     'L3_ffn_beta': 8.0,
     'L3_ffn_Wr': 4.361,
     'L3_ffn_W1': 3.417,
     'L3_ffn_b1': 8.0,
     'L3_ffn_W2': 3.338,
     'L3_ffn_b2': 6.118}
    for name, (base, spread) in spreads.items():
        noise = np.random.default_rng([zlib.crc32(name.encode()), seed]).standard_normal(out[name].shape)
        drawn = base * np.exp(spread * noise) if base else spread * noise
        out[name] = jnp.asarray(drawn.astype(out[name].dtype))
    for name, factor in factors.items():
        out[name] = (out[name] * factor).astype(out[name].dtype)
    return out
```

```python
from contextlib import ExitStack

import concourse.bass as bass
from concourse import mybir

STAGES = 'ABCDEFGH'

F32 = mybir.dt.float32
I32 = mybir.dt.int32
U32 = mybir.dt.uint32
ALU = mybir.AluOpType
ACT = mybir.ActivationFunctionType
AX = mybir.AxisListType

P = 128
NODES = 64
D = 128
TOKENS = 128 * NODES
T = TOKENS // P
GT = 4
NG = T // GT
CH = 16
NCH = T // CH
LN_EPS = 1e-5


def software_pipeline(eng, phases, n, ways=2, at_turn=None):
    depth = len(phases) - 1
    first = -(-(depth + 2) // ways) * ways

    def step(s, slot):
        for p in range(depth, -1, -1):
            if phases[p] is not None and (not isinstance(s, int) or 0 <= s - p < n):
                phases[p](s - p, (slot - p) % ways)

    steady = (n - first) // ways
    at_turn = at_turn or (lambda turn: None)
    for s in range(first):
        if s % ways == 0:
            at_turn(s // ways)
        step(s, s % ways)
    with eng.Fori(0, steady) as i:
        at_turn(i + first // ways)
        for k in range(ways):
            step(i * ways + (first + k), k)
    for s in range(first + ways * steady, n + depth):
        if s % ways == 0:
            at_turn(s // ways)
        step(s, s % ways)


def has(item, back):
    return not isinstance(item, int) or item >= back


class Chain:

    def __init__(self, eng, sem, length):
        self.eng, self.sem, self.length = eng, sem, length

    def start(self, item):
        self.base, self.n = item * self.length, 0

    def link(self, ins):
        self.n += 1
        ins.then_inc(self.sem, 1)
        self.eng.wait_ge(self.sem, self.base + self.n)


class Scope:

    def __init__(self, nc, stack, name):
        self.nc, self.stack, self.name, self.held = nc, stack, name, []
        stack.callback(self.release)

    def release(self):
        if self.held:
            self.nc.clear_and_free_semaphores(self.held)
            self.nc.all_engine_barrier()

    def sb(self, name, shape, dt=F32):
        return self.stack.enter_context(self.nc.sbuf_tensor(f"{self.name}_{name}", shape, dt))

    def sem(self, name):
        self.held.append(self.nc.alloc_semaphore(f"{self.name}_{name}"))
        return self.held[-1]

    def sems(self, name, n=2):
        return [self.sem(f"{name}{i}") for i in range(n)]


def bcast(ap, shape):
    return ap.to_broadcast(shape)


def group(buf, g):
    return buf[:, bass.ds(g * GT, GT), :]


def layer_norm(nc, name, X, XC, R, res_bias=None, twice=False):
    with ExitStack() as stack:
        sc = Scope(nc, stack, name)
        sq = sc.sb("sq", [P, CH, D])
        total = sc.sb("total", [P, T])
        mean = sc.sb("mean", [P, T])
        var = sc.sb("var", [P, T])
        std = sc.sb("std", [P, T])
        mean_ready, centred = sc.sem("mean_ready"), sc.sem("centred")
        squared, sum_done = sc.sem("squared"), sc.sem("sum_done")
        var_ready, std_ready, ln_chain = sc.sem("var_ready"), sc.sem("std_ready"), sc.sem("chain")
        block = stack.enter_context(nc.Block())

        @block.vector
        def _(dve):
            for c in range(NCH):
                t = slice(c * CH, (c + 1) * CH)
                dve.tensor_reduce(total[:, t], X[:, t, :], AX.X, ALU.add).then_inc(sum_done, 1)
                dve.wait_ge(sum_done, c + 1)
                dve.tensor_scalar(mean[:, t], total[:, t], 1.0 / D, None, ALU.mult).then_inc(mean_ready, 1)
                dve.wait_ge(mean_ready, c + 1)
                dve.tensor_tensor(XC[:, t, :], X[:, t, :], bcast(mean[:, t].unsqueeze(2), [P, CH, D]),
                                  ALU.subtract).then_inc(centred, 1)
                if c:
                    pt = slice((c - 1) * CH, c * CH)
                    dve.wait_ge(squared, c)
                    dve.tensor_reduce(var[:, pt], sq[:, :, :], AX.X, ALU.add).then_inc(var_ready, 1)
            pt = slice((NCH - 1) * CH, NCH * CH)
            dve.wait_ge(squared, NCH)
            dve.tensor_reduce(var[:, pt], sq[:, :, :], AX.X, ALU.add).then_inc(var_ready, 1)
            dve.wait_ge(var_ready, NCH)
            chain = Chain(dve, ln_chain, 1)
            chain.start(0)
            chain.link(dve.tensor_scalar(var[:, :], var[:, :], 1.0 / D, LN_EPS, ALU.mult, ALU.add))
            if twice:
                chain.link(dve.tensor_scalar(total[:, :], var[:, :], -LN_EPS, None, ALU.add))
                chain.link(dve.scalar_tensor_tensor(var[:, :], var[:, :], LN_EPS, total[:, :], ALU.mult, ALU.add))
            dve.wait_ge(std_ready, 1)
            dve.reciprocal(R[:, :], std[:, :]).then_inc(ln_chain, 1)

        @block.scalar
        def _(act):
            for c in range(NCH):
                act.wait_ge(centred, c + 1)
                if c:
                    act.wait_ge(var_ready, c)
                nc.scalar.activation(sq[:, :, :], XC[:, c * CH:(c + 1) * CH, :], ACT.Square).then_inc(squared, 1)
            act.wait_ge(ln_chain, 3 if twice else 1)
            nc.scalar.activation(std[:, :], var[:, :], ACT.Sqrt).then_inc(std_ready, 1)

        @block.gpsimd
        def _(pool):
            if res_bias is not None:
                for c in range(NCH):
                    t = slice(c * CH, (c + 1) * CH)
                    pool.wait_ge(centred, c + 1)
                    nc.gpsimd.tensor_tensor(X[:, t, :], X[:, t, :],
                                            bcast(res_bias[:, :].unsqueeze(1), [P, CH, D]), ALU.add)


def dense_gcn(nc, g_in, X, XC, R, ident, banks):
    with ExitStack() as stack:
        sc = Scope(nc, stack, "G")
        adj = sc.sb("adj", [P, T, NODES])
        wt = sc.sb("wt", [P, D])
        bias = sc.sb("bias", [P, D])
        mask = sc.sb("mask", [P, T])
        deg = sc.sb("deg", [P, T])
        dis = sc.sb("dis", [P, T])
        dism = sc.sb("dism", [P, T])
        lnb = [sc.sb(f"lnb{u}", [P, GT, D]) for u in range(2)]
        lnT = [sc.sb(f"lnT{u}", [P, GT, P]) for u in range(2)]
        adjT = [sc.sb(f"adjT{u}", [P, GT, P]) for u in range(2)]
        dh = [sc.sb(f"dh{u}", [P, GT, D]) for u in range(2)]
        agg = [sc.sb(f"agg{u}", [P, GT, D]) for u in range(2)]
        loaded, setup_done, deg_sem = sc.sem("loaded"), sc.sem("setup"), sc.sem("deg")
        zeroed, adjT_in = sc.sem("zeroed"), sc.sems("adjT_in")
        ln_ready, turned, lnT_ready = sc.sem("ln_ready"), sc.sem("turned"), sc.sem("lnT_ready")
        lin_done, dh_ready, agg_done = sc.sem("lin_done"), sc.sem("dh_ready"), sc.sem("agg_done")
        x_done, lin_chain, out_chain = sc.sem("x_done"), sc.sem("lin_chain"), sc.sem("out_chain")
        agg_read = sc.sem("agg_read")
        pT, pL, pA = banks[0:3]
        block = stack.enter_context(nc.Block())

        @block.sync
        def _(sp):
            sp.dma_start(adj[:, :, :], g_in["adj"].rearrange("(t p) j -> p t j", p=P)).then_inc(loaded, 16)
            sp.dma_start(wt[:, :], g_in["L3_gnn_W"]).then_inc(loaded, 16)
            sp.dma_start(bias[:, :], bcast(g_in["L3_gnn_b"], [P, D])).then_inc(loaded, 16)
            sp.dma_start(mask[:, :], g_in["nodemask"]).then_inc(loaded, 16)
            sp.wait_ge(zeroed, 2)

            def load_adjT(g, u):
                if has(g, 2):
                    sp.wait_ge(agg_done, g - 1)
                for b in range(2):
                    h = slice(b * NODES, (b + 1) * NODES)
                    src = g_in["adjT"][bass.ds(g * GT * P, GT * P), :].rearrange("(t p) j -> p t j", p=P)
                    sp.dma_start(adjT[u][h, :, h], src[h, :, :]).then_inc(adjT_in[u], 16)

            software_pipeline(sp, [load_adjT, None, None, None], NG)

        @block.gpsimd
        def _(pool):
            for u in range(2):
                nc.gpsimd.memset(adjT[u][:, :, :], 0.0).then_inc(zeroed, 1)

        @block.scalar
        def _(act):
            act.wait_ge(deg_sem, 3)
            nc.scalar.activation(deg[:, :], deg[:, :], ACT.Sqrt).then_inc(deg_sem, 1)

            def turn(g, u):
                act.wait_ge(turned, g + 1)
                if has(g, 2):
                    act.wait_ge(lin_done, g - 1)
                nc.scalar.activation(lnT[u][:, :, :], pT[:, :].rearrange("p (t d) -> p t d", t=GT),
                                     ACT.Copy).then_inc(lnT_ready, 1)

            software_pipeline(act, [None, turn, None, None], NG)

        @block.tensor
        def _(pe):
            def turn(g, u):
                pe.wait_ge(ln_ready, g + 1)
                if has(g, 1):
                    pe.wait_ge(lnT_ready, g)
                for j in range(GT):
                    last = nc.tensor.transpose(pT[:, j * P:(j + 1) * P], lnb[u][:, j, :], ident[:, :])
                last.then_inc(turned, 1)

            def linear(g, u):
                pe.wait_ge(lnT_ready, g + 1)
                if has(g, 1):
                    pe.wait_ge(dh_ready, g)
                for j in range(GT):
                    last = nc.tensor.matmul(pL[:, j * D:(j + 1) * D], lnT[u][:, j, :], wt[:, :], start=True, stop=True)
                last.then_inc(lin_done, 1)

            def aggregate(g, u):
                pe.wait_ge(dh_ready, g + 1)
                pe.wait_ge(adjT_in[u], g * 16 + (32 - 16 * u))
                if has(g, 1):
                    pe.wait_ge(agg_read, g)
                for j in range(GT):
                    last = nc.tensor.matmul(pA[:, j * D:(j + 1) * D], adjT[u][:, j, :], dh[u][:, j, :],
                                            start=True, stop=True)
                last.then_inc(agg_done, 1)

            pe.wait_ge(loaded, 64)
            software_pipeline(pe, [None, turn, linear, aggregate], NG)

        @block.vector
        def _(dve):
            dve.wait_ge(loaded, 64)
            dve.tensor_reduce(deg[:, :], adj[:, :, :], AX.X, ALU.add).then_inc(deg_sem, 1)
            dve.wait_ge(deg_sem, 1)
            dve.tensor_scalar(deg[:, :], deg[:, :], 1.0, None, ALU.add).then_inc(deg_sem, 1)
            dve.wait_ge(deg_sem, 2)
            dve.tensor_scalar(deg[:, :], deg[:, :], 1e-8, None, ALU.add).then_inc(deg_sem, 1)
            dve.wait_ge(deg_sem, 4)
            dve.reciprocal(dis[:, :], deg[:, :]).then_inc(setup_done, 1)
            dve.wait_ge(setup_done, 1)
            dve.tensor_tensor(dism[:, :], dis[:, :], mask[:, :], ALU.mult).then_inc(setup_done, 1)
            dve.wait_ge(setup_done, 2)

            def normalise(g, u):
                if has(g, 2):
                    dve.wait_ge(turned, g - 1)
                dve.tensor_tensor(lnb[u][:, :, :], group(XC, g),
                                  bcast(R[:, bass.ds(g * GT, GT)].unsqueeze(2), [P, GT, D]),
                                  ALU.mult).then_inc(ln_ready, 1)

            def scale_linear(g, u):
                dve.wait_ge(lin_done, g + 1)
                if has(g, 2):
                    dve.wait_ge(agg_done, g - 1)
                dve.tensor_tensor(dh[u][:, :, :], pL[:, :].rearrange("p (t d) -> p t d", t=GT),
                                  bcast(bias[:, :].unsqueeze(1), [P, GT, D]), ALU.add).then_inc(lin_chain, 1)
                dve.wait_ge(lin_chain, g + 1)
                dve.tensor_tensor(dh[u][:, :, :], dh[u][:, :, :],
                                  bcast(dis[:, bass.ds(g * GT, GT)].unsqueeze(2), [P, GT, D]),
                                  ALU.mult).then_inc(dh_ready, 1)

            def finish(g, u):
                dve.wait_ge(agg_done, g + 1)
                dve.wait_ge(dh_ready, g + 1)
                dve.tensor_tensor(agg[u][:, :, :], pA[:, :].rearrange("p (t d) -> p t d", t=GT), dh[u][:, :, :],
                                  ALU.add).then_inc(agg_read, 1)
                dve.wait_ge(agg_read, g + 1)
                dve.tensor_tensor(agg[u][:, :, :], agg[u][:, :, :],
                                  bcast(dism[:, bass.ds(g * GT, GT)].unsqueeze(2), [P, GT, D]),
                                  ALU.mult).then_inc(out_chain, 1)
                dve.wait_ge(out_chain, g + 1)
                dve.scalar_tensor_tensor(group(X, g), agg[u][:, :, :], 0.0, group(X, g), ALU.max,
                                         ALU.add).then_inc(x_done, 1)

            software_pipeline(dve, [normalise, None, scale_linear, finish], NG)


HEADS = 8
HD = D // HEADS
PAIRS = HEADS // 2
VW = HD + 1


def graph_attention(nc, g_in, X, XC, R, ident, banks):
    with ExitStack() as stack:
        sc = Scope(nc, stack, "A")
        adj = sc.sb("adj", [P, T, NODES])
        wq, wk, wv, wo = (sc.sb(n, [P, D]) for n in ("wq", "wk", "wv", "wo"))
        head_of = sc.sb("head_of", [P, HEADS])
        lnb = [sc.sb(f"lnb{u}", [P, D]) for u in range(2)]
        lnT = [sc.sb(f"lnT{u}", [P, 2, 2, NODES]) for u in range(2)]
        qk = [sc.sb(f"qk{u}", [P, 2, P]) for u in range(2)]
        k_wide = [sc.sb(f"k_wide{u}", [P, HEADS, P]) for u in range(2)]
        v_wide = [sc.sb(f"v_wide{u}", [P, 2, PAIRS, 2, VW]) for u in range(4)]
        top = [sc.sb(f"top{u}", [P, HEADS]) for u in range(2)]
        s = [sc.sb(f"s{u}", [P, HEADS, NODES]) for u in range(2)]
        pT = [sc.sb(f"pT{u}", [P, PAIRS, P]) for u in range(2)]
        inv = [sc.sb(f"inv{u}", [P, HEADS]) for u in range(2)]
        o = [sc.sb(f"o{u}", [P, D]) for u in range(2)]
        oT = [sc.sb(f"oT{u}", [P, P]) for u in range(2)]
        (loaded, adj_ready, zeroed, v_preset, ln_ready, turned, lnT_ready, qk_done, v_done, qk_ready, k_ready, v_ready,
         scores_done, top_ready, shifted, exp_done, p_ready, p_turned, pT_ready, av_done, inv_ready, o_ready, o_turned,
         oT_ready, proj_done, x_done) = (sc.sem(n) for n in (
             "loaded", "adj_ready", "zeroed", "v_preset", "ln_ready", "turned", "lnT_ready", "qk_done", "v_done",
             "qk_ready", "k_ready", "v_ready", "scores_done", "top_ready", "shifted", "exp_done", "p_ready",
             "p_turned", "pT_ready", "av_done", "inv_ready", "o_ready", "o_turned", "oT_ready", "proj_done", "x_done"))
        bX, bQK, bV, bS, bP, bO, bOT, bY = banks
        block = stack.enter_context(nc.Block())

        @block.sync
        def _(sp):
            sp.dma_start(adj[:, :, :], g_in["adj"].rearrange("(t p) j -> p t j", p=P)).then_inc(loaded, 16)
            for buf, name in ((wq, "L0_gnn_Wq"), (wk, "L0_gnn_Wk"), (wv, "L0_gnn_Wv"), (wo, "L0_gnn_Wo"),
                              (head_of, "c_head_of")):
                sp.dma_start(buf[:, :], g_in[name]).then_inc(loaded, 16)

        @block.tensor
        def _(pe):
            def turn(t, w):
                pe.wait_ge(ln_ready, t + 1)
                if has(t, 1):
                    pe.wait_ge(lnT_ready, t)
                nc.tensor.transpose(bX[:, 0:P], lnb[w % 2][:, :], ident[:, :]).then_inc(turned, 1)

            def project(t, w):
                pe.wait_ge(lnT_ready, t + 1)
                if has(t, 1):
                    pe.wait_ge(qk_ready, t)
                nc.tensor.matmul(bQK[:, 0:P], wq[:, :], lnT[w % 2][:, :, 0, :], start=True, stop=True)
                nc.tensor.matmul(bQK[:, P:2 * P], wk[:, :], lnT[w % 2][:, :, 0, :], start=True, stop=True).then_inc(qk_done, 1)
                if has(t, 1):
                    pe.wait_ge(v_ready, t)
                for b in range(2):
                    last = nc.tensor.matmul(bV[:, b * D:(b + 1) * D], lnT[w % 2][:, b, :, :].rearrange("p a k -> p (a k)"),
                                            wv[:, :], start=True, stop=True)
                last.then_inc(v_done, 1)

            def scores(t, w):
                pe.wait_ge(qk_ready, t + 1)
                pe.wait_ge(k_ready, t + 1)
                if has(t, 1):
                    pe.wait_ge(shifted, t)
                for b in range(2):
                    h = slice(b * NODES, (b + 1) * NODES)
                    last = nc.tensor.matmul(bS[h, :], qk[w % 2][:, 0, h], k_wide[w % 2][:, :, h], start=True, stop=True)
                last.then_inc(scores_done, 1)

            def turn_p(t, w):
                pe.wait_ge(p_ready, t + 1)
                if has(t, 1):
                    pe.wait_ge(pT_ready, t)
                for c in range(PAIRS):
                    last = nc.tensor.transpose(bP[:, c * P:(c + 1) * P],
                                               s[w % 2][:, 2 * c:2 * c + 2, :].rearrange("p h k -> p (h k)"), ident[:, :])
                last.then_inc(p_turned, 1)

            def values(t, w):
                pe.wait_ge(pT_ready, t + 1)
                pe.wait_ge(v_ready, t + 1)
                if has(t, 1):
                    pe.wait_ge(o_ready, t)
                for b in range(2):
                    h = slice(b * NODES, (b + 1) * NODES)
                    for c in range(PAIRS):
                        last = nc.tensor.matmul(bO[h, c * 2 * VW:(c + 1) * 2 * VW], pT[w % 2][:, c, h],
                                                v_wide[w][:, b, c, :, :].rearrange("p s d -> p (s d)"),
                                                start=True, stop=True)
                last.then_inc(av_done, 1)

            def turn_o(t, w):
                pe.wait_ge(o_ready, t + 1)
                if has(t, 1):
                    pe.wait_ge(oT_ready, t)
                nc.tensor.transpose(bOT[:, 0:P], o[w % 2][:, :], ident[:, :]).then_inc(o_turned, 1)

            def project_out(t, w):
                pe.wait_ge(oT_ready, t + 1)
                if has(t, 1):
                    pe.wait_ge(x_done, t)
                nc.tensor.matmul(bY[:, 0:D], oT[w % 2][:, :], wo[:, :], start=True, stop=True).then_inc(proj_done, 1)

            pe.wait_ge(loaded, 96)
            software_pipeline(pe, [None, turn, project, scores, turn_p, values, turn_o, project_out], T, 4)

        @block.scalar
        def _(act):
            def turn(t, w):
                act.wait_ge(turned, t + 1)
                if has(t, 2):
                    act.wait_ge(v_done, t - 1)
                src = bX[:, 0:P].rearrange("p (b k) -> p b k", b=2).unsqueeze(2)
                nc.scalar.activation(lnT[w % 2][:, :, :, :], bcast(src, [P, 2, 2, NODES]), ACT.Copy).then_inc(lnT_ready, 1)

            def project(t, w):
                act.wait_ge(qk_done, t + 1)
                if has(t, 2):
                    act.wait_ge(scores_done, t - 1)
                    act.wait_ge(k_ready, t - 1)
                nc.scalar.activation(qk[w % 2][:, :, :], bQK[:, 0:2 * P].rearrange("p (a q) -> p a q", a=2),
                                     ACT.Copy).then_inc(qk_ready, 1)

            def exponentials(t, w):
                act.wait_ge(shifted, t + 1)
                nc.scalar.activation(s[w % 2][:, :, :], s[w % 2][:, :, :], ACT.Exp,
                                     scale=HD ** -0.5).then_inc(exp_done, 1)

            def turn_p(t, w):
                act.wait_ge(p_turned, t + 1)
                if has(t, 2):
                    act.wait_ge(av_done, t - 1)
                nc.scalar.activation(pT[w % 2][:, :, :], bP[:, :].rearrange("p (c q) -> p c q", c=PAIRS),
                                     ACT.Copy).then_inc(pT_ready, 1)

            def turn_o(t, w):
                act.wait_ge(o_turned, t + 1)
                if has(t, 2):
                    act.wait_ge(proj_done, t - 1)
                nc.scalar.activation(oT[w % 2][:, :], bOT[:, 0:P], ACT.Copy).then_inc(oT_ready, 1)

            software_pipeline(act, [None, turn, project, exponentials, turn_p, None, turn_o, None], T, 4)

        @block.gpsimd
        def _(pool):
            for u in range(4):
                nc.gpsimd.memset(v_wide[u][:, :, :, :, :], 0.0).then_inc(zeroed, 1)
            pool.wait_ge(zeroed, 4)
            for u in range(4):
                for s2 in range(2):
                    h = slice(s2 * NODES, (s2 + 1) * NODES)
                    ones = v_wide[u][h, :, :, s2, HD:VW].rearrange("p b c d -> p (b c) d")
                    nc.gpsimd.memset(ones, 1.0).then_inc(v_preset, 1)
            pool.wait_ge(v_preset, 8)
            pool.wait_ge(loaded, 96)
            nc.gpsimd.tensor_scalar(adj[:, :, :], adj[:, :, :], 1e-6, None, ALU.add).then_inc(adj_ready, 1)
            pool.wait_ge(adj_ready, 1)

            def widen_k(t, w):
                pool.wait_ge(qk_ready, t + 1)
                if has(t, 2):
                    pool.wait_ge(scores_done, t - 1)
                nc.gpsimd.tensor_tensor(k_wide[w % 2][:, :, :], bcast(qk[w % 2][:, 1:2, :], [P, HEADS, P]),
                                        bcast(head_of[:, :].unsqueeze(2), [P, HEADS, P]), ALU.mult).then_inc(k_ready, 1)

            def weigh(t, w):
                pool.wait_ge(exp_done, t + 1)
                nc.gpsimd.tensor_tensor(s[w % 2][:, :, :], s[w % 2][:, :, :],
                                        bcast(adj[:, bass.ds(t, 1), :], [P, HEADS, NODES]), ALU.mult).then_inc(p_ready, 1)

            software_pipeline(pool, [None, None, widen_k, weigh, None, None, None, None], T, 4)

        @block.vector
        def _(dve):
            dve.wait_ge(v_preset, 8)

            def normalise(t, w):
                if has(t, 2):
                    dve.wait_ge(turned, t - 1)
                dve.tensor_scalar(lnb[w % 2][:, :], XC[:, bass.ds(t, 1), :].rearrange("p o d -> p (o d)"),
                                  R[:, bass.ds(t, 1)], None, ALU.mult).then_inc(ln_ready, 1)

            def widen_v(t, w):
                dve.wait_ge(v_done, t + 1)
                if has(t, 4):
                    dve.wait_ge(av_done, t - 3)
                for s2 in range(2):
                    h = slice(s2 * NODES, (s2 + 1) * NODES)
                    src = bV[h, 0:2 * D].rearrange("p (c s d) -> p c s d", s=2, d=HD)[:, :, s2, :]
                    last = dve.tensor_copy(v_wide[w][h, :, :, s2, 0:HD].rearrange("p b c d -> p (b c) d"), src)
                last.then_inc(v_ready, 1)

            def shift(t, w):
                dve.wait_ge(scores_done, t + 1)
                src = bS[:, :].rearrange("p (h k) -> p h k", h=HEADS)
                dve.tensor_reduce(top[w % 2][:, :], src, AX.X, ALU.max).then_inc(top_ready, 1)
                dve.wait_ge(top_ready, t + 1)
                if has(t, 2):
                    dve.wait_ge(p_turned, t - 1)
                dve.tensor_tensor(s[w % 2][:, :, :], src, bcast(top[w % 2][:, :].unsqueeze(2), [P, HEADS, NODES]),
                                  ALU.subtract).then_inc(shifted, 1)

            def divide(t, w):
                dve.wait_ge(av_done, t + 1)
                src = bO[:, 0:HEADS * VW].rearrange("p (h d) -> p h d", h=HEADS)
                dve.reciprocal(inv[w % 2][:, :].unsqueeze(2), src[:, :, HD:VW]).then_inc(inv_ready, 1)
                dve.wait_ge(inv_ready, t + 1)
                if has(t, 2):
                    dve.wait_ge(o_turned, t - 1)
                dve.tensor_tensor(o[w % 2][:, :].rearrange("p (h d) -> p h d", h=HEADS), src[:, :, 0:HD],
                                  bcast(inv[w % 2][:, :].unsqueeze(2), [P, HEADS, HD]), ALU.mult).then_inc(o_ready, 1)

            def add(t, w):
                dve.wait_ge(proj_done, t + 1)
                xt = X[:, bass.ds(t, 1), :].rearrange("p o d -> p (o d)")
                dve.tensor_tensor(xt, bY[:, 0:D], xt, ALU.add).then_inc(x_done, 1)

            software_pipeline(dve, [normalise, None, widen_v, shift, None, divide, None, add], T, 4)


GROUPS = [list(range(25)), [0, 1, 2, 3, 4, 5, 6, 7, 8], [0, 9, 10, 11, 12, 13, 14], [6, 7, 8, 12, 13, 14],
          [3, 4, 5, 9, 10, 11]]
SLOT0 = [sum(len(n) for n in GROUPS[:g]) for g in range(len(GROUPS))]
SLOTS = sum(len(n) for n in GROUPS)
MID = 256


def group_gcns(nc, g_in, X, XC, R, ident, banks):
    with ExitStack() as stack:
        sc = Scope(nc, stack, "C")
        NGR = len(GROUPS)
        adj = sc.sb("adj", [P, T, NODES])
        w1 = sc.sb("w1", [P, NGR, MID])
        w2 = sc.sb("w2", [P, NGR, 2, D])
        b1 = sc.sb("b1", [P, NGR, 2])
        b2 = sc.sb("b2", [P, D])
        fusion = sc.sb("fusion", [P, NGR])
        slot_group = sc.sb("slot_group", [P, NGR])
        fmax, fsum, finv, slot_w = (sc.sb(n, [P, 1]) for n in ("fmax", "fsum", "finv", "slot_w"))
        pick = sc.sb("pick", [P, P])
        spread = sc.sb("spread", [P, P])
        deg, zero, dinv = (sc.sb(n, [P, T]) for n in ("deg", "zero", "dinv"))
        ring = lambda name, shape: [sc.sb(f"{name}{u}", shape) for u in range(2)]
        lnb, xs, z, ys, f = (ring(n, [P, GT, D]) for n in ("lnb", "xs", "z", "ys", "f"))
        adj1, adj2 = ring("adj1", [P, GT, P]), ring("adj2", [P, GT, P])
        zT, sT = ring("zT", [P, 2 * GT, NODES]), ring("sT", [P, 2 * GT, NODES])
        hT = ring("hT", [P, 2, 2 * GT, NODES])
        (loaded, zeroed, chain_sem, exp_done, sqrt_done, ln_ready, picked, xs_ready, conv1_done, z_sum, z_scaled, z_turned,
         zT_ready, up_done, hT_ready, down_done, sT_ready, s_turned, ys_ready, conv2_done, bank7_read, spread_done,
         x_done, f_chain, f_ready) = (sc.sem(n) for n in (
             "loaded", "zeroed", "chain", "exp_done", "sqrt_done", "ln_ready", "picked", "xs_ready", "conv1_done",
             "z_sum", "z_scaled", "z_turned", "zT_ready", "up_done", "hT_ready", "down_done", "sT_ready", "s_turned",
             "ys_ready", "conv2_done", "bank7_read", "spread_done", "x_done", "f_chain", "f_ready"))
        adj1_in, adj2_in = sc.sems("adj1_in"), sc.sems("adj2_in")
        bPick, bA1, bZT, bH0, bH1, bS, bST, bA2 = banks
        bSpread = bPick
        LAST = 8
        cols = lambda bank: bank[:, :].rearrange("p (a s) -> p a s", s=NODES)
        tiles = lambda bank: bank[:, :].rearrange("p (t d) -> p t d", t=GT)
        block = stack.enter_context(nc.Block())

        @block.sync
        def _(sp):
            for buf, src in ((adj[:, :, :], g_in["slot_adj"].rearrange("(t p) j -> p t j", p=P)),
                             (w1[:, :, :], g_in["L1_gnn_W1"].rearrange("g d f -> d g f")),
                             (w2[:, :, :, :], g_in["L1_gnn_W2"].rearrange("g (c f) d -> f g c d", f=P)),
                             (b1[:, :, :], g_in["L1_gnn_b1"]), (b2[:, :], g_in["L1_gnn_b2"]),
                             (fusion[:, :], bcast(g_in["L1_gnn_fusion_w"], [P, NGR])),
                             (slot_group[:, :], g_in["c_slot_group"]),
                             (pick[:, :], g_in["c_pick"]), (spread[:, :], g_in["c_spread"])):
                sp.dma_start(buf, src).then_inc(loaded, 16)
            sp.wait_ge(zeroed, 6)

            def load(dst, arrived, readers):
                def run(g, u):
                    if has(g, 2):
                        sp.wait_ge(readers, g - 1)
                    src = g_in["slot_adjT"][bass.ds(g * GT * P, GT * P), :].rearrange("(t p) j -> p t j", p=P)
                    for b in range(2):
                        h = slice(b * NODES, (b + 1) * NODES)
                        sp.dma_start(dst[u][h, :, h], src[h, :, :]).then_inc(arrived[u], 16)
                return run

            software_pipeline(sp, [None, load(adj1, adj1_in, conv1_done), None, None, None, None,
                                   load(adj2, adj2_in, conv2_done), None, None], NG)

        @block.gpsimd
        def _(pool):
            for buf in adj1 + adj2 + sT:
                nc.gpsimd.memset(buf[:, :, :], 0.0).then_inc(zeroed, 1)

        @block.tensor
        def _(pe):
            def pick_slots(g, u):
                pe.wait_ge(ln_ready, g + 1)
                if has(g, 1):
                    pe.wait_ge(xs_ready, g)
                if has(g, LAST - 1):
                    pe.wait_ge(x_done, g - (LAST - 2))
                nc.tensor.matmul(bPick[:, :], pick[:, :], lnb[u][:, :, :].rearrange("p t d -> p (t d)"),
                                 start=True, stop=True).then_inc(picked, 1)

            def conv1(g, u):
                pe.wait_ge(xs_ready, g + 1)
                pe.wait_ge(adj1_in[u], g * 16 + (32 - 16 * u))
                if has(g, 1):
                    pe.wait_ge(z_sum, g)
                for j in range(GT):
                    last = nc.tensor.matmul(bA1[:, j * D:(j + 1) * D], adj1[u][:, j, :], xs[u][:, j, :],
                                            start=True, stop=True)
                last.then_inc(conv1_done, 1)

            def turn_z(g, u):
                pe.wait_ge(z_scaled, g + 1)
                if has(g, 1):
                    pe.wait_ge(zT_ready, g)
                for j in range(GT):
                    last = nc.tensor.transpose(bZT[:, j * P:(j + 1) * P], z[u][:, j, :], ident[:, :])
                last.then_inc(z_turned, 1)

            def up(g, u):
                pe.wait_ge(zT_ready, g + 1)
                if has(g, 1):
                    pe.wait_ge(hT_ready, g)
                for c, bank in enumerate((bH0, bH1)):
                    for i, nodes in enumerate(GROUPS):
                        sl = slice(SLOT0[i], SLOT0[i] + len(nodes))
                        last = nc.tensor.matmul(cols(bank)[:, :, sl], w1[:, i, c * P:(c + 1) * P], zT[u][:, :, sl],
                                                start=True, stop=True)
                last.then_inc(up_done, 1)

            def down(g, u):
                pe.wait_ge(hT_ready, g + 1)
                if has(g, 1):
                    pe.wait_ge(sT_ready, g)
                for i, nodes in enumerate(GROUPS):
                    sl = slice(SLOT0[i], SLOT0[i] + len(nodes))
                    for c in range(2):
                        last = nc.tensor.matmul(cols(bS)[:, :, sl], w2[:, i, c, :], hT[u][:, c, :, sl],
                                                start=(c == 0), stop=(c == 1))
                last.then_inc(down_done, 1)

            def turn_s(g, u):
                pe.wait_ge(sT_ready, g + 1)
                if has(g, 1):
                    pe.wait_ge(ys_ready, g)
                for j in range(GT):
                    last = nc.tensor.transpose(bST[:, j * P:(j + 1) * P],
                                               sT[u][:, 2 * j:2 * j + 2, :].rearrange("p b s -> p (b s)"), ident[:, :])
                last.then_inc(s_turned, 1)

            def conv2(g, u):
                pe.wait_ge(ys_ready, g + 1)
                pe.wait_ge(adj2_in[u], g * 16 + (32 - 16 * u))
                if has(g, 1):
                    pe.wait_ge(bank7_read, g)
                for j in range(GT):
                    last = nc.tensor.matmul(bA2[:, j * D:(j + 1) * D], adj2[u][:, j, :], ys[u][:, j, :],
                                            start=True, stop=True)
                last.then_inc(conv2_done, 1)

            def spread_slots(g, u):
                pe.wait_ge(f_ready, g + 1)
                n = g + (LAST - 1)
                pe.wait_ge(xs_ready, min(n, NG) if isinstance(n, int) else n)
                if has(g, 1):
                    pe.wait_ge(x_done, g)
                nc.tensor.matmul(bSpread[:, :], spread[:, :], f[u][:, :, :].rearrange("p t d -> p (t d)"),
                                 start=True, stop=True).then_inc(spread_done, 1)

            pe.wait_ge(loaded, 144)
            software_pipeline(pe, [None, pick_slots, conv1, turn_z, up, down, turn_s, conv2, spread_slots], NG)

        @block.scalar
        def _(act):
            act.wait_ge(chain_sem, 2)
            nc.scalar.activation(fusion[:, :], fusion[:, :], ACT.Exp).then_inc(exp_done, 1)
            act.wait_ge(chain_sem, 12)
            nc.scalar.activation(deg[:, :], deg[:, :], ACT.Sqrt).then_inc(sqrt_done, 1)

            def turn_z(g, u):
                act.wait_ge(z_turned, g + 1)
                if has(g, 2):
                    act.wait_ge(up_done, g - 1)
                nc.scalar.activation(zT[u][:, :, :], cols(bZT), ACT.Copy).then_inc(zT_ready, 1)

            def up(g, u):
                act.wait_ge(up_done, g + 1)
                if has(g, 2):
                    act.wait_ge(down_done, g - 1)
                for c, bank in enumerate((bH0, bH1)):
                    for i, nodes in enumerate(GROUPS):
                        sl = slice(SLOT0[i], SLOT0[i] + len(nodes))
                        last = nc.scalar.activation(hT[u][:, c, :, sl], cols(bank)[:, :, sl], ACT.Relu,
                                                    bias=b1[:, i, c:c + 1])
                last.then_inc(hT_ready, 1)

            def down(g, u):
                act.wait_ge(down_done, g + 1)
                if has(g, 2):
                    act.wait_ge(s_turned, g - 1)
                nc.scalar.activation(sT[u][:, :, 0:SLOTS], cols(bS)[:, :, 0:SLOTS], ACT.Copy).then_inc(sT_ready, 1)

            software_pipeline(act, [None, None, None, turn_z, up, down, None, None, None], NG)

        @block.vector
        def _(dve):
            chain = Chain(dve, chain_sem, 0)
            chain.start(0)
            link = chain.link
            dve.wait_ge(loaded, 144)
            link(dve.tensor_reduce(fmax[:, :], fusion[:, :], AX.X, ALU.max))
            link(dve.tensor_scalar(fusion[:, :], fusion[:, :], fmax[:, :], None, ALU.subtract))
            dve.wait_ge(exp_done, 1)
            link(dve.tensor_reduce(fsum[:, :], fusion[:, :], AX.X, ALU.add))
            link(dve.reciprocal(finv[:, :], fsum[:, :]))
            link(dve.tensor_tensor(fusion[:, :], fusion[:, :], slot_group[:, :], ALU.mult))
            link(dve.tensor_reduce(slot_w[:, :], fusion[:, :], AX.X, ALU.add))
            link(dve.tensor_tensor(slot_w[:, :], slot_w[:, :], finv[:, :], ALU.mult))
            link(dve.tensor_reduce(deg[:, :], adj[:, :, :], AX.X, ALU.add))
            link(dve.tensor_scalar(deg[:, :], deg[:, :], 1.0, None, ALU.add))
            link(dve.tensor_scalar(zero[:, :], deg[:, :], 0.0, None, ALU.is_equal))
            link(dve.tensor_tensor(deg[:, :], deg[:, :], zero[:, :], ALU.add))
            link(dve.tensor_scalar(zero[:, :], zero[:, :], -1.0, 1.0, ALU.mult, ALU.add))
            dve.wait_ge(sqrt_done, 1)
            link(dve.reciprocal(dinv[:, :], deg[:, :]))
            link(dve.tensor_tensor(dinv[:, :], dinv[:, :], zero[:, :], ALU.mult))

            def dinv_of(g):
                return bcast(dinv[:, bass.ds(g * GT, GT)].unsqueeze(2), [P, GT, D])

            def normalise(g, u):
                if has(g, 2):
                    dve.wait_ge(picked, g - 1)
                dve.tensor_tensor(lnb[u][:, :, :], group(XC, g),
                                  bcast(R[:, bass.ds(g * GT, GT)].unsqueeze(2), [P, GT, D]),
                                  ALU.mult).then_inc(ln_ready, 1)

            def pick_slots(g, u):
                dve.wait_ge(picked, g + 1)
                if has(g, 2):
                    dve.wait_ge(conv1_done, g - 1)
                    dve.wait_ge(z_sum, g - 1)
                dve.tensor_tensor(xs[u][:, :, :], tiles(bPick), dinv_of(g), ALU.mult).then_inc(xs_ready, 1)

            def conv1(g, u):
                dve.wait_ge(conv1_done, g + 1)
                if has(g, 2):
                    dve.wait_ge(z_turned, g - 1)
                dve.tensor_tensor(z[u][:, :, :], tiles(bA1), xs[u][:, :, :], ALU.add).then_inc(z_sum, 1)
                dve.wait_ge(z_sum, g + 1)
                dve.tensor_tensor(z[u][:, :, :], z[u][:, :, :], dinv_of(g), ALU.mult).then_inc(z_scaled, 1)

            def turn_s(g, u):
                dve.wait_ge(s_turned, g + 1)
                if has(g, 2):
                    dve.wait_ge(conv2_done, g - 1)
                dve.tensor_tensor(ys[u][:, :, :], tiles(bST), dinv_of(g), ALU.mult).then_inc(ys_ready, 1)

            def conv2(g, u):
                dve.wait_ge(conv2_done, g + 1)
                if has(g, 2):
                    dve.wait_ge(spread_done, g - 1)
                dve.tensor_tensor(f[u][:, :, :], tiles(bA2), ys[u][:, :, :], ALU.add).then_inc(bank7_read, 1)
                dve.wait_ge(bank7_read, g + 1)
                dve.tensor_tensor(f[u][:, :, :], f[u][:, :, :], dinv_of(g), ALU.mult).then_inc(f_chain, 1)
                dve.wait_ge(f_chain, g * 2 + 1)
                dve.tensor_tensor(f[u][:, :, :], f[u][:, :, :], bcast(b2[:, :].unsqueeze(1), [P, GT, D]),
                                  ALU.add).then_inc(f_chain, 1)
                dve.wait_ge(f_chain, g * 2 + 2)
                dve.tensor_scalar(f[u][:, :, :], f[u][:, :, :], 0.0, slot_w[:, :], ALU.max, ALU.mult).then_inc(f_ready, 1)

            def add(g, u):
                dve.wait_ge(spread_done, g + 1)
                dve.tensor_tensor(group(X, g), tiles(bSpread), group(X, g), ALU.add).then_inc(x_done, 1)

            software_pipeline(dve, [normalise, pick_slots, conv1, None, None, None, turn_s, conv2, add], NG)


ROUTES = 16
LAYERS = 2
D_WAYS = 4
FIRST, SECOND = 3, 5
D_TURNS = (T + 7 - 1) // D_WAYS + 1


def routed_mlp(nc, g_in, X, XC, R, ident, banks):
    with ExitStack() as stack:
        sc = Scope(nc, stack, "D")
        w = sc.sb("w", [P, LAYERS, ROUTES, 2, MID])
        ws = sc.sb("ws", [P, LAYERS, 2, MID])
        eye2 = sc.sb("eye2", [P, 2, MID])
        br = sc.sb("br", [P, LAYERS, ROUTES, MID])
        bs = sc.sb("bs", [P, LAYERS, MID])
        wi = sc.sb("wi", [P, MID])
        bi = sc.sb("bi", [P, 2])
        wo = sc.sb("wo", [P, 2, D])
        route = sc.sb("route", [1, T], I32)
        route_f = sc.sb("route_f", [1, SECOND + D_WAYS * D_TURNS])
        digits = sc.sb("digits", [1, D_WAYS])
        words = sc.sb("words", [1, 2, D_TURNS, D_WAYS])
        word_sum = sc.sb("word_sum", [1, 2, D_TURNS])
        packed = sc.sb("packed", [1, 2, D_TURNS], I32)
        ring = lambda name, shape: [sc.sb(f"{name}{u}", shape) for u in range(2)]
        lnb, lnT = ring("lnb", [P, D]), ring("lnT", [P, P])
        h0T, h1T, h2T = (ring(n, [P, 2, P]) for n in ("h0T", "h1T", "h2T"))
        h1, h2 = ring("h1", [P, MID]), ring("h2", [P, MID])
        (loaded, chain_sem, words_ready, weights_ready, ln_ready, turned, lnT_ready, in_done, h0_ready, mm1_done,
         h1_ready, turned1, h1T_ready, mm2_done, h2_ready, turned2, h2T_ready, out_done, x_done) = (
             sc.sem(n) for n in (
                 "loaded", "chain", "words_ready", "weights_ready", "ln_ready", "turned", "lnT_ready", "in_done",
                 "h0_ready", "mm1_done", "h1_ready", "turned1", "h1T_ready", "mm2_done", "h2_ready", "turned2",
                 "h2T_ready", "out_done", "x_done"))
        bX, b0, b1, bT1, b2, bT2, bY = banks[0:7]
        block = stack.enter_context(nc.Block())

        @block.sync
        def _(sp):
            for buf, src in ((route[:, :], g_in["L1_ffn_route_id"]), (digits[:, :], g_in["c_hex_digits"]),
                             (w[:, :, :, :, :], g_in["L1_ffn_Wr"]), (ws[:, :, :, :], g_in["L1_ffn_Ws"]),
                             (eye2[:, :, :], g_in["c_eye2"]),
                             (br[:, :, :, :].rearrange("p l e f -> p (l e f)"),
                              bcast(g_in["L1_ffn_br"], [P, LAYERS * ROUTES * MID])),
                             (bs[:, :, :].rearrange("p l f -> p (l f)"), bcast(g_in["L1_ffn_bs"], [P, LAYERS * MID])),
                             (wi[:, :], g_in["L1_ffn_Wi"]), (bi[:, :], g_in["L1_ffn_bi"]), (wo[:, :, :], g_in["L1_ffn_Wo"])):
                sp.dma_start(buf, src).then_inc(loaded, 16)

        weights_sem = sc.sems("shared_ready")

        def combine_weights(eng, layer):
            shared = ws[:, layer, :, :]
            eng.tensor_tensor(shared, shared, eye2[:, :, :], ALU.add).then_inc(weights_sem[layer], 1)
            eng.wait_ge(weights_sem[layer], 1)
            ww = w[:, layer, :, :, :].rearrange("p e c f -> p e (c f)")
            eng.tensor_tensor(ww, ww, bcast(shared.rearrange("p c f -> p (c f)").unsqueeze(1), [P, ROUTES, 2 * MID]),
                              ALU.add).then_inc(weights_ready, 1)
            bb = br[:, layer, :, :]
            eng.tensor_tensor(bb, bb, bcast(bs[:, layer:layer + 1, :], [P, ROUTES, MID]), ALU.add).then_inc(weights_ready, 1)

        @block.gpsimd
        def _(pool):
            pool.wait_ge(loaded, 160)
            combine_weights(pool, 1)

        class Routes:

            def __init__(self, eng):
                self.eng = eng

            def turn(self, j):
                self.words = [self.eng.value_load(packed[:, i, bass.ds(j, 1)], min_val=0, max_val=ROUTES ** D_WAYS - 1)
                              for i in range(2)]

            def of(self, slot, phase):
                return (self.words[phase == SECOND] >> (4 * ((slot + phase) % D_WAYS))) & (ROUTES - 1)

        @block.tensor
        def _(pe):
            routes = Routes(pe)

            def turn(t, k):
                pe.wait_ge(ln_ready, t + 1)
                if has(t, 1):
                    pe.wait_ge(lnT_ready, t)
                nc.tensor.transpose(bX[:, 0:P], lnb[k % 2][:, :], ident[:, :]).then_inc(turned, 1)

            def project_in(t, k):
                pe.wait_ge(lnT_ready, t + 1)
                if has(t, 1):
                    pe.wait_ge(h0_ready, t)
                for c in range(2):
                    last = nc.tensor.matmul(b0[:, c * P:(c + 1) * P], wi[:, c * P:(c + 1) * P], lnT[k % 2][:, :],
                                            start=True, stop=True)
                last.then_inc(in_done, 1)

            def layer(n, phase, bank, src, src_ready, bank_read, done):
                def run(t, k):
                    e = routes.of(k, phase)
                    pe.wait_ge(src_ready, t + 1)
                    if has(t, 1):
                        pe.wait_ge(bank_read, t)
                    for c in range(2):
                        last = nc.tensor.matmul(bank[:, 0:MID], src[k % 2][:, c, :],
                                                w[:, n, bass.ds(e, 1), c, :].rearrange("p o f -> p (o f)"),
                                                start=(c == 0), stop=(c == 1))
                    last.then_inc(done, 1)
                return run

            def turn_h(bank, src, src_ready, bank_read, done):
                def run(t, k):
                    pe.wait_ge(src_ready, t + 1)
                    if has(t, 1):
                        pe.wait_ge(bank_read, t)
                    for c in range(2):
                        last = nc.tensor.transpose(bank[:, c * P:(c + 1) * P], src[k % 2][:, c * P:(c + 1) * P], ident[:, :])
                    last.then_inc(done, 1)
                return run

            def project_out(t, k):
                pe.wait_ge(h2T_ready, t + 1)
                if has(t, 1):
                    pe.wait_ge(x_done, t)
                for c in range(2):
                    last = nc.tensor.matmul(bY[:, 0:D], h2T[k % 2][:, c, :], wo[:, c, :], start=(c == 0), stop=(c == 1))
                last.then_inc(out_done, 1)

            pe.wait_ge(loaded, 160)
            pe.wait_ge(words_ready, 1)
            pe.wait_ge(weights_ready, 4)
            software_pipeline(pe, [None, turn, project_in, layer(0, FIRST, b1, h0T, h0_ready, h1_ready, mm1_done),
                                   turn_h(bT1, h1, h1_ready, h1T_ready, turned1),
                                   layer(1, SECOND, b2, h1T, h1T_ready, h2_ready, mm2_done),
                                   turn_h(bT2, h2, h2_ready, h2T_ready, turned2), project_out],
                              T, D_WAYS, routes.turn)

        @block.scalar
        def _(act):
            act.wait_ge(loaded, 160)

            def turn(t, k):
                act.wait_ge(turned, t + 1)
                if has(t, 2):
                    act.wait_ge(in_done, t - 1)
                nc.scalar.activation(lnT[k % 2][:, :], bX[:, 0:P], ACT.Copy).then_inc(lnT_ready, 1)

            def project_in(t, k):
                act.wait_ge(in_done, t + 1)
                if has(t, 2):
                    act.wait_ge(mm1_done, t - 1)
                for c in range(2):
                    last = nc.scalar.activation(h0T[k % 2][:, c, :], b0[:, c * P:(c + 1) * P], ACT.Relu, bias=bi[:, c:c + 1])
                last.then_inc(h0_ready, 1)

            def turn_h(bank, dst, done, readers, ready):
                def run(t, k):
                    act.wait_ge(done, t + 1)
                    if has(t, 2):
                        act.wait_ge(readers, t - 1)
                    nc.scalar.activation(dst[k % 2][:, :, :], bank[:, 0:2 * P].rearrange("p (c q) -> p c q", c=2),
                                         ACT.Relu).then_inc(ready, 1)
                return run

            software_pipeline(act, [None, turn, project_in, None, turn_h(bT1, h1T, turned1, mm2_done, h1T_ready), None,
                                    turn_h(bT2, h2T, turned2, out_done, h2T_ready), None], T, D_WAYS)

        @block.vector
        def _(dve):
            chain = Chain(dve, chain_sem, 0)
            chain.start(0)
            link = chain.link
            routes = Routes(dve)
            dve.wait_ge(loaded, 160)
            link(dve.memset(route_f[:, :], 0.0))
            link(dve.tensor_copy(route_f[:, SECOND:SECOND + T], route[:, :]))
            for i, first in enumerate((SECOND - FIRST, 0)):
                part = route_f[:, first:first + D_WAYS * D_TURNS].rearrange("p (j k) -> p j k", k=D_WAYS)
                link(dve.tensor_tensor(words[:, i, :, :], part, bcast(digits[:, :].unsqueeze(1), [1, D_TURNS, D_WAYS]),
                                       ALU.mult))
            link(dve.tensor_reduce(word_sum[:, :, :], words[:, :, :, :], AX.X, ALU.add))
            dve.tensor_copy(packed[:, :, :], word_sum[:, :, :]).then_inc(words_ready, 1)
            dve.wait_ge(words_ready, 1)
            combine_weights(dve, 0)
            dve.wait_ge(weights_ready, 4)

            def normalise(t, k):
                if has(t, 2):
                    dve.wait_ge(turned, t - 1)
                dve.tensor_scalar(lnb[k % 2][:, :], XC[:, bass.ds(t, 1), :].rearrange("p o d -> p (o d)"),
                                  R[:, bass.ds(t, 1)], None, ALU.mult).then_inc(ln_ready, 1)

            def layer(n, phase, bank, dst, done, readers, ready):
                def run(t, k):
                    e = routes.of(k, phase)
                    dve.wait_ge(done, t + 1)
                    if has(t, 2):
                        dve.wait_ge(readers, t - 1)
                    dve.tensor_tensor(dst[k % 2][:, :], bank[:, 0:MID],
                                      br[:, n, bass.ds(e, 1), :].rearrange("p o f -> p (o f)"), ALU.add).then_inc(ready, 1)
                return run

            def add(t, k):
                dve.wait_ge(out_done, t + 1)
                xt = X[:, bass.ds(t, 1), :].rearrange("p o d -> p (o d)")
                dve.tensor_tensor(xt, bY[:, 0:D], xt, ALU.add).then_inc(x_done, 1)

            software_pipeline(dve, [normalise, None, None, layer(0, FIRST, b1, h1, mm1_done, turned1, h1_ready), None,
                                    layer(1, SECOND, b2, h2, mm2_done, turned2, h2_ready), None, add],
                              T, D_WAYS, routes.turn)


def edge_attention(nc, g_in, X, XC, R, ident, banks):
    with ExitStack() as stack:
        sc = Scope(nc, stack, "E")
        SLOPE, FAR = 0.2, 9e15
        adj = sc.sb("adj", [P, T, NODES])
        w1, w2 = sc.sb("w1", [P, D]), sc.sb("w2", [P, D])
        w3 = sc.sb("w3", [P, 2])
        v1, v2 = sc.sb("v1", [P, P]), sc.sb("v2", [P, P])
        deg, some, rdeg = (sc.sb(n, [P, T]) for n in ("deg", "some", "rdeg"))
        ring = lambda name, shape: [sc.sb(f"{name}{u}", shape) for u in range(2)]
        lnb, lnT, pD, pT = (ring(n, [P, GT, P]) for n in ("lnb", "lnT", "pD", "pT"))
        s1, s2j, e, mask, a = (ring(n, [P, GT, NODES]) for n in ("s1", "s2j", "e", "mask", "a"))
        s2, top, inv = (ring(n, [P, GT]) for n in ("s2", "top", "inv"))
        (loaded, zeroed, v_done, chain_sem, setup, ln_ready, kept, turned, lnT_ready, sums_done, s1_ready, s2_read,
         pre_ready, alpha_ready, e_chain, a_chain, mask_ready, shifted, exp_done, inv_ready, pD_ready, p_turned,
         pT_ready, edge_done, x_done) = (sc.sem(n) for n in (
             "loaded", "zeroed", "v_done", "chain", "setup", "ln_ready", "kept", "turned", "lnT_ready", "sums_done",
             "s1_ready", "s2_read", "pre_ready", "alpha_ready", "e_chain", "a_chain", "mask_ready", "shifted",
             "exp_done", "inv_ready", "pD_ready", "p_turned", "pT_ready", "edge_done", "x_done"))
        begun = sc.sem("begun")
        bX, b1, b2, bP, bY = banks[0:5]
        halves = [slice(0, NODES), slice(NODES, P)]
        tiles = lambda bank: bank[:, :].rearrange("p (t d) -> p t d", t=GT)
        block = stack.enter_context(nc.Block())

        @block.sync
        def _(sp):
            sp.dma_start(adj[:, :, :], g_in["adj"].rearrange("(t p) j -> p t j", p=P)).then_inc(loaded, 16)
            for buf, name in ((w1, "L2_gnn_W1"), (w2, "L2_gnn_W2"), (w3, "L2_gnn_w3")):
                sp.dma_start(buf[:, :], g_in[name]).then_inc(loaded, 16)

        @block.tensor
        def _(pe):
            pe.wait_ge(loaded, 64)
            nc.tensor.matmul(b1[:, 0:1], w1[:, :], w3[:, 0:1], start=True, stop=True)
            nc.tensor.matmul(b1[:, 1:2], w2[:, :], w3[:, 1:2], start=True, stop=True).then_inc(v_done, 1)

            def turn(g, u):
                pe.wait_ge(ln_ready, g + 1)
                if has(g, 1):
                    pe.wait_ge(lnT_ready, g)
                for j in range(GT):
                    last = nc.tensor.transpose(bX[:, j * P:(j + 1) * P], lnb[u][:, j, :], ident[:, :])
                last.then_inc(turned, 1)

            def sums(g, u):
                pe.wait_ge(lnT_ready, g + 1)
                if has(g, 1):
                    pe.wait_ge(s1_ready, g)
                    pe.wait_ge(s2_read, g)
                rhs = lnT[u][:, :, :].rearrange("p t q -> p (t q)")
                nc.tensor.matmul(b1[:, :], v1[:, :], rhs, start=True, stop=True)
                nc.tensor.matmul(b2[:, :], v2[:, :], rhs, start=True, stop=True).then_inc(sums_done, 1)

            def turn_p(g, u):
                pe.wait_ge(pD_ready, g + 1)
                if has(g, 1):
                    pe.wait_ge(pT_ready, g)
                for j in range(GT):
                    last = nc.tensor.transpose(bP[:, j * P:(j + 1) * P], pD[u][:, j, :], ident[:, :])
                last.then_inc(p_turned, 1)

            def edges(g, u):
                pe.wait_ge(pT_ready, g + 1)
                pe.wait_ge(kept, g + 1)
                if has(g, 1):
                    pe.wait_ge(x_done, g)
                for j in range(GT):
                    last = nc.tensor.matmul(bY[:, j * D:(j + 1) * D], pT[u][:, j, :],
                                            XC[:, bass.ds(g * GT + j, 1), :].rearrange("p o d -> p (o d)"),
                                            start=True, stop=True)
                last.then_inc(edge_done, 1)

            pe.wait_ge(setup, 1)
            software_pipeline(pe, [None, turn, sums, None, turn_p, edges], NG)

        @block.scalar
        def _(act):
            def turn(g, u):
                act.wait_ge(ln_ready, g + 1)
                nc.scalar.activation(group(XC, g), lnb[u][:, :, :], ACT.Copy).then_inc(kept, 1)
                act.wait_ge(turned, g + 1)
                if has(g, 2):
                    act.wait_ge(sums_done, g - 1)
                nc.scalar.activation(lnT[u][:, :, :], tiles(bX), ACT.Copy).then_inc(lnT_ready, 1)

            def sums(g, u):
                act.wait_ge(sums_done, g + 1)
                if has(g, 2):
                    act.wait_ge(e_chain, (g - 1) * 5)
                for b, h in enumerate(halves):
                    last = nc.scalar.activation(s1[u][h, :, :], tiles(b1)[h, :, h], ACT.Copy)
                last.then_inc(s1_ready, 1)

            def alpha(g, u):
                act.wait_ge(pre_ready, g + 1)
                nc.scalar.activation(e[u][:, :, :], e[u][:, :, :], ACT.Exp).then_inc(alpha_ready, 1)

            def second(g, u):
                act.wait_ge(shifted, g + 1)
                nc.scalar.activation(a[u][:, :, :], a[u][:, :, :], ACT.Exp).then_inc(exp_done, 1)

            def turn_p(g, u):
                act.wait_ge(p_turned, g + 1)
                if has(g, 2):
                    act.wait_ge(edge_done, g - 1)
                nc.scalar.activation(pT[u][:, :, :], tiles(bP), ACT.Copy).then_inc(pT_ready, 1)

            def sums_and_alpha(g, u):
                sums(g, u)
                alpha(g, u)

            software_pipeline(act, [None, turn, sums_and_alpha, second, turn_p, None], NG)

        @block.gpsimd
        def _(pool):
            for u in range(2):
                nc.gpsimd.memset(pD[u][:, :, :], 0.0).then_inc(zeroed, 1)
            pool.wait_ge(zeroed, 2)

            def place(g, u):
                pool.wait_ge(exp_done, g + 1)
                if has(g, 2):
                    pool.wait_ge(p_turned, g - 1)
                pool.sem_inc(begun, 1)
                for b, h in enumerate(halves):
                    last = nc.gpsimd.tensor_copy(pD[u][h, :, h], a[u][h, :, :])
                last.then_inc(pD_ready, 1)

            software_pipeline(pool, [None, None, None, place, None, None], NG)

        @block.vector
        def _(dve):
            chain = Chain(dve, chain_sem, 0)
            chain.start(0)
            link = chain.link
            dve.wait_ge(loaded, 64)
            dve.wait_ge(v_done, 1)
            link(dve.tensor_copy(v1[:, :], bcast(b1[:, 0:1], [P, P])))
            link(dve.tensor_copy(v2[:, :], bcast(b1[:, 1:2], [P, P])))
            link(dve.tensor_reduce(deg[:, :], adj[:, :, :], AX.X, ALU.add))
            link(dve.tensor_scalar(some[:, :], deg[:, :], 0.0, None, ALU.is_gt))
            link(dve.tensor_tensor(deg[:, :], deg[:, :], some[:, :], ALU.mult))
            link(dve.tensor_scalar(some[:, :], some[:, :], -1.0, 1.0, ALU.mult, ALU.add))
            link(dve.tensor_tensor(deg[:, :], deg[:, :], some[:, :], ALU.add))
            dve.reciprocal(rdeg[:, :], deg[:, :]).then_inc(setup, 1)
            dve.wait_ge(setup, 1)
            e_links = Chain(dve, e_chain, 5)
            a_links = Chain(dve, a_chain, 4)

            def normalise(g, u):
                if has(g, 2):
                    dve.wait_ge(turned, g - 1)
                    dve.wait_ge(kept, g - 1)
                dve.tensor_tensor(lnb[u][:, :, :], group(XC, g),
                                  bcast(R[:, bass.ds(g * GT, GT)].unsqueeze(2), [P, GT, D]),
                                  ALU.mult).then_inc(ln_ready, 1)

            def wide(ap):
                return bcast(ap.unsqueeze(2), [P, GT, NODES])

            def before_alpha(g, u):
                e_links.start(g)
                dve.wait_ge(sums_done, g + 1)
                for b, h in enumerate(halves):
                    last = dve.tensor_tensor(s2j[u][h, :, :], group(adj, g)[h, :, :], tiles(b2)[h, :, h], ALU.mult)
                last.then_inc(s2_read, 1)
                dve.wait_ge(s2_read, g + 1)
                e_links.link(dve.tensor_reduce(s2[u][:, :], s2j[u][:, :, :], AX.X, ALU.add))
                e_links.link(dve.tensor_tensor(s2[u][:, :], s2[u][:, :], rdeg[:, bass.ds(g * GT, GT)], ALU.mult))
                dve.wait_ge(s1_ready, g + 1)
                e_links.link(dve.tensor_tensor(e[u][:, :, :], s1[u][:, :, :], wide(s2[u][:, :]), ALU.add))
                e_links.link(dve.tensor_tensor(e[u][:, :, :], e[u][:, :, :], group(adj, g), ALU.mult))
                e_links.link(dve.tensor_scalar(mask[u][:, :, :], group(adj, g), 0.0, None, ALU.is_gt))
                dve.scalar_tensor_tensor(e[u][:, :, :], e[u][:, :, :], SLOPE, e[u][:, :, :], ALU.mult,
                                         ALU.max).then_inc(pre_ready, 1)

            def after_alpha(g, u):
                a_links.start(g)
                dve.wait_ge(alpha_ready, g + 1)
                if has(g, 2):
                    dve.wait_ge(pD_ready, g - 1)
                a_links.link(dve.tensor_tensor(a[u][:, :, :], e[u][:, :, :], mask[u][:, :, :], ALU.mult))
                a_links.link(dve.tensor_scalar(mask[u][:, :, :], mask[u][:, :, :], -1.0, FAR, ALU.add, ALU.mult))
                a_links.link(dve.tensor_tensor(a[u][:, :, :], a[u][:, :, :], mask[u][:, :, :], ALU.add))
                a_links.link(dve.tensor_reduce(top[u][:, :], a[u][:, :, :], AX.X, ALU.max))
                dve.tensor_tensor(a[u][:, :, :], a[u][:, :, :], wide(top[u][:, :]), ALU.subtract).then_inc(shifted, 1)

            def totals(g, u):
                dve.wait_ge(exp_done, g + 1)
                dve.tensor_reduce(inv[u][:, :], a[u][:, :, :], AX.X, ALU.add).then_inc(inv_ready, 1)
                dve.wait_ge(inv_ready, g * 2 + 1)
                dve.reciprocal(inv[u][:, :], inv[u][:, :]).then_inc(inv_ready, 1)

            def add(g, u):
                dve.wait_ge(edge_done, g + 1)
                dve.wait_ge(inv_ready, g * 2 + 2)
                for j in range(GT):
                    xt = X[:, bass.ds(g * GT + j, 1), :].rearrange("p o d -> p (o d)")
                    last = dve.scalar_tensor_tensor(xt, bY[:, j * D:(j + 1) * D], inv[u][:, j:j + 1], xt,
                                                    ALU.mult, ALU.add)
                last.then_inc(x_done, 1)

            software_pipeline(dve, [normalise, None, before_alpha, after_alpha, totals, add], NG)


class Experts:

    def __init__(self, name, src, top_k, hidden, capacity, act, tiles):
        self.name, self.src, self.top_k, self.hidden = name, src, top_k, hidden
        self.capacity, self.act, self.tiles = capacity, act, tiles
        self.chunks = [(c, min(P, hidden - c)) for c in range(0, hidden, P)]
        self.gated = act == "silu"


E = 8
ROW = D + 2
NO_ROW = 1 << 30
L0_CAPACITY = -(-5 * TOKENS // (4 * E))
WAYS = 8
UP, DOWN = 2, 4
TURNS = (2 * T + E + 5) // WAYS + 1
SPARE = E
EXPERTS = {
    "B": Experts("B", "L0_ffn", 1, 512, L0_CAPACITY, "relu", E * L0_CAPACITY // P),
    "F": Experts("F", "L2_ffn", 2, 341, None, "silu", 2 * T + SPARE),
    "H": Experts("H", "L3_ffn", 2, 256, None, "gelu", 2 * T + SPARE),
}


def prefill(nc, stack, scratch):
    sc = Scope(nc, stack, "fill")
    blank = sc.sb("blank", [P, ROW])
    blank_ready, filled = sc.sem("blank_ready"), sc.sem("filled")
    count = 0
    with nc.Block() as block:
        @block.vector
        def _(dve):
            dve.memset(blank[:, 0:D + 1], 0.0).then_inc(blank_ready, 1)
            dve.memset(blank[:, D + 1:ROW].bitcast(U32), NO_ROW).then_inc(blank_ready, 1)

        @block.sync
        def _(sp):
            sp.wait_ge(blank_ready, 2)
            for name, (rows, result) in scratch.items():
                n = EXPERTS[name].tiles
                sp.dma_start(rows.rearrange("(n p) c -> p n c", p=P),
                             bcast(blank[:, :].unsqueeze(1), [P, n, ROW])).then_inc(filled, 16)
                if name == "B":
                    sp.dma_start(result.rearrange("(n p) c -> p n c", p=P),
                                 bcast(blank[:, 0:D].unsqueeze(1), [P, T, D])).then_inc(filled, 16)
    return filled, 16 * (len(scratch) + ("B" in scratch))


def expert_logits(nc, m, g_in, XC, R, LOG, ident, banks):
    with ExitStack() as stack:
        sc = Scope(nc, stack, m.name + "1")
        affine, biased = m.act == "gelu", m.act != "silu"
        gate = sc.sb("gate", [P, E])
        gate_b = sc.sb("gate_b", [P, E])
        gamma = sc.sb("gamma", [P, D])
        beta = sc.sb("beta", [P, D])
        lnb = [sc.sb(f"lnb{u}", [P, GT, D]) for u in range(2)]
        lnT = [sc.sb(f"lnT{u}", [P, GT, P]) for u in range(2)]
        loaded, ln_chain, ln_ready = sc.sem("loaded"), sc.sem("ln_chain"), sc.sem("ln_ready")
        turned, lnT_ready, kept = sc.sem("turned"), sc.sem("lnT_ready"), sc.sem("kept")
        logits_done, logits_read = sc.sem("logits_done"), sc.sem("logits_read")
        pT, pL = banks[0:2]
        loads = 16 * (1 + biased + 2 * affine)
        block = stack.enter_context(nc.Block())

        @block.sync
        def _(sp):
            sp.dma_start(gate[:, :], g_in[m.src + "_gate"]).then_inc(loaded, 16)
            if biased:
                sp.dma_start(gate_b[:, :], bcast(g_in[m.src + "_gate_b"], [P, E])).then_inc(loaded, 16)
            if affine:
                sp.dma_start(gamma[:, :], bcast(g_in[m.src + "_gamma"], [P, D])).then_inc(loaded, 16)
                sp.dma_start(beta[:, :], bcast(g_in[m.src + "_beta"], [P, D])).then_inc(loaded, 16)

        @block.vector
        def _(dve):
            dve.wait_ge(loaded, loads)

            def normalise(g, u):
                if has(g, 2):
                    dve.wait_ge(turned, g - 1)
                    dve.wait_ge(kept, g - 1)
                ins = dve.tensor_tensor(lnb[u][:, :, :], group(XC, g),
                                        bcast(R[:, bass.ds(g * GT, GT)].unsqueeze(2), [P, GT, D]), ALU.mult)
                if affine:
                    ins.then_inc(ln_chain, 1)
                    dve.wait_ge(ln_chain, g * 2 + 1)
                    dve.tensor_tensor(lnb[u][:, :, :], lnb[u][:, :, :],
                                      bcast(gamma[:, :].unsqueeze(1), [P, GT, D]), ALU.mult).then_inc(ln_chain, 1)
                    dve.wait_ge(ln_chain, g * 2 + 2)
                    ins = dve.tensor_tensor(lnb[u][:, :, :], lnb[u][:, :, :],
                                            bcast(beta[:, :].unsqueeze(1), [P, GT, D]), ALU.add)
                ins.then_inc(ln_ready, 1)

            def logits(g, u):
                dve.wait_ge(logits_done, g + 1)
                src = pL[:, 0:GT * E].rearrange("p (t e) -> p t e", t=GT)
                if biased:
                    dve.tensor_tensor(group(LOG, g), src, bcast(gate_b[:, :].unsqueeze(1), [P, GT, E]),
                                      ALU.add).then_inc(logits_read, 1)
                else:
                    dve.tensor_copy(group(LOG, g), src).then_inc(logits_read, 1)

            software_pipeline(dve, [normalise, None, logits], NG)

        @block.tensor
        def _(pe):
            def turn(g, u):
                pe.wait_ge(ln_ready, g + 1)
                if has(g, 1):
                    pe.wait_ge(lnT_ready, g)
                for j in range(GT):
                    last = nc.tensor.transpose(pT[:, j * P:(j + 1) * P], lnb[u][:, j, :], ident[:, :])
                last.then_inc(turned, 1)

            def logits(g, u):
                pe.wait_ge(lnT_ready, g + 1)
                if has(g, 1):
                    pe.wait_ge(logits_read, g)
                for j in range(GT):
                    last = nc.tensor.matmul(pL[:, j * E:(j + 1) * E], lnT[u][:, j, :], gate[:, :],
                                            start=True, stop=True)
                last.then_inc(logits_done, 1)

            pe.wait_ge(loaded, loads)
            software_pipeline(pe, [None, turn, logits], NG)

        @block.scalar
        def _(act):
            def turn(g, u):
                act.wait_ge(ln_ready, g + 1)
                nc.scalar.activation(group(XC, g), lnb[u][:, :, :], ACT.Copy).then_inc(kept, 1)
                act.wait_ge(turned, g + 1)
                if has(g, 2):
                    act.wait_ge(logits_done, g - 1)
                nc.scalar.activation(lnT[u][:, :, :], pT[:, :].rearrange("p (t d) -> p t d", t=GT),
                                     ACT.Copy).then_inc(lnT_ready, 1)

            software_pipeline(act, [None, turn, None], NG)


def route(nc, m, g_in, LOG, META, ROWS, TILE_E, banks):
    with ExitStack() as stack:
        sc = Scope(nc, stack, m.name + "2")
        K, NT = m.top_k, m.tiles
        tri = sc.sb("tri", [P, P])
        ones = sc.sb("ones", [P, P])
        steps = sc.sb("steps", [P, T])
        tile_no = sc.sb("tile_no", [P, NT])
        places = sc.sb("places", [P, T, 2], U32)
        top = [sc.sb(f"top{k}", [P, T]) for k in range(K)]
        masked = sc.sb("masked", [P, T, E])
        equal = sc.sb("equal", [P, T, E])
        taken = sc.sb("taken", [P, 2, T])
        chosen = [sc.sb(f"chosen{k}", [P, T, E]) for k in range(K)]
        any_chosen = sc.sb("any_chosen", [P, T, E])
        z = sc.sb("z", [P, T, E])
        esum = sc.sb("esum", [P, T])
        inv = sc.sb("inv", [P, T])
        e2 = sc.sb("e2", [P, T])
        tot = sc.sb("tot", [P, E, T])
        cum = sc.sb("cum", [P, E, T])
        cmp = sc.sb("cmp", [P, E, T])
        cmp2 = sc.sb("cmp2", [P, NT, E])
        nt = sc.sb("nt", [P, E])
        nt_cum = sc.sb("nt_cum", [P, E])
        off = sc.sb("off", [P, E])
        pos = sc.sb("pos", [P, T, E])
        row = sc.sb("row", [P, T])
        over = sc.sb("over", [P, T])
        tile_e = sc.sb("tile_e", [1, DOWN + WAYS * TURNS])
        digits = sc.sb("digits", [1, WAYS])
        words = sc.sb("words", [1, 2, TURNS, WAYS])
        word_sum = sc.sb("word_sum", [1, 2, TURNS])
        loaded, chain_sem = sc.sem("loaded"), sc.sem("chain")
        z_ready, exp_done, chosen_ready = sc.sem("z_ready"), sc.sem("exp_done"), sc.sem("chosen_ready")
        counted = sc.sem("counted")
        pU, pO = banks[0:2]
        block = stack.enter_context(nc.Block())

        @block.sync
        def _(sp):
            sp.dma_start(tri[:, :], g_in["c_tri"]).then_inc(loaded, 16)
            sp.dma_start(digits[:, :], g_in["c_digits"]).then_inc(loaded, 16)
            sp.dma_start(ones[:, :], g_in["c_ones"]).then_inc(loaded, 16)
            sp.dma_start(steps[:, :], bcast(g_in["c_steps"], [P, T])).then_inc(loaded, 16)
            sp.dma_start(tile_no[:, :], bcast(g_in["c_tile_no"][:, 0:NT], [P, NT])).then_inc(loaded, 16)
            sp.dma_start(places[:, :, :], g_in["c_places"]).then_inc(loaded, 16)

        @block.scalar
        def _(act):
            act.wait_ge(z_ready, 1)
            nc.scalar.activation(z[:, :, :], z[:, :, :], ACT.Exp).then_inc(exp_done, 1)
            if K == 2:
                act.wait_ge(z_ready, 2)
                nc.scalar.activation(e2[:, :], e2[:, :], ACT.Exp).then_inc(exp_done, 1)

        @block.tensor
        def _(pe):
            pe.wait_ge(loaded, 96)
            pe.wait_ge(chosen_ready, 1)
            flat = any_chosen[:, :, :].rearrange("p t e -> p (t e)")
            nc.tensor.matmul(pU[:, :], tri[:, :], flat, start=True, stop=True).then_inc(counted, 1)
            nc.tensor.matmul(pO[:, :], ones[:, :], flat, start=True, stop=True).then_inc(counted, 1)

        @block.vector
        def _(dve):
            chain = Chain(dve, chain_sem, 0)
            chain.start(0)
            link = chain.link

            def wide(ap):
                return bcast(ap.unsqueeze(2), [P, T, E])

            dve.wait_ge(loaded, 96)
            for k in range(K):
                src = LOG if k == 0 else masked
                link(dve.tensor_reduce(top[k][:, :], src[:, :, :], AX.X, ALU.max))
                link(dve.tensor_tensor(equal[:, :, :], src[:, :, :], wide(top[k][:, :]), ALU.is_equal))
                link(dve.memset(taken[:, 0, :], 0.0))
                for e in range(E):
                    link(dve.tensor_tensor(chosen[k][:, :, e], equal[:, :, e], taken[:, e % 2, :], ALU.is_gt))
                    link(dve.tensor_tensor(taken[:, (e + 1) % 2, :], equal[:, :, e], taken[:, e % 2, :], ALU.max))
                if k == 0:
                    dve.tensor_tensor(z[:, :, :], LOG[:, :, :], wide(top[0][:, :]),
                                      ALU.subtract).then_inc(z_ready, 1)
                    if K == 2:
                        link(dve.scalar_tensor_tensor(masked[:, :, :], chosen[0][:, :, :], -1e30, LOG[:, :, :],
                                                      ALU.mult, ALU.add))
            if K == 2:
                dve.tensor_tensor(e2[:, :], top[1][:, :], top[0][:, :], ALU.subtract).then_inc(z_ready, 1)
                dve.tensor_tensor(any_chosen[:, :, :], chosen[0][:, :, :], chosen[1][:, :, :],
                                  ALU.add).then_inc(chosen_ready, 1)
            else:
                dve.tensor_copy(any_chosen[:, :, :], chosen[0][:, :, :]).then_inc(chosen_ready, 1)

            dve.wait_ge(exp_done, K)
            weights = [META[:, :, k, 0] for k in range(K)]
            if m.name == "H":
                link(dve.tensor_scalar(esum[:, :], e2[:, :], 1.0, None, ALU.add))
                link(dve.reciprocal(weights[0], esum[:, :]))
                link(dve.tensor_tensor(weights[1], e2[:, :], weights[0], ALU.mult))
            else:
                link(dve.tensor_reduce(esum[:, :], z[:, :, :], AX.X, ALU.add))
                link(dve.reciprocal(inv[:, :], esum[:, :]))
                if K == 1:
                    link(dve.tensor_copy(weights[0], inv[:, :]))
                else:
                    link(dve.tensor_tensor(e2[:, :], e2[:, :], inv[:, :], ALU.mult))
                    link(dve.tensor_tensor(esum[:, :], e2[:, :], inv[:, :], ALU.add))
                    link(dve.tensor_scalar(esum[:, :], esum[:, :], 1e-9, None, ALU.add))
                    link(dve.reciprocal(over[:, :], esum[:, :]))
                    link(dve.tensor_tensor(weights[0], inv[:, :], over[:, :], ALU.mult))
                    link(dve.tensor_tensor(weights[1], e2[:, :], over[:, :], ALU.mult))
            for k in range(K):
                link(dve.tensor_copy(META[:, :, k, 1].bitcast(U32), places[:, :, k]))

            dve.wait_ge(counted, 2)
            link(dve.tensor_copy(tot[:, :, :], pO[:, :].rearrange("p (t e) -> p e t", e=E)))
            for e in range(E):
                link(dve.tensor_tensor_scan(cum[:, e, :], ones[:, 0:T], tot[:, e, :], 0.0, ALU.mult, ALU.add))
            link(dve.tensor_tensor(tot[:, :, :], cum[:, :, :], tot[:, :, :], ALU.subtract))
            link(dve.tensor_tensor(pos[:, :, :], pU[:, :].rearrange("p (t e) -> p t e", e=E),
                                   tot[:, :, :].rearrange("p e t -> p t e"), ALU.add))
            if m.capacity is None:
                link(dve.tensor_tensor(cmp[:, :, :], bcast(cum[:, :, T - 1:T], [P, E, T]),
                                       bcast(steps[:, :].unsqueeze(1), [P, E, T]), ALU.is_gt))
                link(dve.tensor_reduce(nt[:, :], cmp[:, :, :], AX.X, ALU.add))
                link(dve.tensor_tensor_scan(nt_cum[:, :], ones[:, 0:E], nt[:, :], 0.0, ALU.mult, ALU.add))
                link(dve.tensor_tensor(off[:, :], nt_cum[:, :], nt[:, :], ALU.subtract))
                link(dve.tensor_scalar(off[:, :], off[:, :], float(P), -1.0, ALU.mult, ALU.add))
            else:
                link(dve.tensor_scalar(nt_cum[:, :], tile_no[:, 0:E], 1.0, float(m.capacity // P), ALU.add, ALU.mult))
                link(dve.tensor_scalar(off[:, :], tile_no[:, 0:E], float(m.capacity), -1.0, ALU.mult, ALU.add))
            link(dve.tensor_tensor(cmp2[:, :, 0:E - 1], bcast(nt_cum[:, 0:E - 1].unsqueeze(1), [P, NT, E - 1]),
                                   bcast(tile_no[:, :].unsqueeze(2), [P, NT, E - 1]), ALU.is_le))
            link(dve.memset(tile_e[:, :], 0.0))
            link(dve.tensor_reduce(tile_e[:, DOWN:DOWN + NT], cmp2[0:1, :, 0:E - 1], AX.X, ALU.add))
            for i, first in enumerate((DOWN - UP, 0)):
                part = tile_e[:, first:first + WAYS * TURNS].rearrange("p (j k) -> p j k", k=WAYS)
                link(dve.tensor_tensor(words[:, i, :, :], part, bcast(digits[:, :].unsqueeze(1), [1, TURNS, WAYS]),
                                       ALU.mult))
            link(dve.tensor_reduce(word_sum[:, :, :], words[:, :, :, :], AX.X, ALU.add))
            link(dve.tensor_copy(TILE_E[:, :, :], word_sum[:, :, :]))
            for k in range(K):
                if m.capacity is not None:
                    link(dve.tensor_tensor(masked[:, :, :], pos[:, :, :], chosen[k][:, :, :], ALU.mult))
                    link(dve.tensor_reduce(over[:, :], masked[:, :, :], AX.X, ALU.add))
                    link(dve.tensor_scalar(over[:, :], over[:, :], float(m.capacity), 1e6, ALU.is_gt, ALU.mult))
                link(dve.tensor_tensor(equal[:, :, :], pos[:, :, :], bcast(off[:, :].unsqueeze(1), [P, T, E]),
                                       ALU.add))
                link(dve.tensor_tensor(equal[:, :, :], equal[:, :, :], chosen[k][:, :, :], ALU.mult))
                link(dve.tensor_reduce(row[:, :], equal[:, :, :], AX.X, ALU.add))
                if m.capacity is not None:
                    link(dve.tensor_tensor(row[:, :], row[:, :], over[:, :], ALU.add))
                link(dve.tensor_copy(ROWS[:, :, k], row[:, :]))


def dispatch(nc, m, XC, META, ROWS, rows, filled, fills):
    with ExitStack() as stack:
        sc = Scope(nc, stack, m.name + "3")
        K, n_rows = m.top_k, m.tiles * P
        stage = [sc.sb(f"stage{u}", [P, K, ROW]) for u in range(2)]
        index = [[sc.sb(f"index{u}_{k}", [P, 1], U32) for k in range(K)] for u in range(2)]
        begun = sc.sem("begun")
        x_staged, meta_staged, sent = sc.sem("x_staged"), sc.sem("meta_staged"), sc.sems("sent")
        block = stack.enter_context(nc.Block())

        def free(eng, t, u):
            if has(t, 2):
                eng.wait_ge(sent[u], (t - u) * (8 * K))

        @block.scalar
        def _(act):
            def copy_x(t, u):
                free(act, t, u)
                nc.scalar.activation(stage[u][:, :, 0:D], bcast(XC[:, bass.ds(t, 1), :], [P, K, D]),
                                     ACT.Copy).then_inc(x_staged, 1)

            software_pipeline(act, [copy_x, None], T)

        @block.vector
        def _(dve):
            def copy_meta(t, u):
                free(dve, t, u)
                dve.tensor_copy(stage[u][:, :, D:ROW].bitcast(U32),
                                META[:, bass.ds(t, 1), :, :].rearrange("p o k c -> p (o k) c").bitcast(U32)
                                ).then_inc(meta_staged, 1)
                for k in range(K):
                    dve.tensor_copy(index[u][k][:, :], ROWS[:, bass.ds(t, 1), k]).then_inc(meta_staged, 1)

            software_pipeline(dve, [copy_meta, None], T)

        @block.gpsimd
        def _(pool):
            pool.wait_ge(filled, fills)

            last_row = pool.to_reg(n_rows - 1)

            def send(t, u):
                pool.wait_ge(x_staged, t + 1)
                pool.wait_ge(meta_staged, (t + 1) * (1 + K))
                pool.sem_inc(begun, 1)
                for k in range(K):
                    pool.indirect_dma_start(rows, bass.IndirectOffsetOnAxis(ap=index[u][k][:, :], axis=0),
                                            stage[u][:, k, :], None, bounds_check=last_row,
                                            oob_is_err=False).then_inc(sent[u], 16)

            software_pipeline(pool, [None, send], T)
            for u in range(2):
                pool.wait_ge(sent[u], 16 * K * T // 2)


def run_experts(nc, m, g_in, TILE_E, rows, result, ident, banks):
    with ExitStack() as stack:
        sc = Scope(nc, stack, m.name + "4")
        NT, H, C = m.tiles, m.hidden, len(m.chunks)
        w_up = sc.sb("w_up", [P, E, H])
        w_gate = sc.sb("w_gate", [P, E, H]) if m.gated else None
        w_down = sc.sb("w_down", [P, E, C, D])
        b_up = None if m.gated else sc.sb("b_up", [P, E, H])
        b_down = None if m.gated else sc.sb("b_down", [P, E, D])
        xt = [sc.sb(f"xt{u}", [P, ROW]) for u in range(WAYS)]
        xT = [sc.sb(f"xT{u}", [P, P]) for u in range(2)]
        h = [sc.sb(f"h{u}", [P, H]) for u in range(2)]
        act_h = [sc.sb(f"act_h{u}", [P, H]) for u in range(2)]
        hT = [sc.sb(f"hT{u}", [P, C, P]) for u in range(2)]
        y = [sc.sb(f"y{u}", [P, D]) for u in range(WAYS)]
        yc = [sc.sb(f"yc{u}", [P, D]) for u in range(2)]
        no_number = [sc.sb(f"no_number{u}", [P, D], U32) for u in range(2)]
        finite = [sc.sb(f"finite{u}", [P, D], U32) for u in range(2)]
        zeros = sc.sb("zeros", [P, D])
        loaded, x_in = sc.sem("loaded"), sc.sems("x_in", WAYS)
        begun = sc.sem("begun")
        turned, xT_ready, up_done, h_ready = sc.sem("turned"), sc.sem("xT_ready"), sc.sem("up_done"), sc.sem("h_ready")
        act_ready, h_turned, hT_ready = sc.sem("act_ready"), sc.sem("h_turned"), sc.sem("hT_ready")
        down_done, down_read, y_ready = sc.sem("down_done"), sc.sem("down_read"), sc.sem("y_ready")
        settled = sc.sem("settled")
        zeroed, chain_sem, out = sc.sem("zeroed"), sc.sem("chain"), sc.sems("out", WAYS)
        up_read = h_ready if m.act == "gelu" else act_ready
        down_bank_read = y_ready if m.gated else down_read
        pX, pUp, pGate, pH, pY = banks[0:5]
        n_loads = 16 * (C + 1 + (1 if m.gated else 2))
        n_result = m.top_k * TOKENS
        block = stack.enter_context(nc.Block())

        @block.sync
        def _(sp):
            sp.dma_start(w_up[:, :, :], g_in[m.src + "_up"].rearrange("e d f -> d e f")).then_inc(loaded, 16)
            if m.gated:
                sp.dma_start(w_gate[:, :, :], g_in[m.src + "_up3"].rearrange("e d f -> d e f")).then_inc(loaded, 16)
            for c, (f0, nf) in enumerate(m.chunks):
                sp.dma_start(w_down[0:nf, :, c, :],
                             g_in[m.src + "_down"][:, f0:f0 + nf, :].rearrange("e f d -> f e d")).then_inc(loaded, 16)
            if not m.gated:
                sp.dma_start(b_up[:, :, :].rearrange("p e f -> p (e f)"),
                             bcast(g_in[m.src + "_b_up"], [P, E * H])).then_inc(loaded, 16)
                sp.dma_start(b_down[:, :, :].rearrange("p e f -> p (e f)"),
                             bcast(g_in[m.src + "_b_down"], [P, E * D])).then_inc(loaded, 16)

            def load(t, w):
                if has(t, WAYS):
                    sp.wait_ge(out[w], (t - w) * (16 // WAYS))
                sp.dma_start(xt[w][:, :], rows[bass.ds(t * P, P), :]).then_inc(x_in[w], 16)

            software_pipeline(sp, [load] + [None] * 5, NT, WAYS)

        class TileExperts:

            def __init__(self, eng):
                self.eng = eng

            def turn(self, j):
                self.words = [self.eng.value_load(TILE_E[:, i, bass.ds(j, 1)], min_val=0, max_val=E ** WAYS - 1)
                              for i in range(2)]

            def of(self, w, phase):
                return (self.words[phase == DOWN] >> (3 * ((w + phase) % WAYS))) & (E - 1)

        @block.tensor
        def _(pe):
            pe.wait_ge(loaded, n_loads)
            experts = TileExperts(pe)

            def turn(t, w):
                pe.wait_ge(x_in[w], (t - w) * (16 // WAYS) + 16)
                if has(t, 1):
                    pe.wait_ge(xT_ready, t)
                nc.tensor.transpose(pX[:, 0:P], xt[w][:, 0:D], ident[:, :]).then_inc(turned, 1)

            def up(t, w):
                e = experts.of(w, UP)
                pe.wait_ge(xT_ready, t + 1)
                if has(t, 1):
                    pe.wait_ge(up_read, t)
                mm = nc.tensor.matmul(pUp[:, 0:H], xT[w % 2][:, :],
                                      w_up[:, bass.ds(e, 1), :].rearrange("p o f -> p (o f)"), start=True, stop=True)
                if m.gated:
                    mm = nc.tensor.matmul(pGate[:, 0:H], xT[w % 2][:, :],
                                          w_gate[:, bass.ds(e, 1), :].rearrange("p o f -> p (o f)"),
                                          start=True, stop=True)
                mm.then_inc(up_done, 1)

            def turn_h(t, w):
                pe.wait_ge(act_ready, t + 1)
                if has(t, 1):
                    pe.wait_ge(hT_ready, t)
                for c, (f0, nf) in enumerate(m.chunks):
                    last = nc.tensor.transpose(pH[0:nf, c * P:(c + 1) * P], act_h[w % 2][:, f0:f0 + nf], ident[:, :])
                last.then_inc(h_turned, 1)

            def down(t, w):
                e = experts.of(w, DOWN)
                pe.wait_ge(hT_ready, t + 1)
                if has(t, 1):
                    pe.wait_ge(down_bank_read, t)
                for c, (f0, nf) in enumerate(m.chunks):
                    last = nc.tensor.matmul(pY[:, 0:D], hT[w % 2][0:nf, c, :],
                                            w_down[0:nf, bass.ds(e, 1), c, :].rearrange("p o d -> p (o d)"),
                                            start=(c == 0), stop=(c == C - 1))
                last.then_inc(down_done, 1)

            software_pipeline(pe, [None, turn, up, turn_h, down, None], NT, WAYS, experts.turn)

        @block.scalar
        def _(act):
            def turn(t, w):
                act.wait_ge(turned, t + 1)
                if has(t, 2):
                    act.wait_ge(up_done, t - 1)
                nc.scalar.activation(xT[w % 2][:, :], pX[:, 0:P], ACT.Copy).then_inc(xT_ready, 1)

            def activate(t, w):
                if m.gated:
                    act.wait_ge(up_done, t + 1)
                    if has(t, 2):
                        act.wait_ge(act_ready, t - 1)
                    nc.scalar.activation(h[w % 2][:, :], pUp[:, 0:H], ACT.Silu).then_inc(h_ready, 1)
                elif m.act == "gelu":
                    act.wait_ge(h_ready, t + 1)
                    if has(t, 2):
                        act.wait_ge(h_turned, t - 1)
                    nc.scalar.activation(act_h[w % 2][:, :], h[w % 2][:, :], ACT.Gelu).then_inc(act_ready, 1)

            def turn_h(t, w):
                act.wait_ge(h_turned, t + 1)
                if has(t, 2):
                    act.wait_ge(down_done, t - 1)
                func = ACT.Relu if m.act == "relu" else ACT.Copy
                full = H // P
                ins = nc.scalar.activation(hT[w % 2][:, 0:full, :],
                                           pH[:, 0:full * P].rearrange("p (c q) -> p c q", q=P), func)
                if H % P:
                    ins = nc.scalar.activation(hT[w % 2][0:H % P, full, :], pH[0:H % P, full * P:(full + 1) * P], func)
                ins.then_inc(hT_ready, 1)

            software_pipeline(act, [None, turn, activate, turn_h, None, None], NT, WAYS)

        @block.vector
        def _(dve):
            dve.wait_ge(loaded, n_loads)
            chain = Chain(dve, chain_sem, 3)
            experts = TileExperts(dve)
            dve.memset(zeros[:, :], 0.0).then_inc(zeroed, 1)
            dve.wait_ge(zeroed, 1)

            def activate(t, w):
                if m.gated:
                    dve.wait_ge(h_ready, t + 1)
                    if has(t, 2):
                        dve.wait_ge(h_turned, t - 1)
                    dve.tensor_tensor(act_h[w % 2][:, :], h[w % 2][:, :], pGate[:, 0:H], ALU.mult).then_inc(act_ready, 1)
                    return
                e = experts.of(w, UP)
                dve.wait_ge(up_done, t + 1)
                if has(t, 2):
                    dve.wait_ge(h_turned if m.act == "relu" else act_ready, t - 1)
                dst = act_h if m.act == "relu" else h
                ready = act_ready if m.act == "relu" else h_ready
                dve.tensor_tensor(dst[w % 2][:, :], pUp[:, 0:H],
                                  b_up[:, bass.ds(e, 1), :].rearrange("p o f -> p (o f)"), ALU.add).then_inc(ready, 1)

            def finish(t, w):
                weight = xt[w][:, D:D + 1]
                if m.gated:
                    dve.wait_ge(down_done, t + 1)
                    free_y(dve, t, w)
                    dve.tensor_scalar(y[w][:, :], pY[:, 0:D], weight, None, ALU.mult).then_inc(y_ready, 1)
                    return
                e = experts.of(w, DOWN)
                dve.wait_ge(down_done, t + 1)
                free_y(dve, t, w)
                yy, cc = y[w][:, :], yc[w % 2][:, :]
                chain.start(t)
                dve.tensor_tensor(cc, pY[:, 0:D], b_down[:, bass.ds(e, 1), :].rearrange("p o f -> p (o f)"),
                                  ALU.add).then_inc(down_read, 1)
                dve.wait_ge(down_read, t + 1)
                if m.act == "gelu":
                    dve.tensor_scalar(yy, cc, weight, None, ALU.mult).then_inc(y_ready, 1)
                    return
                chain.link(dve.tensor_scalar(cc, cc, weight, None, ALU.mult))
                dve.tensor_scalar(yy, cc, 1e4, -1e4, ALU.min, ALU.max)
                dve.tensor_tensor(no_number[w % 2][:, :], cc, cc, ALU.not_equal)
                chain.link(dve.scalar_tensor_tensor(finite[w % 2][:, :], cc, 0.0, zeros[:, :], ALU.mult, ALU.is_equal))
                dve.sem_inc(settled, 1)
                chain.link(dve.copy_predicated(yy, no_number[w % 2][:, :], zeros[:, :]))
                dve.sem_inc(settled, 1)
                dve.copy_predicated(yy, finite[w % 2][:, :], cc).then_inc(y_ready, 1)

            def free_y(eng, t, w):
                if has(t, WAYS):
                    eng.wait_ge(out[w], (t - w) * (16 // WAYS))

            software_pipeline(dve, [None, None, activate, None, finish, None], NT, WAYS,
                              None if m.gated else experts.turn)

        @block.gpsimd
        def _(pool):
            last_place = pool.to_reg(n_result - 1)

            def send(t, w):
                pool.wait_ge(y_ready, t + 1)
                pool.sem_inc(begun, 1)
                pool.indirect_dma_start(result, bass.IndirectOffsetOnAxis(ap=xt[w][:, D + 1:ROW].bitcast(U32), axis=0),
                                        y[w][:, :], None, bounds_check=last_place,
                                        oob_is_err=False).then_inc(out[w], 16)

            software_pipeline(pool, [None] * 5 + [send], NT, WAYS)
            for w in range(WAYS):
                pool.wait_ge(out[w], 16 * NT // WAYS)


def combine(nc, m, X, result):
    with ExitStack() as stack:
        sc = Scope(nc, stack, m.name + "5")
        K, n = m.top_k, NG // 2
        part = [sc.sb(f"part{u}", [P, K, 2 * GT, D]) for u in range(2)]
        x_done, part_in = sc.sem("x_done"), sc.sems("part_in")
        block = stack.enter_context(nc.Block())

        @block.sync
        def _(sp):
            for g in range(n):
                if g >= 2:
                    sp.wait_ge(x_done, K * (g - 1))
                for k in range(K):
                    src = result[bass.ds(k * TOKENS + g * 2 * GT * P, 2 * GT * P), :]
                    sp.dma_start(part[g % 2][:, k, :, :], src.rearrange("(t p) d -> p t d", p=P)).then_inc(part_in[g % 2], 16)

        @block.vector
        def _(dve):
            for g in range(n):
                dve.wait_ge(part_in[g % 2], 16 * K * (g // 2 + 1))
                xs = X[:, g * 2 * GT:(g + 1) * 2 * GT, :]
                for k in range(K):
                    dve.tensor_tensor(xs, xs, part[g % 2][:, k, :, :], ALU.add).then_inc(x_done, 1)
                    dve.wait_ge(x_done, K * g + k + 1)


def experts_layer(nc, m, g_in, X, XC, R, ident, banks, rows, result, filled, fills):
    layer_norm(nc, "ln" + m.name, X, XC, R, twice=(m.act == "gelu"))
    with ExitStack() as stack:
        sc = Scope(nc, stack, m.name)
        LOG = sc.sb("logits", [P, T, E])
        META = sc.sb("meta", [P, T, m.top_k, 2])
        ROWS = sc.sb("rows", [P, T, m.top_k], U32)
        TILE_E = sc.sb("tile_e", [1, 2, TURNS], I32)
        expert_logits(nc, m, g_in, XC, R, LOG, ident, banks)
        route(nc, m, g_in, LOG, META, ROWS, TILE_E, banks)
        dispatch(nc, m, XC, META, ROWS, rows, filled, fills)
        run_experts(nc, m, g_in, TILE_E, rows, result, ident, banks)
    combine(nc, m, X, result)


def program(nc, g_in, out):
    with ExitStack() as stack:
        sc = Scope(nc, stack, "all")
        X = sc.sb("X", [P, T, D])
        XC = sc.sb("XC", [P, T, D])
        R = sc.sb("R", [P, T])
        ident = sc.sb("ident", [P, P])
        banks = [stack.enter_context(nc.psum_tensor(f"bank{i}", [P, 512], F32)) for i in range(8)]
        x_in, x_out = sc.sem("x_in"), sc.sem("x_out")
        out_bias = {name: sc.sb(name, [P, D]) for name in ("L0_gnn_bo", "L1_ffn_bo")}
        scratch = {
            name: (nc.dram_tensor(f"dram_{name}_rows", (m.tiles * P, ROW), F32).ap(),
                   nc.dram_tensor(f"dram_{name}_result", (m.top_k * TOKENS, D), F32).ap())
            for name, m in EXPERTS.items() if name in STAGES
        }

        with nc.Block() as block:
            @block.sync
            def _(sp):
                sp.dma_start(X[:, :, :], g_in["x"].rearrange("(t p) d -> p t d", p=P)).then_inc(x_in, 16)
                sp.dma_start(ident[:, :], g_in["c_ident"]).then_inc(x_in, 16)
                for name, buf in out_bias.items():
                    sp.dma_start(buf[:, :], bcast(g_in[name], [P, D])).then_inc(x_in, 16)
                sp.wait_ge(x_in, 64)

        filled, fills = prefill(nc, stack, scratch)
        for stage in STAGES:
            if stage in EXPERTS:
                experts_layer(nc, EXPERTS[stage], g_in, X, XC, R, ident, banks, *scratch[stage], filled, fills)
            if stage == "A":
                layer_norm(nc, "lnA", X, XC, R, out_bias["L0_gnn_bo"])
                graph_attention(nc, g_in, X, XC, R, ident, banks)
            if stage == "C":
                layer_norm(nc, "lnC", X, XC, R)
                group_gcns(nc, g_in, X, XC, R, ident, banks)
            if stage == "D":
                layer_norm(nc, "lnD", X, XC, R, out_bias["L1_ffn_bo"])
                routed_mlp(nc, g_in, X, XC, R, ident, banks)
            if stage == "E":
                layer_norm(nc, "lnE", X, XC, R)
                edge_attention(nc, g_in, X, XC, R, ident, banks)
            if stage == "G":
                layer_norm(nc, "lnG", X, XC, R)
                dense_gcn(nc, g_in, X, XC, R, ident, banks)

        with nc.Block() as block:
            @block.sync
            def _(sp):
                sp.dma_start(out.rearrange("(t p) d -> p t d", p=P), X[:, :, :]).then_inc(x_out, 16)
                sp.wait_ge(x_out, 16)


def kernel(**inputs):
    import numpy as np
    import concourse.bacc as bacc
    from concourse.bass_utils import run_bass_kernel_spmd

    a = {n: np.asarray(v) for n, v in inputs.items()}
    slot_adj = np.zeros((128, NODES, NODES), np.float32)
    slot_b2 = np.zeros((P, D), np.float32)
    slot_group = np.zeros((P, len(GROUPS)), np.float32)
    pick = np.zeros((P, P), np.float32)
    for g, nodes in enumerate(GROUPS):
        sl = slice(SLOT0[g], SLOT0[g] + len(nodes))
        slot_adj[:, sl, sl] = a["adj"][:, nodes][:, :, nodes]
        for b in range(2):
            rows = NODES * b + np.arange(sl.start, sl.stop)
            slot_b2[rows] = a["L1_gnn_b2"][g]
            slot_group[rows, g] = 1
            pick[NODES * b + np.array(nodes), rows] = 1
    lay = {
        "x": a["x"].reshape(TOKENS, D),
        "adj": a["adj"].reshape(TOKENS, NODES),
        "adjT": a["adj"].transpose(0, 2, 1).reshape(TOKENS, NODES),
        "nodemask": a["nodemask"].reshape(T, P).T,
        "L3_gnn_W": a["L3_gnn_W"].T,
        "L3_gnn_b": a["L3_gnn_b"].reshape(1, D),
        "L0_gnn_Wq": a["L0_gnn_Wq"].T, "L0_gnn_Wk": a["L0_gnn_Wk"].T, "L0_gnn_Wv": a["L0_gnn_Wv"].T,
        "L0_gnn_Wo": a["L0_gnn_Wo"].T, "L0_gnn_bo": a["L0_gnn_bo"].reshape(1, D),
        "c_head_of": np.repeat(np.eye(HEADS, dtype=np.float32), HD, axis=0),
        "slot_adj": slot_adj.reshape(TOKENS, NODES), "slot_adjT": slot_adj.transpose(0, 2, 1).reshape(TOKENS, NODES),
        "L1_gnn_W1": a["L1_gnn_W1"], "L1_gnn_W2": a["L1_gnn_W2"],
        "L1_gnn_b1": a["L1_gnn_b1"].reshape(len(GROUPS), 2, P).transpose(2, 0, 1),
        "L1_gnn_b2": slot_b2, "L1_gnn_fusion_w": a["L1_gnn_fusion_w"].reshape(1, -1),
        "c_slot_group": slot_group, "c_pick": pick, "c_spread": pick.T,
        "L1_ffn_route_id": a["L1_ffn_route_id"].reshape(1, T),
        "c_hex_digits": (float(ROUTES) ** np.arange(D_WAYS)).astype(np.float32).reshape(1, D_WAYS),
        "L1_ffn_Wr": a["L1_ffn_Wr"].reshape(LAYERS, ROUTES, MID, 2, P).transpose(4, 0, 1, 3, 2),
        "L1_ffn_Ws": a["L1_ffn_Ws"].reshape(LAYERS, MID, 2, P).transpose(3, 0, 2, 1),
        "c_eye2": np.eye(MID, dtype=np.float32).reshape(2, P, MID).transpose(1, 0, 2),
        "L1_ffn_br": a["L1_ffn_br"].reshape(1, -1), "L1_ffn_bs": a["L1_ffn_bs"].reshape(1, -1),
        "L1_ffn_Wi": a["L1_ffn_Wi"].T, "L1_ffn_bi": a["L1_ffn_bi"].reshape(2, P).T,
        "L1_ffn_Wo": a["L1_ffn_Wo"].reshape(D, 2, P).transpose(2, 1, 0), "L1_ffn_bo": a["L1_ffn_bo"].reshape(1, D),
        "L2_gnn_W1": a["L2_gnn_W1"].T, "L2_gnn_W2": a["L2_gnn_W2"].T, "L2_gnn_w3": a["L2_gnn_w3"].reshape(2, P).T,
        "c_ident": np.eye(P, dtype=np.float32),
        "c_tri": np.triu(np.ones((P, P), np.float32)),
        "c_digits": (float(E) ** np.arange(WAYS)).astype(np.float32).reshape(1, WAYS),
        "c_ones": np.ones((P, P), np.float32),
        "c_steps": (np.arange(T, dtype=np.float32) * P).reshape(1, T),
        "c_tile_no": np.arange(2 * T + SPARE, dtype=np.float32).reshape(1, -1),
        "c_places": (np.arange(P)[:, None, None] + np.arange(T)[None, :, None] * P
                     + np.arange(2)[None, None, :] * TOKENS).astype(np.uint32),
        "L0_ffn_gate": a["L0_ffn_gate_w"],
        "L0_ffn_gate_b": a["L0_ffn_gate_b"].reshape(1, E),
        "L0_ffn_up": a["L0_ffn_w1"],
        "L0_ffn_b_up": a["L0_ffn_b1"].reshape(1, -1),
        "L0_ffn_down": a["L0_ffn_w2"],
        "L0_ffn_b_down": a["L0_ffn_b2"].reshape(1, -1),
        "L2_ffn_gate": a["L2_ffn_router_w"].T,
        "L2_ffn_up": a["L2_ffn_w1"].transpose(0, 2, 1),
        "L2_ffn_up3": a["L2_ffn_w3"].transpose(0, 2, 1),
        "L2_ffn_down": a["L2_ffn_w2"].transpose(0, 2, 1),
        "L3_ffn_gate": a["L3_ffn_Wr"],
        "L3_ffn_gate_b": a["L3_ffn_br"].reshape(1, E),
        "L3_ffn_gamma": a["L3_ffn_gamma"].reshape(1, D),
        "L3_ffn_beta": a["L3_ffn_beta"].reshape(1, D),
        "L3_ffn_up": a["L3_ffn_W1"],
        "L3_ffn_b_up": a["L3_ffn_b1"].reshape(1, -1),
        "L3_ffn_down": a["L3_ffn_W2"],
        "L3_ffn_b_down": a["L3_ffn_b2"].reshape(1, -1),
    }
    nc = bacc.Bacc("TRN2", target_bir_lowering=False, num_devices=1)
    arrays, g_in = {}, {}
    for name, v in lay.items():
        v = np.ascontiguousarray(v)
        arrays[f"in_{name}"] = v
        g_in[name] = nc.dram_tensor(f"in_{name}", v.shape, mybir.dt.from_np(v.dtype), kind="ExternalInput").ap()
    out = nc.dram_tensor("out_x", (TOKENS, D), F32, kind="ExternalOutput").ap()
    program(nc, g_in, out)
    r = run_bass_kernel_spmd(nc, [arrays], core_ids=[0])
    return r.results[0]["out_x"].reshape(128, NODES, D)
```

```python
from contextlib import ExitStack

import concourse.bass as bass
from concourse import mybir

STAGES = 'ABCDEFGH'

F32 = mybir.dt.float32
I32 = mybir.dt.int32
U32 = mybir.dt.uint32
ALU = mybir.AluOpType
ACT = mybir.ActivationFunctionType
AX = mybir.AxisListType

P = 128
NODES = 64
D = 128
TOKENS = 128 * NODES
T = TOKENS // P
GT = 4
NG = T // GT
CH = 16
NCH = T // CH
LN_EPS = 1e-5


def software_pipeline(eng, phases, n, ways=2, at_turn=None):
    depth = len(phases) - 1
    first = -(-(depth + 2) // ways) * ways

    def step(s, slot):
        for p in range(depth, -1, -1):
            if phases[p] is not None and (not isinstance(s, int) or 0 <= s - p < n):
                phases[p](s - p, (slot - p) % ways)

    steady = (n - first) // ways
    at_turn = at_turn or (lambda turn: None)
    for s in range(first):
        if s % ways == 0:
            at_turn(s // ways)
        step(s, s % ways)
    with eng.Fori(0, steady) as i:
        at_turn(i + first // ways)
        for k in range(ways):
            step(i * ways + (first + k), k)
    for s in range(first + ways * steady, n + depth):
        if s % ways == 0:
            at_turn(s // ways)
        step(s, s % ways)


def has(item, back):
    return not isinstance(item, int) or item >= back


class Chain:

    def __init__(self, eng, sem, length):
        self.eng, self.sem, self.length = eng, sem, length

    def start(self, item):
        self.base, self.n = item * self.length, 0

    def link(self, ins):
        self.n += 1
        ins.then_inc(self.sem, 1)
        self.eng.wait_ge(self.sem, self.base + self.n)


class Scope:

    def __init__(self, nc, stack, name):
        self.nc, self.stack, self.name, self.held = nc, stack, name, []
        stack.callback(self.release)

    def release(self):
        if self.held:
            self.nc.clear_and_free_semaphores(self.held)
            self.nc.all_engine_barrier()

    def sb(self, name, shape, dt=F32):
        return self.stack.enter_context(self.nc.sbuf_tensor(f"{self.name}_{name}", shape, dt))

    def sem(self, name):
        self.held.append(self.nc.alloc_semaphore(f"{self.name}_{name}"))
        return self.held[-1]

    def sems(self, name, n=2):
        return [self.sem(f"{name}{i}") for i in range(n)]


def bcast(ap, shape):
    return ap.to_broadcast(shape)


def group(buf, g):
    return buf[:, bass.ds(g * GT, GT), :]


def tile_of(buf, t):
    return buf[:, bass.ds(t, 1), :].rearrange("p o d -> p (o d)")


def tile_stats(dve, STATS, X, t):
    return dve.bn_stats(STATS[:, bass.ds(t, 1), :].rearrange("p o s -> p (o s)"), tile_of(X, t))


def normalise_tile(dve, dst, X, MEAN, R, t):
    return dve.tensor_scalar(dst, tile_of(X, t), MEAN[:, bass.ds(t, 1)], R[:, bass.ds(t, 1)], ALU.subtract, ALU.mult)


def normalise_group(dve, dst, X, MEAN, R, g):
    for j in range(GT):
        last = normalise_tile(dve, dst[:, j, :], X, MEAN, R, g * GT + j)
    return last


def group_stats(dve, STATS, X, g, x_done, carried):
    dve.wait_ge(x_done, g + 1)
    dve.sem_inc(carried, 1)
    for j in range(GT):
        tile_stats(dve, STATS, X, g * GT + j)


def layer_norm(nc, name, STATS, MEAN, R, twice=False):
    with ExitStack() as stack:
        sc = Scope(nc, stack, name)
        half = sc.sb("half", [P, T])
        var = sc.sb("var", [P, T])
        var0 = sc.sb("var0", [P, T])
        ln_chain, std_ready = sc.sem("chain"), sc.sem("std_ready")
        links = 6 + 2 * twice
        block = stack.enter_context(nc.Block())

        @block.vector
        def _(dve):
            chain = Chain(dve, ln_chain, 0)
            chain.start(0)
            link = chain.link
            even, odd = STATS[:, :, 1], STATS[:, :, 4]
            dve.tensor_tensor(half[:, :], even, odd, ALU.subtract)
            dve.tensor_tensor(var[:, :], STATS[:, :, 2], STATS[:, :, 5], ALU.add)
            link(dve.tensor_tensor(MEAN[:, :], even, odd, ALU.add))
            link(dve.tensor_scalar(MEAN[:, :], MEAN[:, :], 0.5, None, ALU.mult))
            link(dve.tensor_scalar(half[:, :], half[:, :], 0.5, None, ALU.mult))
            link(dve.tensor_tensor(half[:, :], half[:, :], half[:, :], ALU.mult))
            link(dve.scalar_tensor_tensor(var0[:, :], var[:, :], 1.0 / D, half[:, :], ALU.mult, ALU.add))
            link(dve.tensor_scalar(var[:, :], var0[:, :], LN_EPS, None, ALU.add))
            if twice:
                link(dve.tensor_scalar(var[:, :], var[:, :], LN_EPS, None, ALU.mult))
                link(dve.tensor_tensor(var[:, :], var[:, :], var0[:, :], ALU.add))
            dve.wait_ge(std_ready, 1)
            dve.reciprocal(R[:, :], var[:, :]).then_inc(ln_chain, 1)

        @block.scalar
        def _(act):
            act.wait_ge(ln_chain, links)
            nc.scalar.activation(var[:, :], var[:, :], ACT.Sqrt).then_inc(std_ready, 1)


def dense_gcn(nc, g_in, X, XN, STATS, MEAN, R, ident, banks):
    with ExitStack() as stack:
        sc = Scope(nc, stack, "G")
        adj = sc.sb("adj", [P, T, NODES])
        wt = sc.sb("wt", [P, D])
        bias = sc.sb("bias", [P, D])
        mask = sc.sb("mask", [P, T])
        deg = sc.sb("deg", [P, T])
        dis = sc.sb("dis", [P, T])
        dism = sc.sb("dism", [P, T])
        lnb = [sc.sb(f"lnb{u}", [P, GT, D]) for u in range(2)]
        lnT = [sc.sb(f"lnT{u}", [P, GT, P]) for u in range(2)]
        adjT = [sc.sb(f"adjT{u}", [P, GT, P]) for u in range(2)]
        dh = [sc.sb(f"dh{u}", [P, GT, D]) for u in range(2)]
        agg = [sc.sb(f"agg{u}", [P, GT, D]) for u in range(2)]
        loaded, setup_done, deg_sem = sc.sem("loaded"), sc.sem("setup"), sc.sem("deg")
        zeroed, adjT_in = sc.sem("zeroed"), sc.sems("adjT_in")
        ln_ready, turned, lnT_ready = sc.sem("ln_ready"), sc.sem("turned"), sc.sem("lnT_ready")
        lin_done, dh_ready, agg_done = sc.sem("lin_done"), sc.sem("dh_ready"), sc.sem("agg_done")
        x_done, lin_chain, out_chain = sc.sem("x_done"), sc.sem("lin_chain"), sc.sem("out_chain")
        agg_read, carried = sc.sem("agg_read"), sc.sem("carried")
        pT, pL, pA = banks[0:3]
        block = stack.enter_context(nc.Block())

        @block.sync
        def _(sp):
            sp.dma_start(adj[:, :, :], g_in["adj"].rearrange("(t p) j -> p t j", p=P)).then_inc(loaded, 16)
            sp.dma_start(wt[:, :], g_in["L3_gnn_W"]).then_inc(loaded, 16)
            sp.dma_start(bias[:, :], bcast(g_in["L3_gnn_b"], [P, D])).then_inc(loaded, 16)
            sp.dma_start(mask[:, :], g_in["nodemask"]).then_inc(loaded, 16)
            sp.wait_ge(zeroed, 2)

            def load_adjT(g, u):
                if has(g, 2):
                    sp.wait_ge(agg_done, g - 1)
                for b in range(2):
                    h = slice(b * NODES, (b + 1) * NODES)
                    src = g_in["adjT"][bass.ds(g * GT * P, GT * P), :].rearrange("(t p) j -> p t j", p=P)
                    sp.dma_start(adjT[u][h, :, h], src[h, :, :]).then_inc(adjT_in[u], 16)

            software_pipeline(sp, [load_adjT, None, None, None], NG)

        @block.gpsimd
        def _(pool):
            for u in range(2):
                nc.gpsimd.memset(adjT[u][:, :, :], 0.0).then_inc(zeroed, 1)

        @block.scalar
        def _(act):
            act.wait_ge(deg_sem, 3)
            nc.scalar.activation(deg[:, :], deg[:, :], ACT.Sqrt).then_inc(deg_sem, 1)

            def turn(g, u):
                act.wait_ge(turned, g + 1)
                if has(g, 2):
                    act.wait_ge(lin_done, g - 1)
                nc.scalar.activation(lnT[u][:, :, :], pT[:, :].rearrange("p (t d) -> p t d", t=GT),
                                     ACT.Copy).then_inc(lnT_ready, 1)

            software_pipeline(act, [None, turn, None, None], NG)

        @block.tensor
        def _(pe):
            def turn(g, u):
                pe.wait_ge(ln_ready, g + 1)
                if has(g, 1):
                    pe.wait_ge(lnT_ready, g)
                for j in range(GT):
                    last = nc.tensor.transpose(pT[:, j * P:(j + 1) * P], lnb[u][:, j, :], ident[:, :])
                last.then_inc(turned, 1)

            def linear(g, u):
                pe.wait_ge(lnT_ready, g + 1)
                if has(g, 1):
                    pe.wait_ge(dh_ready, g)
                for j in range(GT):
                    last = nc.tensor.matmul(pL[:, j * D:(j + 1) * D], lnT[u][:, j, :], wt[:, :], start=True, stop=True)
                last.then_inc(lin_done, 1)

            def aggregate(g, u):
                pe.wait_ge(dh_ready, g + 1)
                pe.wait_ge(adjT_in[u], g * 16 + (32 - 16 * u))
                if has(g, 1):
                    pe.wait_ge(agg_read, g)
                for j in range(GT):
                    last = nc.tensor.matmul(pA[:, j * D:(j + 1) * D], adjT[u][:, j, :], dh[u][:, j, :],
                                            start=True, stop=True)
                last.then_inc(agg_done, 1)

            pe.wait_ge(loaded, 64)
            software_pipeline(pe, [None, turn, linear, aggregate], NG)

        @block.vector
        def _(dve):
            dve.wait_ge(loaded, 64)
            dve.tensor_reduce(deg[:, :], adj[:, :, :], AX.X, ALU.add).then_inc(deg_sem, 1)
            dve.wait_ge(deg_sem, 1)
            dve.tensor_scalar(deg[:, :], deg[:, :], 1.0, None, ALU.add).then_inc(deg_sem, 1)
            dve.wait_ge(deg_sem, 2)
            dve.tensor_scalar(deg[:, :], deg[:, :], 1e-8, None, ALU.add).then_inc(deg_sem, 1)
            dve.wait_ge(deg_sem, 4)
            dve.reciprocal(dis[:, :], deg[:, :]).then_inc(setup_done, 1)
            dve.wait_ge(setup_done, 1)
            dve.tensor_tensor(dism[:, :], dis[:, :], mask[:, :], ALU.mult).then_inc(setup_done, 1)
            dve.wait_ge(setup_done, 2)

            def normalise(g, u):
                if has(g, 2):
                    dve.wait_ge(turned, g - 1)
                normalise_group(dve, lnb[u], X, MEAN, R, g).then_inc(ln_ready, 1)

            def scale_linear(g, u):
                dve.wait_ge(lin_done, g + 1)
                if has(g, 2):
                    dve.wait_ge(agg_done, g - 1)
                dve.tensor_tensor(dh[u][:, :, :], pL[:, :].rearrange("p (t d) -> p t d", t=GT),
                                  bcast(bias[:, :].unsqueeze(1), [P, GT, D]), ALU.add).then_inc(lin_chain, 1)
                dve.wait_ge(lin_chain, g + 1)
                dve.tensor_tensor(dh[u][:, :, :], dh[u][:, :, :],
                                  bcast(dis[:, bass.ds(g * GT, GT)].unsqueeze(2), [P, GT, D]),
                                  ALU.mult).then_inc(dh_ready, 1)

            def finish(g, u):
                dve.wait_ge(agg_done, g + 1)
                dve.wait_ge(dh_ready, g + 1)
                dve.tensor_tensor(agg[u][:, :, :], pA[:, :].rearrange("p (t d) -> p t d", t=GT), dh[u][:, :, :],
                                  ALU.add).then_inc(agg_read, 1)
                dve.wait_ge(agg_read, g + 1)
                dve.tensor_tensor(agg[u][:, :, :], agg[u][:, :, :],
                                  bcast(dism[:, bass.ds(g * GT, GT)].unsqueeze(2), [P, GT, D]),
                                  ALU.mult).then_inc(out_chain, 1)
                dve.wait_ge(out_chain, g + 1)
                dve.scalar_tensor_tensor(group(X, g), agg[u][:, :, :], 0.0, group(X, g), ALU.max,
                                         ALU.add).then_inc(x_done, 1)
                group_stats(dve, STATS, X, g, x_done, carried)

            software_pipeline(dve, [normalise, None, scale_linear, finish], NG)


HEADS = 8
HD = D // HEADS
PAIRS = HEADS // 2
VW = HD + 1


def graph_attention(nc, g_in, X, XN, STATS, MEAN, R, ident, banks, out_bias, adj, adj_in):
    with ExitStack() as stack:
        sc = Scope(nc, stack, "A")
        wq, wk, wv, wo = (sc.sb(n, [P, D]) for n in ("wq", "wk", "wv", "wo"))
        head_of = sc.sb("head_of", [P, HEADS])
        lnb = [sc.sb(f"lnb{u}", [P, D]) for u in range(2)]
        lnT = [sc.sb(f"lnT{u}", [P, 2, 2, NODES]) for u in range(4)]
        qk = [sc.sb(f"qk{u}", [P, 2, P]) for u in range(4)]
        k_wide = [sc.sb(f"k_wide{u}", [P, HEADS, P]) for u in range(2)]
        v_wide = [sc.sb(f"v_wide{u}", [P, 2, PAIRS, 2, VW]) for u in range(4)]
        top = [sc.sb(f"top{u}", [P, HEADS]) for u in range(2)]
        s = [sc.sb(f"s{u}", [P, HEADS, NODES]) for u in range(4)]
        pT = [sc.sb(f"pT{u}", [P, PAIRS, P]) for u in range(2)]
        inv = [sc.sb(f"inv{u}", [P, HEADS]) for u in range(2)]
        o = [sc.sb(f"o{u}", [P, D]) for u in range(2)]
        oT = [sc.sb(f"oT{u}", [P, P]) for u in range(2)]
        (loaded, adj_ready, zeroed, v_preset, ln_ready, turned, lnT_ready, qk_done, v_done, qk_ready, k_ready, v_ready,
         scores_done, top_ready, shifted, exp_done, p_ready, p_turned, pT_ready, av_done, inv_ready, o_ready, o_turned,
         oT_ready, proj_done, x_done) = (sc.sem(n) for n in (
             "loaded", "adj_ready", "zeroed", "v_preset", "ln_ready", "turned", "lnT_ready", "qk_done", "v_done",
             "qk_ready", "k_ready", "v_ready", "scores_done", "top_ready", "shifted", "exp_done", "p_ready",
             "p_turned", "pT_ready", "av_done", "inv_ready", "o_ready", "o_turned", "oT_ready", "proj_done", "x_done"))
        carried, biased = sc.sem("carried"), sc.sem("biased")
        bX, bQK, bV, bS, bP, bO, bOT, bY = banks
        block = stack.enter_context(nc.Block())

        @block.sync
        def _(sp):
            for buf, name in ((wq, "L0_gnn_Wq"), (wk, "L0_gnn_Wk"), (wv, "L0_gnn_Wv"), (wo, "L0_gnn_Wo"),
                              (head_of, "c_head_of")):
                sp.dma_start(buf[:, :], g_in[name]).then_inc(loaded, 16)

        @block.tensor
        def _(pe):
            def turn(t, w):
                pe.wait_ge(ln_ready, t + 1)
                if has(t, 1):
                    pe.wait_ge(lnT_ready, t)
                nc.tensor.transpose(bX[:, 0:P], lnb[w % 2][:, :], ident[:, :]).then_inc(turned, 1)

            def project(t, w):
                pe.wait_ge(lnT_ready, t + 1)
                if has(t, 1):
                    pe.wait_ge(qk_ready, t)
                nc.tensor.matmul(bQK[:, 0:P], wq[:, :], lnT[w][:, :, 0, :], start=True, stop=True)
                nc.tensor.matmul(bQK[:, P:2 * P], wk[:, :], lnT[w][:, :, 0, :], start=True, stop=True).then_inc(qk_done, 1)

            def project_v(t, w):
                if has(t, 1):
                    pe.wait_ge(v_ready, t)
                for b in range(2):
                    last = nc.tensor.matmul(bV[:, b * D:(b + 1) * D], lnT[w][:, b, :, :].rearrange("p a k -> p (a k)"),
                                            wv[:, :], start=True, stop=True)
                last.then_inc(v_done, 1)

            def scores(t, w):
                pe.wait_ge(qk_ready, t + 1)
                pe.wait_ge(k_ready, t + 1)
                if has(t, 1):
                    pe.wait_ge(shifted, t)
                for b in range(2):
                    h = slice(b * NODES, (b + 1) * NODES)
                    last = nc.tensor.matmul(bS[h, :], qk[w][:, 0, h], k_wide[w % 2][:, :, h], start=True, stop=True)
                last.then_inc(scores_done, 1)

            def turn_p(t, w):
                pe.wait_ge(p_ready, t + 1)
                if has(t, 1):
                    pe.wait_ge(pT_ready, t)
                for c in range(PAIRS):
                    last = nc.tensor.transpose(bP[:, c * P:(c + 1) * P],
                                               s[w][:, 2 * c:2 * c + 2, :].rearrange("p h k -> p (h k)"), ident[:, :])
                last.then_inc(p_turned, 1)

            def values(t, w):
                pe.wait_ge(pT_ready, t + 1)
                pe.wait_ge(v_ready, t + 1)
                if has(t, 1):
                    pe.wait_ge(o_ready, t)
                for b in range(2):
                    h = slice(b * NODES, (b + 1) * NODES)
                    for c in range(PAIRS):
                        last = nc.tensor.matmul(bO[h, c * 2 * VW:(c + 1) * 2 * VW], pT[w % 2][:, c, h],
                                                v_wide[w][:, b, c, :, :].rearrange("p s d -> p (s d)"),
                                                start=True, stop=True)
                last.then_inc(av_done, 1)

            def turn_o(t, w):
                pe.wait_ge(o_ready, t + 1)
                if has(t, 1):
                    pe.wait_ge(oT_ready, t)
                nc.tensor.transpose(bOT[:, 0:P], o[w % 2][:, :], ident[:, :]).then_inc(o_turned, 1)

            def project_out(t, w):
                pe.wait_ge(oT_ready, t + 1)
                if has(t, 1):
                    pe.wait_ge(x_done, t)
                nc.tensor.matmul(bY[:, 0:D], oT[w % 2][:, :], wo[:, :], start=True, stop=True).then_inc(proj_done, 1)

            pe.wait_ge(loaded, 80)
            software_pipeline(pe, [None, turn, project, None, scores, project_v, None, turn_p, values, turn_o,
                                   project_out], T, 4)

        @block.scalar
        def _(act):
            def turn(t, w):
                act.wait_ge(turned, t + 1)
                if has(t, 4):
                    act.wait_ge(v_done, t - 3)
                src = bX[:, 0:P].rearrange("p (b k) -> p b k", b=2).unsqueeze(2)
                nc.scalar.activation(lnT[w][:, :, :, :], bcast(src, [P, 2, 2, NODES]), ACT.Copy).then_inc(lnT_ready, 1)

            def project(t, w):
                act.wait_ge(qk_done, t + 1)
                if has(t, 4):
                    act.wait_ge(scores_done, t - 3)
                    act.wait_ge(k_ready, t - 3)
                nc.scalar.activation(qk[w][:, :, :], bQK[:, 0:2 * P].rearrange("p (a q) -> p a q", a=2),
                                     ACT.Copy).then_inc(qk_ready, 1)

            def exponentials(t, w):
                act.wait_ge(shifted, t + 1)
                nc.scalar.activation(s[w][:, :, :], s[w][:, :, :], ACT.Exp,
                                     scale=HD ** -0.5).then_inc(exp_done, 1)

            def turn_p(t, w):
                act.wait_ge(p_turned, t + 1)
                if has(t, 2):
                    act.wait_ge(av_done, t - 1)
                nc.scalar.activation(pT[w % 2][:, :, :], bP[:, :].rearrange("p (c q) -> p c q", c=PAIRS),
                                     ACT.Copy).then_inc(pT_ready, 1)

            def turn_o(t, w):
                act.wait_ge(o_turned, t + 1)
                if has(t, 2):
                    act.wait_ge(proj_done, t - 1)
                nc.scalar.activation(oT[w % 2][:, :], bOT[:, 0:P], ACT.Copy).then_inc(oT_ready, 1)

            software_pipeline(act, [None, turn, project, None, None, exponentials, None, turn_p, None, turn_o, None],
                              T, 4)

        @block.gpsimd
        def _(pool):
            for u in range(4):
                nc.gpsimd.memset(v_wide[u][:, :, :, :, :], 0.0).then_inc(zeroed, 1)
            pool.wait_ge(zeroed, 4)
            for u in range(4):
                for s2 in range(2):
                    h = slice(s2 * NODES, (s2 + 1) * NODES)
                    ones = v_wide[u][h, :, :, s2, HD:VW].rearrange("p b c d -> p (b c) d")
                    nc.gpsimd.memset(ones, 1.0).then_inc(v_preset, 1)
            pool.wait_ge(v_preset, 8)
            pool.wait_ge(loaded, 80)
            pool.wait_ge(adj_ready, 1)

            def widen_k(t, w):
                pool.wait_ge(qk_ready, t + 1)
                if has(t, 2):
                    pool.wait_ge(scores_done, t - 1)
                nc.gpsimd.tensor_tensor(k_wide[w % 2][:, :, :], bcast(qk[w][:, 1:2, :], [P, HEADS, P]),
                                        bcast(head_of[:, :].unsqueeze(2), [P, HEADS, P]), ALU.mult).then_inc(k_ready, 1)

            def weigh(t, w):
                pool.wait_ge(exp_done, t + 1)
                nc.gpsimd.tensor_tensor(s[w][:, :, :], s[w][:, :, :],
                                        bcast(adj[:, bass.ds(t, 1), :], [P, HEADS, NODES]), ALU.mult).then_inc(p_ready, 1)

            def add_bias(t, w):
                pool.wait_ge(ln_ready, t + 1)
                nc.gpsimd.tensor_tensor(tile_of(X, t), tile_of(X, t), out_bias[:, :], ALU.add).then_inc(biased, 1)

            software_pipeline(pool, [None, add_bias, None, widen_k, None, None, weigh, None, None, None, None], T, 4)

        @block.vector
        def _(dve):
            dve.wait_ge(v_preset, 8)
            dve.wait_ge(adj_in, 16)
            dve.tensor_scalar(adj[:, :, :], adj[:, :, :], 1e-6, None, ALU.add).then_inc(adj_ready, 1)

            def normalise(t, w):
                if has(t, 2):
                    dve.wait_ge(turned, t - 1)
                normalise_tile(dve, lnb[w % 2][:, :], X, MEAN, R, t).then_inc(ln_ready, 1)

            def widen_v(t, w):
                dve.wait_ge(v_done, t + 1)
                if has(t, 4):
                    dve.wait_ge(av_done, t - 3)
                for s2 in range(2):
                    h = slice(s2 * NODES, (s2 + 1) * NODES)
                    src = bV[h, 0:2 * D].rearrange("p (c s d) -> p c s d", s=2, d=HD)[:, :, s2, :]
                    last = dve.tensor_copy(v_wide[w][h, :, :, s2, 0:HD].rearrange("p b c d -> p (b c) d"), src)
                last.then_inc(v_ready, 1)

            def shift(t, w):
                dve.wait_ge(scores_done, t + 1)
                src = bS[:, :].rearrange("p (h k) -> p h k", h=HEADS)
                dve.tensor_reduce(top[w % 2][:, :], src, AX.X, ALU.max).then_inc(top_ready, 1)
                dve.wait_ge(top_ready, t + 1)
                if has(t, 4):
                    dve.wait_ge(p_turned, t - 3)
                dve.tensor_tensor(s[w][:, :, :], src, bcast(top[w % 2][:, :].unsqueeze(2), [P, HEADS, NODES]),
                                  ALU.subtract).then_inc(shifted, 1)

            def divide(t, w):
                dve.wait_ge(av_done, t + 1)
                src = bO[:, 0:HEADS * VW].rearrange("p (h d) -> p h d", h=HEADS)
                dve.reciprocal(inv[w % 2][:, :].unsqueeze(2), src[:, :, HD:VW]).then_inc(inv_ready, 1)
                dve.wait_ge(inv_ready, t + 1)
                if has(t, 2):
                    dve.wait_ge(o_turned, t - 1)
                dve.tensor_tensor(o[w % 2][:, :].rearrange("p (h d) -> p h d", h=HEADS), src[:, :, 0:HD],
                                  bcast(inv[w % 2][:, :].unsqueeze(2), [P, HEADS, HD]), ALU.mult).then_inc(o_ready, 1)

            def add(t, w):
                dve.wait_ge(proj_done, t + 1)
                dve.wait_ge(biased, t + 1)
                dve.tensor_tensor(tile_of(X, t), bY[:, 0:D], tile_of(X, t), ALU.add).then_inc(x_done, 1)
                dve.wait_ge(x_done, t + 1)
                dve.sem_inc(carried, 1)
                tile_stats(dve, STATS, X, t)

            software_pipeline(dve, [normalise, None, None, None, shift, widen_v, None, None, divide, None, add], T, 4)


GROUPS = [list(range(25)), [0, 1, 2, 3, 4, 5, 6, 7, 8], [0, 9, 10, 11, 12, 13, 14], [6, 7, 8, 12, 13, 14],
          [3, 4, 5, 9, 10, 11]]
SLOT0 = [sum(len(n) for n in GROUPS[:g]) for g in range(len(GROUPS))]
SLOTS = sum(len(n) for n in GROUPS)
MID = 256


def group_gcns(nc, g_in, X, XN, STATS, MEAN, R, ident, banks):
    with ExitStack() as stack:
        sc = Scope(nc, stack, "C")
        NGR = len(GROUPS)
        adj = sc.sb("adj", [P, T, NODES])
        w1 = sc.sb("w1", [P, NGR, MID])
        w2 = sc.sb("w2", [P, NGR, 2, D])
        b1 = sc.sb("b1", [P, NGR, 2])
        b2 = sc.sb("b2", [P, D])
        fusion = sc.sb("fusion", [P, NGR])
        slot_group = sc.sb("slot_group", [P, NGR])
        fmax, fsum, finv, slot_w = (sc.sb(n, [P, 1]) for n in ("fmax", "fsum", "finv", "slot_w"))
        pick = sc.sb("pick", [P, P])
        spread = sc.sb("spread", [P, P])
        deg, zero, dinv = (sc.sb(n, [P, T]) for n in ("deg", "zero", "dinv"))
        ring = lambda name, shape: [sc.sb(f"{name}{u}", shape) for u in range(2)]
        lnb, xs, z, ys, f = (ring(n, [P, GT, D]) for n in ("lnb", "xs", "z", "ys", "f"))
        adj1, adj2 = ring("adj1", [P, GT, P]), ring("adj2", [P, GT, P])
        zT, sT = ring("zT", [P, 2 * GT, NODES]), ring("sT", [P, 2 * GT, NODES])
        hT = ring("hT", [P, 2, 2 * GT, NODES])
        (loaded, zeroed, chain_sem, exp_done, sqrt_done, ln_ready, picked, xs_ready, conv1_done, z_sum, z_scaled, z_turned,
         zT_ready, up_done, hT_ready, down_done, sT_ready, s_turned, ys_ready, conv2_done, bank7_read, spread_done,
         x_done, f_chain, f_ready) = (sc.sem(n) for n in (
             "loaded", "zeroed", "chain", "exp_done", "sqrt_done", "ln_ready", "picked", "xs_ready", "conv1_done",
             "z_sum", "z_scaled", "z_turned", "zT_ready", "up_done", "hT_ready", "down_done", "sT_ready", "s_turned",
             "ys_ready", "conv2_done", "bank7_read", "spread_done", "x_done", "f_chain", "f_ready"))
        adj1_in, adj2_in = sc.sems("adj1_in"), sc.sems("adj2_in")
        carried = sc.sem("carried")
        bPick, bA1, bZT, bH0, bH1, bS, bST, bA2 = banks
        bSpread = bPick
        LAST = 8
        cols = lambda bank: bank[:, :].rearrange("p (a s) -> p a s", s=NODES)
        tiles = lambda bank: bank[:, :].rearrange("p (t d) -> p t d", t=GT)
        block = stack.enter_context(nc.Block())

        @block.sync
        def _(sp):
            for buf, src in ((adj[:, :, :], g_in["slot_adj"].rearrange("(t p) j -> p t j", p=P)),
                             (w1[:, :, :], g_in["L1_gnn_W1"].rearrange("g d f -> d g f")),
                             (w2[:, :, :, :], g_in["L1_gnn_W2"].rearrange("g (c f) d -> f g c d", f=P)),
                             (b1[:, :, :], g_in["L1_gnn_b1"]), (b2[:, :], g_in["L1_gnn_b2"]),
                             (fusion[:, :], bcast(g_in["L1_gnn_fusion_w"], [P, NGR])),
                             (slot_group[:, :], g_in["c_slot_group"]),
                             (pick[:, :], g_in["c_pick"]), (spread[:, :], g_in["c_spread"])):
                sp.dma_start(buf, src).then_inc(loaded, 16)
            sp.wait_ge(zeroed, 6)

            def load(dst, arrived, readers):
                def run(g, u):
                    if has(g, 2):
                        sp.wait_ge(readers, g - 1)
                    src = g_in["slot_adjT"][bass.ds(g * GT * P, GT * P), :].rearrange("(t p) j -> p t j", p=P)
                    for b in range(2):
                        h = slice(b * NODES, (b + 1) * NODES)
                        sp.dma_start(dst[u][h, :, h], src[h, :, :]).then_inc(arrived[u], 16)
                return run

            software_pipeline(sp, [None, load(adj1, adj1_in, conv1_done), None, None, None, None,
                                   load(adj2, adj2_in, conv2_done), None, None], NG)

        @block.gpsimd
        def _(pool):
            for buf in adj1 + adj2 + sT:
                nc.gpsimd.memset(buf[:, :, :], 0.0).then_inc(zeroed, 1)

        @block.tensor
        def _(pe):
            def pick_slots(g, u):
                pe.wait_ge(ln_ready, g + 1)
                if has(g, 1):
                    pe.wait_ge(xs_ready, g)
                if has(g, LAST - 1):
                    pe.wait_ge(x_done, g - (LAST - 2))
                nc.tensor.matmul(bPick[:, :], pick[:, :], lnb[u][:, :, :].rearrange("p t d -> p (t d)"),
                                 start=True, stop=True).then_inc(picked, 1)

            def conv1(g, u):
                pe.wait_ge(xs_ready, g + 1)
                pe.wait_ge(adj1_in[u], g * 16 + (32 - 16 * u))
                if has(g, 1):
                    pe.wait_ge(z_sum, g)
                for j in range(GT):
                    last = nc.tensor.matmul(bA1[:, j * D:(j + 1) * D], adj1[u][:, j, :], xs[u][:, j, :],
                                            start=True, stop=True)
                last.then_inc(conv1_done, 1)

            def turn_z(g, u):
                pe.wait_ge(z_scaled, g + 1)
                if has(g, 1):
                    pe.wait_ge(zT_ready, g)
                for j in range(GT):
                    last = nc.tensor.transpose(bZT[:, j * P:(j + 1) * P], z[u][:, j, :], ident[:, :])
                last.then_inc(z_turned, 1)

            def up(g, u):
                pe.wait_ge(zT_ready, g + 1)
                if has(g, 1):
                    pe.wait_ge(hT_ready, g)
                for c, bank in enumerate((bH0, bH1)):
                    for i, nodes in enumerate(GROUPS):
                        sl = slice(SLOT0[i], SLOT0[i] + len(nodes))
                        last = nc.tensor.matmul(cols(bank)[:, :, sl], w1[:, i, c * P:(c + 1) * P], zT[u][:, :, sl],
                                                start=True, stop=True)
                last.then_inc(up_done, 1)

            def down(g, u):
                pe.wait_ge(hT_ready, g + 1)
                if has(g, 1):
                    pe.wait_ge(sT_ready, g)
                for i, nodes in enumerate(GROUPS):
                    sl = slice(SLOT0[i], SLOT0[i] + len(nodes))
                    for c in range(2):
                        last = nc.tensor.matmul(cols(bS)[:, :, sl], w2[:, i, c, :], hT[u][:, c, :, sl],
                                                start=(c == 0), stop=(c == 1))
                last.then_inc(down_done, 1)

            def turn_s(g, u):
                pe.wait_ge(sT_ready, g + 1)
                if has(g, 1):
                    pe.wait_ge(ys_ready, g)
                for j in range(GT):
                    last = nc.tensor.transpose(bST[:, j * P:(j + 1) * P],
                                               sT[u][:, 2 * j:2 * j + 2, :].rearrange("p b s -> p (b s)"), ident[:, :])
                last.then_inc(s_turned, 1)

            def conv2(g, u):
                pe.wait_ge(ys_ready, g + 1)
                pe.wait_ge(adj2_in[u], g * 16 + (32 - 16 * u))
                if has(g, 1):
                    pe.wait_ge(bank7_read, g)
                for j in range(GT):
                    last = nc.tensor.matmul(bA2[:, j * D:(j + 1) * D], adj2[u][:, j, :], ys[u][:, j, :],
                                            start=True, stop=True)
                last.then_inc(conv2_done, 1)

            def spread_slots(g, u):
                pe.wait_ge(f_ready, g + 1)
                n = g + (LAST - 1)
                pe.wait_ge(xs_ready, min(n, NG) if isinstance(n, int) else n)
                if has(g, 1):
                    pe.wait_ge(x_done, g)
                nc.tensor.matmul(bSpread[:, :], spread[:, :], f[u][:, :, :].rearrange("p t d -> p (t d)"),
                                 start=True, stop=True).then_inc(spread_done, 1)

            pe.wait_ge(loaded, 144)
            software_pipeline(pe, [None, pick_slots, conv1, turn_z, up, down, turn_s, conv2, spread_slots], NG)

        @block.scalar
        def _(act):
            act.wait_ge(chain_sem, 2)
            nc.scalar.activation(fusion[:, :], fusion[:, :], ACT.Exp).then_inc(exp_done, 1)
            act.wait_ge(chain_sem, 12)
            nc.scalar.activation(deg[:, :], deg[:, :], ACT.Sqrt).then_inc(sqrt_done, 1)

            def turn_z(g, u):
                act.wait_ge(z_turned, g + 1)
                if has(g, 2):
                    act.wait_ge(up_done, g - 1)
                nc.scalar.activation(zT[u][:, :, :], cols(bZT), ACT.Copy).then_inc(zT_ready, 1)

            def up(g, u):
                act.wait_ge(up_done, g + 1)
                if has(g, 2):
                    act.wait_ge(down_done, g - 1)
                for c, bank in enumerate((bH0, bH1)):
                    for i, nodes in enumerate(GROUPS):
                        sl = slice(SLOT0[i], SLOT0[i] + len(nodes))
                        last = nc.scalar.activation(hT[u][:, c, :, sl], cols(bank)[:, :, sl], ACT.Relu,
                                                    bias=b1[:, i, c:c + 1])
                last.then_inc(hT_ready, 1)

            def down(g, u):
                act.wait_ge(down_done, g + 1)
                if has(g, 2):
                    act.wait_ge(s_turned, g - 1)
                nc.scalar.activation(sT[u][:, :, 0:SLOTS], cols(bS)[:, :, 0:SLOTS], ACT.Copy).then_inc(sT_ready, 1)

            software_pipeline(act, [None, None, None, turn_z, up, down, None, None, None], NG)

        @block.vector
        def _(dve):
            chain = Chain(dve, chain_sem, 0)
            chain.start(0)
            link = chain.link
            dve.wait_ge(loaded, 144)
            link(dve.tensor_reduce(fmax[:, :], fusion[:, :], AX.X, ALU.max))
            link(dve.tensor_scalar(fusion[:, :], fusion[:, :], fmax[:, :], None, ALU.subtract))
            dve.wait_ge(exp_done, 1)
            link(dve.tensor_reduce(fsum[:, :], fusion[:, :], AX.X, ALU.add))
            link(dve.reciprocal(finv[:, :], fsum[:, :]))
            link(dve.tensor_tensor(fusion[:, :], fusion[:, :], slot_group[:, :], ALU.mult))
            link(dve.tensor_reduce(slot_w[:, :], fusion[:, :], AX.X, ALU.add))
            link(dve.tensor_tensor(slot_w[:, :], slot_w[:, :], finv[:, :], ALU.mult))
            link(dve.tensor_reduce(deg[:, :], adj[:, :, :], AX.X, ALU.add))
            link(dve.tensor_scalar(deg[:, :], deg[:, :], 1.0, None, ALU.add))
            link(dve.tensor_scalar(zero[:, :], deg[:, :], 0.0, None, ALU.is_equal))
            link(dve.tensor_tensor(deg[:, :], deg[:, :], zero[:, :], ALU.add))
            link(dve.tensor_scalar(zero[:, :], zero[:, :], -1.0, 1.0, ALU.mult, ALU.add))
            dve.wait_ge(sqrt_done, 1)
            link(dve.reciprocal(dinv[:, :], deg[:, :]))
            link(dve.tensor_tensor(dinv[:, :], dinv[:, :], zero[:, :], ALU.mult))

            def dinv_of(g):
                return bcast(dinv[:, bass.ds(g * GT, GT)].unsqueeze(2), [P, GT, D])

            def normalise(g, u):
                if has(g, 2):
                    dve.wait_ge(picked, g - 1)
                normalise_group(dve, lnb[u], X, MEAN, R, g).then_inc(ln_ready, 1)

            def pick_slots(g, u):
                dve.wait_ge(picked, g + 1)
                if has(g, 2):
                    dve.wait_ge(conv1_done, g - 1)
                    dve.wait_ge(z_sum, g - 1)
                dve.tensor_tensor(xs[u][:, :, :], tiles(bPick), dinv_of(g), ALU.mult).then_inc(xs_ready, 1)

            def conv1(g, u):
                dve.wait_ge(conv1_done, g + 1)
                if has(g, 2):
                    dve.wait_ge(z_turned, g - 1)
                dve.tensor_tensor(z[u][:, :, :], tiles(bA1), xs[u][:, :, :], ALU.add).then_inc(z_sum, 1)
                dve.wait_ge(z_sum, g + 1)
                dve.tensor_tensor(z[u][:, :, :], z[u][:, :, :], dinv_of(g), ALU.mult).then_inc(z_scaled, 1)

            def turn_s(g, u):
                dve.wait_ge(s_turned, g + 1)
                if has(g, 2):
                    dve.wait_ge(conv2_done, g - 1)
                dve.tensor_tensor(ys[u][:, :, :], tiles(bST), dinv_of(g), ALU.mult).then_inc(ys_ready, 1)

            def conv2(g, u):
                dve.wait_ge(conv2_done, g + 1)
                if has(g, 2):
                    dve.wait_ge(spread_done, g - 1)
                dve.tensor_tensor(f[u][:, :, :], tiles(bA2), ys[u][:, :, :], ALU.add).then_inc(bank7_read, 1)
                dve.wait_ge(bank7_read, g + 1)
                dve.tensor_tensor(f[u][:, :, :], f[u][:, :, :], dinv_of(g), ALU.mult).then_inc(f_chain, 1)
                dve.wait_ge(f_chain, g * 2 + 1)
                dve.tensor_tensor(f[u][:, :, :], f[u][:, :, :], bcast(b2[:, :].unsqueeze(1), [P, GT, D]),
                                  ALU.add).then_inc(f_chain, 1)
                dve.wait_ge(f_chain, g * 2 + 2)
                dve.tensor_scalar(f[u][:, :, :], f[u][:, :, :], 0.0, slot_w[:, :], ALU.max, ALU.mult).then_inc(f_ready, 1)

            def add(g, u):
                dve.wait_ge(spread_done, g + 1)
                dve.tensor_tensor(group(X, g), tiles(bSpread), group(X, g), ALU.add).then_inc(x_done, 1)
                group_stats(dve, STATS, X, g, x_done, carried)

            software_pipeline(dve, [normalise, pick_slots, conv1, None, None, None, turn_s, conv2, add], NG)


ROUTES = 16
LAYERS = 2
D_WAYS = 4
FIRST, SECOND = 3, 5
D_TURNS = (T + 7 - 1) // D_WAYS + 1


def routed_mlp(nc, g_in, X, XN, STATS, MEAN, R, ident, banks, out_bias):
    with ExitStack() as stack:
        sc = Scope(nc, stack, "D")
        w = sc.sb("w", [P, LAYERS, ROUTES, 2, MID])
        ws = sc.sb("ws", [P, LAYERS, 2, MID])
        eye2 = sc.sb("eye2", [P, 2, MID])
        br = sc.sb("br", [P, LAYERS, ROUTES, MID])
        bs = sc.sb("bs", [P, LAYERS, MID])
        wi = sc.sb("wi", [P, MID])
        bi = sc.sb("bi", [P, 2])
        wo = sc.sb("wo", [P, 2, D])
        route = sc.sb("route", [1, T], I32)
        route_f = sc.sb("route_f", [1, SECOND + D_WAYS * D_TURNS])
        digits = sc.sb("digits", [1, D_WAYS])
        words = sc.sb("words", [1, 2, D_TURNS, D_WAYS])
        word_sum = sc.sb("word_sum", [1, 2, D_TURNS])
        packed = sc.sb("packed", [1, 2, D_TURNS], I32)
        ring = lambda name, shape: [sc.sb(f"{name}{u}", shape) for u in range(2)]
        lnb, lnT = ring("lnb", [P, D]), ring("lnT", [P, P])
        h0T, h1T, h2T = (ring(n, [P, 2, P]) for n in ("h0T", "h1T", "h2T"))
        h1, h2 = ring("h1", [P, MID]), ring("h2", [P, MID])
        (loaded, chain_sem, words_ready, weights_ready, ln_ready, turned, lnT_ready, in_done, h0_ready, mm1_done,
         h1_ready, turned1, h1T_ready, mm2_done, h2_ready, turned2, h2T_ready, out_done, x_done) = (
             sc.sem(n) for n in (
                 "loaded", "chain", "words_ready", "weights_ready", "ln_ready", "turned", "lnT_ready", "in_done",
                 "h0_ready", "mm1_done", "h1_ready", "turned1", "h1T_ready", "mm2_done", "h2_ready", "turned2",
                 "h2T_ready", "out_done", "x_done"))
        carried, biased = sc.sem("carried"), sc.sem("biased")
        bX, b0, b1, bT1, b2, bT2, bY = banks[0:7]
        block = stack.enter_context(nc.Block())

        @block.sync
        def _(sp):
            for buf, src in ((route[:, :], g_in["L1_ffn_route_id"]), (digits[:, :], g_in["c_hex_digits"]),
                             (w[:, :, :, :, :], g_in["L1_ffn_Wr"]), (ws[:, :, :, :], g_in["L1_ffn_Ws"]),
                             (eye2[:, :, :], g_in["c_eye2"]),
                             (br[:, :, :, :].rearrange("p l e f -> p (l e f)"),
                              bcast(g_in["L1_ffn_br"], [P, LAYERS * ROUTES * MID])),
                             (bs[:, :, :].rearrange("p l f -> p (l f)"), bcast(g_in["L1_ffn_bs"], [P, LAYERS * MID])),
                             (wi[:, :], g_in["L1_ffn_Wi"]), (bi[:, :], g_in["L1_ffn_bi"]), (wo[:, :, :], g_in["L1_ffn_Wo"])):
                sp.dma_start(buf, src).then_inc(loaded, 16)

        weights_sem = sc.sems("shared_ready")

        def combine_weights(eng, layer):
            shared = ws[:, layer, :, :]
            eng.tensor_tensor(shared, shared, eye2[:, :, :], ALU.add).then_inc(weights_sem[layer], 1)
            eng.wait_ge(weights_sem[layer], 1)
            ww = w[:, layer, :, :, :].rearrange("p e c f -> p e (c f)")
            eng.tensor_tensor(ww, ww, bcast(shared.rearrange("p c f -> p (c f)").unsqueeze(1), [P, ROUTES, 2 * MID]),
                              ALU.add).then_inc(weights_ready, 1)
            bb = br[:, layer, :, :]
            eng.tensor_tensor(bb, bb, bcast(bs[:, layer:layer + 1, :], [P, ROUTES, MID]), ALU.add).then_inc(weights_ready, 1)

        @block.gpsimd
        def _(pool):
            pool.wait_ge(loaded, 160)
            combine_weights(pool, 1)

            def add_bias(t, k):
                pool.wait_ge(ln_ready, t + 1)
                nc.gpsimd.tensor_tensor(tile_of(X, t), tile_of(X, t), out_bias[:, :], ALU.add).then_inc(biased, 1)

            software_pipeline(pool, [None, add_bias] + [None] * 6, T, D_WAYS)

        class Routes:

            def __init__(self, eng):
                self.eng = eng

            def turn(self, j):
                self.words = [self.eng.value_load(packed[:, i, bass.ds(j, 1)], min_val=0, max_val=ROUTES ** D_WAYS - 1)
                              for i in range(2)]

            def of(self, slot, phase):
                return (self.words[phase == SECOND] >> (4 * ((slot + phase) % D_WAYS))) & (ROUTES - 1)

        @block.tensor
        def _(pe):
            routes = Routes(pe)

            def turn(t, k):
                pe.wait_ge(ln_ready, t + 1)
                if has(t, 1):
                    pe.wait_ge(lnT_ready, t)
                nc.tensor.transpose(bX[:, 0:P], lnb[k % 2][:, :], ident[:, :]).then_inc(turned, 1)

            def project_in(t, k):
                pe.wait_ge(lnT_ready, t + 1)
                if has(t, 1):
                    pe.wait_ge(h0_ready, t)
                for c in range(2):
                    last = nc.tensor.matmul(b0[:, c * P:(c + 1) * P], wi[:, c * P:(c + 1) * P], lnT[k % 2][:, :],
                                            start=True, stop=True)
                last.then_inc(in_done, 1)

            def layer(n, phase, bank, src, src_ready, bank_read, done):
                def run(t, k):
                    e = routes.of(k, phase)
                    pe.wait_ge(src_ready, t + 1)
                    if has(t, 1):
                        pe.wait_ge(bank_read, t)
                    for c in range(2):
                        last = nc.tensor.matmul(bank[:, 0:MID], src[k % 2][:, c, :],
                                                w[:, n, bass.ds(e, 1), c, :].rearrange("p o f -> p (o f)"),
                                                start=(c == 0), stop=(c == 1))
                    last.then_inc(done, 1)
                return run

            def turn_h(bank, src, src_ready, bank_read, done):
                def run(t, k):
                    pe.wait_ge(src_ready, t + 1)
                    if has(t, 1):
                        pe.wait_ge(bank_read, t)
                    for c in range(2):
                        last = nc.tensor.transpose(bank[:, c * P:(c + 1) * P], src[k % 2][:, c * P:(c + 1) * P], ident[:, :])
                    last.then_inc(done, 1)
                return run

            def project_out(t, k):
                pe.wait_ge(h2T_ready, t + 1)
                if has(t, 1):
                    pe.wait_ge(x_done, t)
                for c in range(2):
                    last = nc.tensor.matmul(bY[:, 0:D], h2T[k % 2][:, c, :], wo[:, c, :], start=(c == 0), stop=(c == 1))
                last.then_inc(out_done, 1)

            pe.wait_ge(loaded, 160)
            pe.wait_ge(words_ready, 1)
            pe.wait_ge(weights_ready, 4)
            software_pipeline(pe, [None, turn, project_in, layer(0, FIRST, b1, h0T, h0_ready, h1_ready, mm1_done),
                                   turn_h(bT1, h1, h1_ready, h1T_ready, turned1),
                                   layer(1, SECOND, b2, h1T, h1T_ready, h2_ready, mm2_done),
                                   turn_h(bT2, h2, h2_ready, h2T_ready, turned2), project_out],
                              T, D_WAYS, routes.turn)

        @block.scalar
        def _(act):
            act.wait_ge(loaded, 160)

            def turn(t, k):
                act.wait_ge(turned, t + 1)
                if has(t, 2):
                    act.wait_ge(in_done, t - 1)
                nc.scalar.activation(lnT[k % 2][:, :], bX[:, 0:P], ACT.Copy).then_inc(lnT_ready, 1)

            def project_in(t, k):
                act.wait_ge(in_done, t + 1)
                if has(t, 2):
                    act.wait_ge(mm1_done, t - 1)
                for c in range(2):
                    last = nc.scalar.activation(h0T[k % 2][:, c, :], b0[:, c * P:(c + 1) * P], ACT.Relu, bias=bi[:, c:c + 1])
                last.then_inc(h0_ready, 1)

            def turn_h(bank, dst, done, readers, ready):
                def run(t, k):
                    act.wait_ge(done, t + 1)
                    if has(t, 2):
                        act.wait_ge(readers, t - 1)
                    nc.scalar.activation(dst[k % 2][:, :, :], bank[:, 0:2 * P].rearrange("p (c q) -> p c q", c=2),
                                         ACT.Relu).then_inc(ready, 1)
                return run

            software_pipeline(act, [None, turn, project_in, None, turn_h(bT1, h1T, turned1, mm2_done, h1T_ready), None,
                                    turn_h(bT2, h2T, turned2, out_done, h2T_ready), None], T, D_WAYS)

        @block.vector
        def _(dve):
            chain = Chain(dve, chain_sem, 0)
            chain.start(0)
            link = chain.link
            routes = Routes(dve)
            dve.wait_ge(loaded, 160)
            link(dve.memset(route_f[:, :], 0.0))
            link(dve.tensor_copy(route_f[:, SECOND:SECOND + T], route[:, :]))
            for i, first in enumerate((SECOND - FIRST, 0)):
                part = route_f[:, first:first + D_WAYS * D_TURNS].rearrange("p (j k) -> p j k", k=D_WAYS)
                link(dve.tensor_tensor(words[:, i, :, :], part, bcast(digits[:, :].unsqueeze(1), [1, D_TURNS, D_WAYS]),
                                       ALU.mult))
            link(dve.tensor_reduce(word_sum[:, :, :], words[:, :, :, :], AX.X, ALU.add))
            dve.tensor_copy(packed[:, :, :], word_sum[:, :, :]).then_inc(words_ready, 1)
            dve.wait_ge(words_ready, 1)
            combine_weights(dve, 0)
            dve.wait_ge(weights_ready, 4)

            def normalise(t, k):
                if has(t, 2):
                    dve.wait_ge(turned, t - 1)
                normalise_tile(dve, lnb[k % 2][:, :], X, MEAN, R, t).then_inc(ln_ready, 1)

            def layer(n, phase, bank, dst, done, readers, ready):
                def run(t, k):
                    e = routes.of(k, phase)
                    dve.wait_ge(done, t + 1)
                    if has(t, 2):
                        dve.wait_ge(readers, t - 1)
                    dve.tensor_tensor(dst[k % 2][:, :], bank[:, 0:MID],
                                      br[:, n, bass.ds(e, 1), :].rearrange("p o f -> p (o f)"), ALU.add).then_inc(ready, 1)
                return run

            def add(t, k):
                dve.wait_ge(out_done, t + 1)
                dve.wait_ge(biased, t + 1)
                dve.tensor_tensor(tile_of(X, t), bY[:, 0:D], tile_of(X, t), ALU.add).then_inc(x_done, 1)
                dve.wait_ge(x_done, t + 1)
                dve.sem_inc(carried, 1)
                tile_stats(dve, STATS, X, t)

            software_pipeline(dve, [normalise, None, None, layer(0, FIRST, b1, h1, mm1_done, turned1, h1_ready), None,
                                    layer(1, SECOND, b2, h2, mm2_done, turned2, h2_ready), None, add],
                              T, D_WAYS, routes.turn)


def edge_attention(nc, g_in, X, XN, STATS, MEAN, R, ident, banks):
    with ExitStack() as stack:
        sc = Scope(nc, stack, "E")
        SLOPE, FAR = 0.2, 9e15
        adj = sc.sb("adj", [P, T, NODES])
        w1, w2 = sc.sb("w1", [P, D]), sc.sb("w2", [P, D])
        w3 = sc.sb("w3", [P, 2])
        v1, v2 = sc.sb("v1", [P, P]), sc.sb("v2", [P, P])
        deg, some, rdeg = (sc.sb(n, [P, T]) for n in ("deg", "some", "rdeg"))
        ring = lambda name, shape: [sc.sb(f"{name}{u}", shape) for u in range(2)]
        lnb, lnT, pD, pT = (ring(n, [P, GT, P]) for n in ("lnb", "lnT", "pD", "pT"))
        s1, s2j, e, mask, a = (ring(n, [P, GT, NODES]) for n in ("s1", "s2j", "e", "mask", "a"))
        s2, top, inv = (ring(n, [P, GT]) for n in ("s2", "top", "inv"))
        (loaded, zeroed, v_done, chain_sem, setup, ln_ready, kept, turned, lnT_ready, sums_done, s1_ready, s2_read,
         pre_ready, alpha_ready, e_chain, a_chain, mask_ready, shifted, exp_done, inv_ready, pD_ready, p_turned,
         pT_ready, edge_done, x_done) = (sc.sem(n) for n in (
             "loaded", "zeroed", "v_done", "chain", "setup", "ln_ready", "kept", "turned", "lnT_ready", "sums_done",
             "s1_ready", "s2_read", "pre_ready", "alpha_ready", "e_chain", "a_chain", "mask_ready", "shifted",
             "exp_done", "inv_ready", "pD_ready", "p_turned", "pT_ready", "edge_done", "x_done"))
        begun, carried = sc.sem("begun"), sc.sem("carried")
        bX, b1, b2, bP, bY = banks[0:5]
        halves = [slice(0, NODES), slice(NODES, P)]
        tiles = lambda bank: bank[:, :].rearrange("p (t d) -> p t d", t=GT)
        block = stack.enter_context(nc.Block())

        @block.sync
        def _(sp):
            sp.dma_start(adj[:, :, :], g_in["adj"].rearrange("(t p) j -> p t j", p=P)).then_inc(loaded, 16)
            for buf, name in ((w1, "L2_gnn_W1"), (w2, "L2_gnn_W2"), (w3, "L2_gnn_w3")):
                sp.dma_start(buf[:, :], g_in[name]).then_inc(loaded, 16)

        @block.tensor
        def _(pe):
            pe.wait_ge(loaded, 64)
            nc.tensor.matmul(b1[:, 0:1], w1[:, :], w3[:, 0:1], start=True, stop=True)
            nc.tensor.matmul(b1[:, 1:2], w2[:, :], w3[:, 1:2], start=True, stop=True).then_inc(v_done, 1)

            def turn(g, u):
                pe.wait_ge(ln_ready, g + 1)
                if has(g, 1):
                    pe.wait_ge(lnT_ready, g)
                for j in range(GT):
                    last = nc.tensor.transpose(bX[:, j * P:(j + 1) * P], lnb[u][:, j, :], ident[:, :])
                last.then_inc(turned, 1)

            def sums(g, u):
                pe.wait_ge(lnT_ready, g + 1)
                if has(g, 1):
                    pe.wait_ge(s1_ready, g)
                    pe.wait_ge(s2_read, g)
                rhs = lnT[u][:, :, :].rearrange("p t q -> p (t q)")
                nc.tensor.matmul(b1[:, :], v1[:, :], rhs, start=True, stop=True)
                nc.tensor.matmul(b2[:, :], v2[:, :], rhs, start=True, stop=True).then_inc(sums_done, 1)

            def turn_p(g, u):
                pe.wait_ge(pD_ready, g + 1)
                if has(g, 1):
                    pe.wait_ge(pT_ready, g)
                for j in range(GT):
                    last = nc.tensor.transpose(bP[:, j * P:(j + 1) * P], pD[u][:, j, :], ident[:, :])
                last.then_inc(p_turned, 1)

            def edges(g, u):
                pe.wait_ge(pT_ready, g + 1)
                pe.wait_ge(kept, g + 1)
                if has(g, 1):
                    pe.wait_ge(x_done, g)
                for j in range(GT):
                    last = nc.tensor.matmul(bY[:, j * D:(j + 1) * D], pT[u][:, j, :],
                                            XN[:, bass.ds(g * GT + j, 1), :].rearrange("p o d -> p (o d)"),
                                            start=True, stop=True)
                last.then_inc(edge_done, 1)

            pe.wait_ge(setup, 1)
            software_pipeline(pe, [None, turn, sums, None, turn_p, edges], NG)

        @block.scalar
        def _(act):
            def turn(g, u):
                act.wait_ge(ln_ready, g + 1)
                nc.scalar.activation(group(XN, g), lnb[u][:, :, :], ACT.Copy).then_inc(kept, 1)
                act.wait_ge(turned, g + 1)
                if has(g, 2):
                    act.wait_ge(sums_done, g - 1)
                nc.scalar.activation(lnT[u][:, :, :], tiles(bX), ACT.Copy).then_inc(lnT_ready, 1)

            def sums(g, u):
                act.wait_ge(sums_done, g + 1)
                if has(g, 2):
                    act.wait_ge(e_chain, (g - 1) * 5)
                for b, h in enumerate(halves):
                    last = nc.scalar.activation(s1[u][h, :, :], tiles(b1)[h, :, h], ACT.Copy)
                last.then_inc(s1_ready, 1)

            def alpha(g, u):
                act.wait_ge(pre_ready, g + 1)
                nc.scalar.activation(e[u][:, :, :], e[u][:, :, :], ACT.Exp).then_inc(alpha_ready, 1)

            def second(g, u):
                act.wait_ge(shifted, g + 1)
                nc.scalar.activation(a[u][:, :, :], a[u][:, :, :], ACT.Exp).then_inc(exp_done, 1)

            def turn_p(g, u):
                act.wait_ge(p_turned, g + 1)
                if has(g, 2):
                    act.wait_ge(edge_done, g - 1)
                nc.scalar.activation(pT[u][:, :, :], tiles(bP), ACT.Copy).then_inc(pT_ready, 1)

            def sums_and_alpha(g, u):
                sums(g, u)
                alpha(g, u)

            software_pipeline(act, [None, turn, sums_and_alpha, second, turn_p, None], NG)

        @block.gpsimd
        def _(pool):
            for u in range(2):
                nc.gpsimd.memset(pD[u][:, :, :], 0.0).then_inc(zeroed, 1)
            pool.wait_ge(zeroed, 2)

            def place(g, u):
                pool.wait_ge(exp_done, g + 1)
                if has(g, 2):
                    pool.wait_ge(p_turned, g - 1)
                pool.sem_inc(begun, 1)
                for b, h in enumerate(halves):
                    last = nc.gpsimd.tensor_copy(pD[u][h, :, h], a[u][h, :, :])
                last.then_inc(pD_ready, 1)

            software_pipeline(pool, [None, None, None, place, None, None], NG)

        @block.vector
        def _(dve):
            chain = Chain(dve, chain_sem, 0)
            chain.start(0)
            link = chain.link
            dve.wait_ge(loaded, 64)
            dve.wait_ge(v_done, 1)
            link(dve.tensor_copy(v1[:, :], bcast(b1[:, 0:1], [P, P])))
            link(dve.tensor_copy(v2[:, :], bcast(b1[:, 1:2], [P, P])))
            link(dve.tensor_reduce(deg[:, :], adj[:, :, :], AX.X, ALU.add))
            link(dve.tensor_scalar(some[:, :], deg[:, :], 0.0, None, ALU.is_gt))
            link(dve.tensor_tensor(deg[:, :], deg[:, :], some[:, :], ALU.mult))
            link(dve.tensor_scalar(some[:, :], some[:, :], -1.0, 1.0, ALU.mult, ALU.add))
            link(dve.tensor_tensor(deg[:, :], deg[:, :], some[:, :], ALU.add))
            dve.reciprocal(rdeg[:, :], deg[:, :]).then_inc(setup, 1)
            dve.wait_ge(setup, 1)
            e_links = Chain(dve, e_chain, 5)
            a_links = Chain(dve, a_chain, 4)

            def normalise(g, u):
                if has(g, 2):
                    dve.wait_ge(turned, g - 1)
                    dve.wait_ge(kept, g - 1)
                normalise_group(dve, lnb[u], X, MEAN, R, g).then_inc(ln_ready, 1)

            def wide(ap):
                return bcast(ap.unsqueeze(2), [P, GT, NODES])

            def before_alpha(g, u):
                e_links.start(g)
                dve.wait_ge(sums_done, g + 1)
                for b, h in enumerate(halves):
                    last = dve.tensor_tensor(s2j[u][h, :, :], group(adj, g)[h, :, :], tiles(b2)[h, :, h], ALU.mult)
                last.then_inc(s2_read, 1)
                dve.wait_ge(s2_read, g + 1)
                e_links.link(dve.tensor_reduce(s2[u][:, :], s2j[u][:, :, :], AX.X, ALU.add))
                e_links.link(dve.tensor_tensor(s2[u][:, :], s2[u][:, :], rdeg[:, bass.ds(g * GT, GT)], ALU.mult))
                dve.wait_ge(s1_ready, g + 1)
                e_links.link(dve.tensor_tensor(e[u][:, :, :], s1[u][:, :, :], wide(s2[u][:, :]), ALU.add))
                e_links.link(dve.tensor_tensor(e[u][:, :, :], e[u][:, :, :], group(adj, g), ALU.mult))
                e_links.link(dve.tensor_scalar(mask[u][:, :, :], group(adj, g), 0.0, None, ALU.is_gt))
                dve.scalar_tensor_tensor(e[u][:, :, :], e[u][:, :, :], SLOPE, e[u][:, :, :], ALU.mult,
                                         ALU.max).then_inc(pre_ready, 1)

            def after_alpha(g, u):
                a_links.start(g)
                dve.wait_ge(alpha_ready, g + 1)
                if has(g, 2):
                    dve.wait_ge(pD_ready, g - 1)
                a_links.link(dve.tensor_tensor(a[u][:, :, :], e[u][:, :, :], mask[u][:, :, :], ALU.mult))
                a_links.link(dve.tensor_scalar(mask[u][:, :, :], mask[u][:, :, :], -1.0, FAR, ALU.add, ALU.mult))
                a_links.link(dve.tensor_tensor(a[u][:, :, :], a[u][:, :, :], mask[u][:, :, :], ALU.add))
                a_links.link(dve.tensor_reduce(top[u][:, :], a[u][:, :, :], AX.X, ALU.max))
                dve.tensor_tensor(a[u][:, :, :], a[u][:, :, :], wide(top[u][:, :]), ALU.subtract).then_inc(shifted, 1)

            def totals(g, u):
                dve.wait_ge(exp_done, g + 1)
                dve.tensor_reduce(inv[u][:, :], a[u][:, :, :], AX.X, ALU.add).then_inc(inv_ready, 1)
                dve.wait_ge(inv_ready, g * 2 + 1)
                dve.reciprocal(inv[u][:, :], inv[u][:, :]).then_inc(inv_ready, 1)

            def add(g, u):
                dve.wait_ge(edge_done, g + 1)
                dve.wait_ge(inv_ready, g * 2 + 2)
                for j in range(GT):
                    xt = X[:, bass.ds(g * GT + j, 1), :].rearrange("p o d -> p (o d)")
                    last = dve.scalar_tensor_tensor(xt, bY[:, j * D:(j + 1) * D], inv[u][:, j:j + 1], xt,
                                                    ALU.mult, ALU.add)
                last.then_inc(x_done, 1)
                group_stats(dve, STATS, X, g, x_done, carried)

            software_pipeline(dve, [normalise, None, before_alpha, after_alpha, totals, add], NG)


class Experts:

    def __init__(self, name, src, top_k, hidden, capacity, act, tiles):
        self.name, self.src, self.top_k, self.hidden = name, src, top_k, hidden
        self.capacity, self.act, self.tiles = capacity, act, tiles
        self.chunks = [(c, min(P, hidden - c)) for c in range(0, hidden, P)]
        self.gated = act == "silu"


E = 8
ROW = D + 2
NO_ROW = 1 << 30
L0_CAPACITY = -(-5 * TOKENS // (4 * E))
WAYS = 8
UP, DOWN = 3, 6
TURNS = (2 * T + E + 7) // WAYS + 1
SPARE = E
EXPERTS = {
    "B": Experts("B", "L0_ffn", 1, 512, L0_CAPACITY, "relu", E * L0_CAPACITY // P),
    "F": Experts("F", "L2_ffn", 2, 341, None, "silu", 2 * T + SPARE),
    "H": Experts("H", "L3_ffn", 2, 256, None, "gelu", 2 * T + SPARE),
}


def prefill(nc, stack, scratch, blank):
    sc = Scope(nc, stack, "fill")
    blank_ready, filled = sc.sem("blank_ready"), sc.sem("filled")
    count = 0
    with nc.Block() as block:
        @block.vector
        def _(dve):
            dve.memset(blank[:, 0:D + 1], 0.0).then_inc(blank_ready, 1)
            dve.memset(blank[:, D + 1:ROW].bitcast(U32), NO_ROW).then_inc(blank_ready, 1)

        @block.sync
        def _(sp):
            sp.wait_ge(blank_ready, 2)
            for name, (rows, result) in scratch.items():
                n = EXPERTS[name].tiles
                sp.dma_start(rows.rearrange("(n p) c -> p n c", p=P),
                             bcast(blank[:, :].unsqueeze(1), [P, n, ROW])).then_inc(filled, 16)
                if name == "B":
                    sp.dma_start(result.rearrange("(n p) c -> p n c", p=P),
                                 bcast(blank[:, 0:D].unsqueeze(1), [P, T, D])).then_inc(filled, 16)
    return filled, 16 * (len(scratch) + ("B" in scratch))


def expert_logits(nc, m, g_in, X, XN, MEAN, R, LOG, ident, banks):
    with ExitStack() as stack:
        sc = Scope(nc, stack, m.name + "1")
        affine, biased = m.act == "gelu", m.act != "silu"
        gate = sc.sb("gate", [P, E])
        gate_b = sc.sb("gate_b", [P, E])
        gamma = sc.sb("gamma", [P, D])
        beta = sc.sb("beta", [P, D])
        lnb = [sc.sb(f"lnb{u}", [P, GT, D]) for u in range(2)]
        lnT = [sc.sb(f"lnT{u}", [P, GT, P]) for u in range(2)]
        loaded, ln_chain, ln_ready = sc.sem("loaded"), sc.sem("ln_chain"), sc.sem("ln_ready")
        turned, lnT_ready, kept = sc.sem("turned"), sc.sem("lnT_ready"), sc.sem("kept")
        logits_done, logits_read = sc.sem("logits_done"), sc.sem("logits_read")
        pT, pL = banks[0:2], banks[2:4]
        loads = 16 * (1 + biased + 2 * affine)
        block = stack.enter_context(nc.Block())

        @block.sync
        def _(sp):
            sp.dma_start(gate[:, :], g_in[m.src + "_gate"]).then_inc(loaded, 16)
            if biased:
                sp.dma_start(gate_b[:, :], bcast(g_in[m.src + "_gate_b"], [P, E])).then_inc(loaded, 16)
            if affine:
                sp.dma_start(gamma[:, :], bcast(g_in[m.src + "_gamma"], [P, D])).then_inc(loaded, 16)
                sp.dma_start(beta[:, :], bcast(g_in[m.src + "_beta"], [P, D])).then_inc(loaded, 16)

        @block.vector
        def _(dve):
            dve.wait_ge(loaded, loads)

            def normalise(g, u):
                if has(g, 2):
                    dve.wait_ge(turned, g - 1)
                    dve.wait_ge(kept, g - 1)
                ins = normalise_group(dve, lnb[u], X, MEAN, R, g)
                if affine:
                    ins.then_inc(ln_chain, 1)
                    dve.wait_ge(ln_chain, g * 2 + 1)
                    dve.tensor_tensor(lnb[u][:, :, :], lnb[u][:, :, :],
                                      bcast(gamma[:, :].unsqueeze(1), [P, GT, D]), ALU.mult).then_inc(ln_chain, 1)
                    dve.wait_ge(ln_chain, g * 2 + 2)
                    ins = dve.tensor_tensor(lnb[u][:, :, :], lnb[u][:, :, :],
                                            bcast(beta[:, :].unsqueeze(1), [P, GT, D]), ALU.add)
                ins.then_inc(ln_ready, 1)

            def logits(g, u):
                dve.wait_ge(logits_done, g + 1)
                src = pL[u][:, 0:GT * E].rearrange("p (t e) -> p t e", t=GT)
                if biased:
                    dve.tensor_tensor(group(LOG, g), src, bcast(gate_b[:, :].unsqueeze(1), [P, GT, E]),
                                      ALU.add).then_inc(logits_read, 1)
                else:
                    dve.tensor_copy(group(LOG, g), src).then_inc(logits_read, 1)

            software_pipeline(dve, [normalise, None, None, logits], NG)

        @block.tensor
        def _(pe):
            def turn(g, u):
                pe.wait_ge(ln_ready, g + 1)
                if has(g, 2):
                    pe.wait_ge(lnT_ready, g - 1)
                for j in range(GT):
                    last = nc.tensor.transpose(pT[u][:, j * P:(j + 1) * P], lnb[u][:, j, :], ident[:, :])
                last.then_inc(turned, 1)

            def logits(g, u):
                pe.wait_ge(lnT_ready, g + 1)
                if has(g, 2):
                    pe.wait_ge(logits_read, g - 1)
                for j in range(GT):
                    last = nc.tensor.matmul(pL[u][:, j * E:(j + 1) * E], lnT[u][:, j, :], gate[:, :],
                                            start=True, stop=True)
                last.then_inc(logits_done, 1)

            pe.wait_ge(loaded, loads)
            software_pipeline(pe, [None, turn, logits, None], NG)

        @block.scalar
        def _(act):
            def turn(g, u):
                act.wait_ge(turned, g + 1)
                if has(g, 2):
                    act.wait_ge(logits_done, g - 1)
                nc.scalar.activation(lnT[u][:, :, :], pT[u][:, :].rearrange("p (t d) -> p t d", t=GT),
                                     ACT.Copy).then_inc(lnT_ready, 1)
                nc.scalar.activation(group(XN, g), lnb[u][:, :, :], ACT.Copy).then_inc(kept, 1)

            software_pipeline(act, [None, turn, None, None], NG)


def route(nc, m, g_in, LOG, META, ROWS, TILE_E, banks):
    with ExitStack() as stack:
        sc = Scope(nc, stack, m.name + "2")
        K, NT = m.top_k, m.tiles
        tri = sc.sb("tri", [P, P])
        ones = sc.sb("ones", [P, P])
        steps = sc.sb("steps", [P, T])
        tile_no = sc.sb("tile_no", [P, NT])
        places = sc.sb("places", [P, T, 2], U32)
        top = [sc.sb(f"top{k}", [P, T]) for k in range(K)]
        masked = sc.sb("masked", [P, T, E])
        equal = sc.sb("equal", [P, T, E])
        taken = sc.sb("taken", [P, 2, T])
        chosen = [sc.sb(f"chosen{k}", [P, T, E]) for k in range(K)]
        any_chosen = sc.sb("any_chosen", [P, T, E])
        z = sc.sb("z", [P, T, E])
        esum = sc.sb("esum", [P, T])
        inv = sc.sb("inv", [P, T])
        e2 = sc.sb("e2", [P, T])
        tot = sc.sb("tot", [P, E, T])
        cum = sc.sb("cum", [P, E, T])
        cmp = sc.sb("cmp", [P, E, T])
        cmp2 = sc.sb("cmp2", [P, NT, E])
        nt = sc.sb("nt", [P, E])
        nt_cum = sc.sb("nt_cum", [P, E])
        off = sc.sb("off", [P, E])
        pos = sc.sb("pos", [P, T, E])
        row = sc.sb("row", [P, T])
        over = sc.sb("over", [P, T])
        tile_e = sc.sb("tile_e", [1, DOWN + WAYS * TURNS])
        digits = sc.sb("digits", [1, WAYS])
        words = sc.sb("words", [1, 2, TURNS, WAYS])
        word_sum = sc.sb("word_sum", [1, 2, TURNS])
        loaded, chain_sem = sc.sem("loaded"), sc.sem("chain")
        z_ready, exp_done, chosen_ready = sc.sem("z_ready"), sc.sem("exp_done"), sc.sem("chosen_ready")
        counted = sc.sem("counted")
        pU, pO = banks[0:2]
        block = stack.enter_context(nc.Block())

        @block.sync
        def _(sp):
            sp.dma_start(tri[:, :], g_in["c_tri"]).then_inc(loaded, 16)
            sp.dma_start(digits[:, :], g_in["c_digits"]).then_inc(loaded, 16)
            sp.dma_start(ones[:, :], g_in["c_ones"]).then_inc(loaded, 16)
            sp.dma_start(steps[:, :], bcast(g_in["c_steps"], [P, T])).then_inc(loaded, 16)
            sp.dma_start(tile_no[:, :], bcast(g_in["c_tile_no"][:, 0:NT], [P, NT])).then_inc(loaded, 16)
            sp.dma_start(places[:, :, :], g_in["c_places"]).then_inc(loaded, 16)

        @block.scalar
        def _(act):
            act.wait_ge(z_ready, 1)
            nc.scalar.activation(z[:, :, :], z[:, :, :], ACT.Exp).then_inc(exp_done, 1)
            if K == 2:
                act.wait_ge(z_ready, 2)
                nc.scalar.activation(e2[:, :], e2[:, :], ACT.Exp).then_inc(exp_done, 1)

        @block.tensor
        def _(pe):
            pe.wait_ge(loaded, 96)
            pe.wait_ge(chosen_ready, 1)
            flat = any_chosen[:, :, :].rearrange("p t e -> p (t e)")
            nc.tensor.matmul(pU[:, :], tri[:, :], flat, start=True, stop=True).then_inc(counted, 1)
            nc.tensor.matmul(pO[:, :], ones[:, :], flat, start=True, stop=True).then_inc(counted, 1)

        @block.vector
        def _(dve):
            chain = Chain(dve, chain_sem, 0)
            chain.start(0)
            link = chain.link

            def wide(ap):
                return bcast(ap.unsqueeze(2), [P, T, E])

            dve.wait_ge(loaded, 96)
            for k in range(K):
                src = LOG if k == 0 else masked
                link(dve.tensor_reduce(top[k][:, :], src[:, :, :], AX.X, ALU.max))
                link(dve.tensor_tensor(equal[:, :, :], src[:, :, :], wide(top[k][:, :]), ALU.is_equal))
                link(dve.memset(taken[:, 0, :], 0.0))
                for e in range(E):
                    link(dve.tensor_tensor(chosen[k][:, :, e], equal[:, :, e], taken[:, e % 2, :], ALU.is_gt))
                    link(dve.tensor_tensor(taken[:, (e + 1) % 2, :], equal[:, :, e], taken[:, e % 2, :], ALU.max))
                if k == 0:
                    dve.tensor_tensor(z[:, :, :], LOG[:, :, :], wide(top[0][:, :]),
                                      ALU.subtract).then_inc(z_ready, 1)
                    if K == 2:
                        link(dve.scalar_tensor_tensor(masked[:, :, :], chosen[0][:, :, :], -1e30, LOG[:, :, :],
                                                      ALU.mult, ALU.add))
            if K == 2:
                dve.tensor_tensor(e2[:, :], top[1][:, :], top[0][:, :], ALU.subtract).then_inc(z_ready, 1)
                dve.tensor_tensor(any_chosen[:, :, :], chosen[0][:, :, :], chosen[1][:, :, :],
                                  ALU.add).then_inc(chosen_ready, 1)
            else:
                dve.tensor_copy(any_chosen[:, :, :], chosen[0][:, :, :]).then_inc(chosen_ready, 1)

            dve.wait_ge(exp_done, K)
            weights = [META[:, :, k, 0] for k in range(K)]
            if m.name == "H":
                link(dve.tensor_scalar(esum[:, :], e2[:, :], 1.0, None, ALU.add))
                link(dve.reciprocal(weights[0], esum[:, :]))
                link(dve.tensor_tensor(weights[1], e2[:, :], weights[0], ALU.mult))
            else:
                link(dve.tensor_reduce(esum[:, :], z[:, :, :], AX.X, ALU.add))
                link(dve.reciprocal(inv[:, :], esum[:, :]))
                if K == 1:
                    link(dve.tensor_copy(weights[0], inv[:, :]))
                else:
                    link(dve.tensor_tensor(e2[:, :], e2[:, :], inv[:, :], ALU.mult))
                    link(dve.tensor_tensor(esum[:, :], e2[:, :], inv[:, :], ALU.add))
                    link(dve.tensor_scalar(esum[:, :], esum[:, :], 1e-9, None, ALU.add))
                    link(dve.reciprocal(over[:, :], esum[:, :]))
                    link(dve.tensor_tensor(weights[0], inv[:, :], over[:, :], ALU.mult))
                    link(dve.tensor_tensor(weights[1], e2[:, :], over[:, :], ALU.mult))
            for k in range(K):
                link(dve.tensor_copy(META[:, :, k, 1].bitcast(U32), places[:, :, k]))

            dve.wait_ge(counted, 2)
            link(dve.tensor_copy(tot[:, :, :], pO[:, :].rearrange("p (t e) -> p e t", e=E)))
            for e in range(E):
                link(dve.tensor_tensor_scan(cum[:, e, :], ones[:, 0:T], tot[:, e, :], 0.0, ALU.mult, ALU.add))
            link(dve.tensor_tensor(tot[:, :, :], cum[:, :, :], tot[:, :, :], ALU.subtract))
            link(dve.tensor_tensor(pos[:, :, :], pU[:, :].rearrange("p (t e) -> p t e", e=E),
                                   tot[:, :, :].rearrange("p e t -> p t e"), ALU.add))
            if m.capacity is None:
                link(dve.tensor_tensor(cmp[:, :, :], bcast(cum[:, :, T - 1:T], [P, E, T]),
                                       bcast(steps[:, :].unsqueeze(1), [P, E, T]), ALU.is_gt))
                link(dve.tensor_reduce(nt[:, :], cmp[:, :, :], AX.X, ALU.add))
                link(dve.tensor_tensor_scan(nt_cum[:, :], ones[:, 0:E], nt[:, :], 0.0, ALU.mult, ALU.add))
                link(dve.tensor_tensor(off[:, :], nt_cum[:, :], nt[:, :], ALU.subtract))
                link(dve.tensor_scalar(off[:, :], off[:, :], float(P), -1.0, ALU.mult, ALU.add))
            else:
                link(dve.tensor_scalar(nt_cum[:, :], tile_no[:, 0:E], 1.0, float(m.capacity // P), ALU.add, ALU.mult))
                link(dve.tensor_scalar(off[:, :], tile_no[:, 0:E], float(m.capacity), -1.0, ALU.mult, ALU.add))
            link(dve.tensor_tensor(cmp2[:, :, 0:E - 1], bcast(nt_cum[:, 0:E - 1].unsqueeze(1), [P, NT, E - 1]),
                                   bcast(tile_no[:, :].unsqueeze(2), [P, NT, E - 1]), ALU.is_le))
            link(dve.memset(tile_e[:, :], 0.0))
            link(dve.tensor_reduce(tile_e[:, DOWN:DOWN + NT], cmp2[0:1, :, 0:E - 1], AX.X, ALU.add))
            for i, first in enumerate((DOWN - UP, 0)):
                part = tile_e[:, first:first + WAYS * TURNS].rearrange("p (j k) -> p j k", k=WAYS)
                link(dve.tensor_tensor(words[:, i, :, :], part, bcast(digits[:, :].unsqueeze(1), [1, TURNS, WAYS]),
                                       ALU.mult))
            link(dve.tensor_reduce(word_sum[:, :, :], words[:, :, :, :], AX.X, ALU.add))
            link(dve.tensor_copy(TILE_E[:, :, :], word_sum[:, :, :]))
            for k in range(K):
                if m.capacity is not None:
                    link(dve.tensor_tensor(masked[:, :, :], pos[:, :, :], chosen[k][:, :, :], ALU.mult))
                    link(dve.tensor_reduce(over[:, :], masked[:, :, :], AX.X, ALU.add))
                    link(dve.tensor_scalar(over[:, :], over[:, :], float(m.capacity), 1e6, ALU.is_gt, ALU.mult))
                link(dve.tensor_tensor(equal[:, :, :], pos[:, :, :], bcast(off[:, :].unsqueeze(1), [P, T, E]),
                                       ALU.add))
                link(dve.tensor_tensor(equal[:, :, :], equal[:, :, :], chosen[k][:, :, :], ALU.mult))
                link(dve.tensor_reduce(row[:, :], equal[:, :, :], AX.X, ALU.add))
                if m.capacity is not None:
                    link(dve.tensor_tensor(row[:, :], row[:, :], over[:, :], ALU.add))
                link(dve.tensor_copy(ROWS[:, :, k], row[:, :]))


def dispatch(nc, m, XN, META, ROWS, rows, filled, fills):
    SENDS = 4
    with ExitStack() as stack:
        sc = Scope(nc, stack, m.name + "3")
        K, n_rows = m.top_k, m.tiles * P
        stage = [sc.sb(f"stage{u}", [P, K, ROW]) for u in range(SENDS)]
        index = [[sc.sb(f"index{u}_{k}", [P, 1], U32) for k in range(K)] for u in range(SENDS)]
        begun = sc.sem("begun")
        x_staged, meta_staged, sent = sc.sem("x_staged"), sc.sem("meta_staged"), sc.sems("sent", SENDS)
        block = stack.enter_context(nc.Block())

        def free(eng, t, u):
            if has(t, SENDS):
                eng.wait_ge(sent[u], (t - u) * (16 * K // SENDS))

        @block.scalar
        def _(act):
            def copy_x(t, u):
                free(act, t, u)
                nc.scalar.activation(stage[u][:, :, 0:D], bcast(XN[:, bass.ds(t, 1), :], [P, K, D]),
                                     ACT.Copy).then_inc(x_staged, 1)

            software_pipeline(act, [copy_x, None], T, SENDS)

        @block.vector
        def _(dve):
            def copy_meta(t, u):
                free(dve, t, u)
                dve.tensor_copy(stage[u][:, :, D:ROW].bitcast(U32),
                                META[:, bass.ds(t, 1), :, :].rearrange("p o k c -> p (o k) c").bitcast(U32)
                                ).then_inc(meta_staged, 1)
                for k in range(K):
                    dve.tensor_copy(index[u][k][:, :], ROWS[:, bass.ds(t, 1), k]).then_inc(meta_staged, 1)

            software_pipeline(dve, [copy_meta, None], T, SENDS)

        @block.gpsimd
        def _(pool):
            pool.wait_ge(filled, fills)

            last_row = pool.to_reg(n_rows - 1)

            def send(t, u):
                pool.wait_ge(x_staged, t + 1)
                pool.wait_ge(meta_staged, (t + 1) * (1 + K))
                pool.sem_inc(begun, 1)
                for k in range(K):
                    pool.indirect_dma_start(rows, bass.IndirectOffsetOnAxis(ap=index[u][k][:, :], axis=0),
                                            stage[u][:, k, :], None, bounds_check=last_row,
                                            oob_is_err=False).then_inc(sent[u], 16)

            software_pipeline(pool, [None, send], T, SENDS)
            for u in range(SENDS):
                pool.wait_ge(sent[u], 16 * K * T // SENDS)


def load_weights(nc, sc, m, g_in):
    H, C = m.hidden, len(m.chunks)
    w_up = sc.sb("w_up", [P, E, H])
    w_gate = sc.sb("w_gate", [P, E, H]) if m.gated else None
    w_down = sc.sb("w_down", [P, E, C, D])
    b_up = None if m.gated else sc.sb("b_up", [P, E, H])
    b_down = None if m.gated else sc.sb("b_down", [P, E, D])
    loaded = sc.sem("loaded")
    with nc.Block() as block:
        @block.scalar
        def _(act):
            act.dma_start(w_up[:, :, :], g_in[m.src + "_up"].rearrange("e d f -> d e f")).then_inc(loaded, 16)
            if m.gated:
                act.dma_start(w_gate[:, :, :], g_in[m.src + "_up3"].rearrange("e d f -> d e f")).then_inc(loaded, 16)
            for c, (f0, nf) in enumerate(m.chunks):
                act.dma_start(w_down[0:nf, :, c, :],
                              g_in[m.src + "_down"][:, f0:f0 + nf, :].rearrange("e f d -> f e d")).then_inc(loaded, 16)
            if not m.gated:
                act.dma_start(b_up[:, :, :].rearrange("p e f -> p (e f)"),
                              bcast(g_in[m.src + "_b_up"], [P, E * H])).then_inc(loaded, 16)
                act.dma_start(b_down[:, :, :].rearrange("p e f -> p (e f)"),
                              bcast(g_in[m.src + "_b_down"], [P, E * D])).then_inc(loaded, 16)
    return (w_up, w_gate, w_down, b_up, b_down), loaded, 16 * (C + 1 + (1 if m.gated else 2))


def run_experts(nc, m, g_in, TILE_E, rows, result, ident, banks, weights, loaded, n_loads):
    with ExitStack() as stack:
        sc = Scope(nc, stack, m.name + "4")
        NT, H, C = m.tiles, m.hidden, len(m.chunks)
        w_up, w_gate, w_down, b_up, b_down = weights
        xt = [sc.sb(f"xt{u}", [P, ROW]) for u in range(WAYS)]
        xT = [sc.sb(f"xT{u}", [P, P]) for u in range(2)]
        h = [sc.sb(f"h{u}", [P, H]) for u in range(2)]
        act_h = [sc.sb(f"act_h{u}", [P, H]) for u in range(2)]
        hT = [sc.sb(f"hT{u}", [P, C, P]) for u in range(2)]
        place = [sc.sb(f"place{u}", [P, 1], U32) for u in range(WAYS)]
        y = [sc.sb(f"y{u}", [P, D]) for u in range(WAYS)]
        yc = [sc.sb(f"yc{u}", [P, D]) for u in range(2)]
        no_number = [sc.sb(f"no_number{u}", [P, D], U32) for u in range(2)]
        finite = [sc.sb(f"finite{u}", [P, D], U32) for u in range(2)]
        zeros = sc.sb("zeros", [P, D])
        x_in = sc.sems("x_in", WAYS)
        begun = sc.sem("begun")
        turned, xT_ready, up_done, h_ready = sc.sem("turned"), sc.sem("xT_ready"), sc.sem("up_done"), sc.sem("h_ready")
        act_ready, h_turned, hT_ready = sc.sem("act_ready"), sc.sem("h_turned"), sc.sem("hT_ready")
        down_done, down_read, y_ready = sc.sem("down_done"), sc.sem("down_read"), sc.sem("y_ready")
        settled = sc.sem("settled")
        zeroed, chain_sem, out = sc.sem("zeroed"), sc.sem("chain"), sc.sems("out", WAYS)
        up_read = h_ready if m.act == "gelu" else act_ready
        down_bank_read = y_ready if m.gated else down_read
        pX, pH, pY = banks[0:3]
        pUp, pGate = banks[3:5], banks[5:7]
        n_result = m.top_k * TOKENS
        block = stack.enter_context(nc.Block())

        @block.sync
        def _(sp):
            def load(t, w):
                if has(t, WAYS):
                    sp.wait_ge(y_ready, t - (WAYS - 1))
                sp.dma_start(xt[w][:, :], rows[bass.ds(t * P, P), :]).then_inc(x_in[w], 16)

            software_pipeline(sp, [load] + [None] * 7, NT, WAYS)

        class TileExperts:

            def __init__(self, eng):
                self.eng = eng

            def turn(self, j):
                self.words = [self.eng.value_load(TILE_E[:, i, bass.ds(j, 1)], min_val=0, max_val=E ** WAYS - 1)
                              for i in range(2)]

            def of(self, w, phase):
                return (self.words[phase == DOWN] >> (3 * ((w + phase) % WAYS))) & (E - 1)

        @block.tensor
        def _(pe):
            pe.wait_ge(loaded, n_loads)
            experts = TileExperts(pe)

            def turn(t, w):
                pe.wait_ge(x_in[w], (t - w) * (16 // WAYS) + 16)
                if has(t, 1):
                    pe.wait_ge(xT_ready, t)
                nc.tensor.transpose(pX[:, 0:P], xt[w][:, 0:D], ident[:, :]).then_inc(turned, 1)

            def up(t, w):
                e = experts.of(w, UP)
                pe.wait_ge(xT_ready, t + 1)
                if has(t, 2):
                    pe.wait_ge(up_read, t - 1)
                mm = nc.tensor.matmul(pUp[w % 2][:, 0:H], xT[w % 2][:, :],
                                      w_up[:, bass.ds(e, 1), :].rearrange("p o f -> p (o f)"), start=True, stop=True)
                if m.gated:
                    mm = nc.tensor.matmul(pGate[w % 2][:, 0:H], xT[w % 2][:, :],
                                          w_gate[:, bass.ds(e, 1), :].rearrange("p o f -> p (o f)"),
                                          start=True, stop=True)
                mm.then_inc(up_done, 1)

            def turn_h(t, w):
                pe.wait_ge(act_ready, t + 1)
                if has(t, 1):
                    pe.wait_ge(hT_ready, t)
                for c, (f0, nf) in enumerate(m.chunks):
                    last = nc.tensor.transpose(pH[0:nf, c * P:(c + 1) * P], act_h[w % 2][:, f0:f0 + nf], ident[:, :])
                last.then_inc(h_turned, 1)

            def down(t, w):
                e = experts.of(w, DOWN)
                pe.wait_ge(hT_ready, t + 1)
                if has(t, 1):
                    pe.wait_ge(down_bank_read, t)
                for c, (f0, nf) in enumerate(m.chunks):
                    last = nc.tensor.matmul(pY[:, 0:D], hT[w % 2][0:nf, c, :],
                                            w_down[0:nf, bass.ds(e, 1), c, :].rearrange("p o d -> p (o d)"),
                                            start=(c == 0), stop=(c == C - 1))
                last.then_inc(down_done, 1)

            software_pipeline(pe, [None, None, turn, up, None, turn_h, down, None], NT, WAYS, experts.turn)

        @block.scalar
        def _(act):
            def turn(t, w):
                act.wait_ge(turned, t + 1)
                if has(t, 2):
                    act.wait_ge(up_done, t - 1)
                nc.scalar.activation(xT[w % 2][:, :], pX[:, 0:P], ACT.Copy).then_inc(xT_ready, 1)

            def silu_or_gelu(t, w):
                if m.gated:
                    act.wait_ge(up_done, t + 1)
                    if has(t, 2):
                        act.wait_ge(act_ready, t - 1)
                    nc.scalar.activation(h[w % 2][:, :], pUp[w % 2][:, 0:H], ACT.Silu).then_inc(h_ready, 1)
                elif m.act == "gelu":
                    act.wait_ge(h_ready, t + 1)
                    if has(t, 2):
                        act.wait_ge(h_turned, t - 1)
                    nc.scalar.activation(act_h[w % 2][:, :], h[w % 2][:, :], ACT.Gelu).then_inc(act_ready, 1)

            def turn_h(t, w):
                act.wait_ge(h_turned, t + 1)
                if has(t, 2):
                    act.wait_ge(down_done, t - 1)
                func = ACT.Relu if m.act == "relu" else ACT.Copy
                full = H // P
                ins = nc.scalar.activation(hT[w % 2][:, 0:full, :],
                                           pH[:, 0:full * P].rearrange("p (c q) -> p c q", q=P), func)
                if H % P:
                    ins = nc.scalar.activation(hT[w % 2][0:H % P, full, :], pH[0:H % P, full * P:(full + 1) * P], func)
                ins.then_inc(hT_ready, 1)

            software_pipeline(act, [None, None, turn, silu_or_gelu if m.gated else None,
                                    silu_or_gelu if m.act == "gelu" else None, turn_h, None, None], NT, WAYS)

        @block.vector
        def _(dve):
            dve.wait_ge(loaded, n_loads)
            chain = Chain(dve, chain_sem, 3)
            experts = TileExperts(dve)
            dve.memset(zeros[:, :], 0.0).then_inc(zeroed, 1)
            dve.wait_ge(zeroed, 1)

            def activate(t, w):
                if m.gated:
                    dve.wait_ge(h_ready, t + 1)
                    if has(t, 2):
                        dve.wait_ge(h_turned, t - 1)
                    dve.tensor_tensor(act_h[w % 2][:, :], h[w % 2][:, :], pGate[w % 2][:, 0:H], ALU.mult).then_inc(act_ready, 1)
                    return
                e = experts.of(w, UP)
                dve.wait_ge(up_done, t + 1)
                if has(t, 2):
                    dve.wait_ge(h_turned if m.act == "relu" else act_ready, t - 1)
                dst = act_h if m.act == "relu" else h
                ready = act_ready if m.act == "relu" else h_ready
                dve.tensor_tensor(dst[w % 2][:, :], pUp[w % 2][:, 0:H],
                                  b_up[:, bass.ds(e, 1), :].rearrange("p o f -> p (o f)"), ALU.add).then_inc(ready, 1)

            def finish(t, w):
                weight = xt[w][:, D:D + 1]
                free_y(dve, t, w)
                dve.tensor_copy(place[w][:, :], xt[w][:, D + 1:ROW].bitcast(U32))
                if m.gated:
                    dve.wait_ge(down_done, t + 1)
                    dve.tensor_scalar(y[w][:, :], pY[:, 0:D], weight, None, ALU.mult).then_inc(y_ready, 1)
                    return
                e = experts.of(w, DOWN)
                dve.wait_ge(down_done, t + 1)
                yy, cc = y[w][:, :], yc[w % 2][:, :]
                chain.start(t)
                dve.tensor_tensor(cc, pY[:, 0:D], b_down[:, bass.ds(e, 1), :].rearrange("p o f -> p (o f)"),
                                  ALU.add).then_inc(down_read, 1)
                dve.wait_ge(down_read, t + 1)
                if m.act == "gelu":
                    dve.tensor_scalar(yy, cc, weight, None, ALU.mult).then_inc(y_ready, 1)
                    return
                chain.link(dve.tensor_scalar(cc, cc, weight, None, ALU.mult))
                dve.tensor_scalar(yy, cc, 1e4, -1e4, ALU.min, ALU.max)
                dve.tensor_tensor(no_number[w % 2][:, :], cc, cc, ALU.not_equal)
                chain.link(dve.scalar_tensor_tensor(finite[w % 2][:, :], cc, 0.0, zeros[:, :], ALU.mult, ALU.is_equal))
                dve.sem_inc(settled, 1)
                chain.link(dve.copy_predicated(yy, no_number[w % 2][:, :], zeros[:, :]))
                dve.sem_inc(settled, 1)
                dve.copy_predicated(yy, finite[w % 2][:, :], cc).then_inc(y_ready, 1)

            def free_y(eng, t, w):
                if has(t, WAYS):
                    eng.wait_ge(out[w], (t - w) * (16 // WAYS))

            software_pipeline(dve, [None, None, None, None if m.gated else activate, activate if m.gated else None, None,
                                    finish, None], NT, WAYS,
                              None if m.gated else experts.turn)

        @block.gpsimd
        def _(pool):
            last_place = pool.to_reg(n_result - 1)

            def send(t, w):
                pool.wait_ge(y_ready, t + 1)
                pool.sem_inc(begun, 1)
                pool.indirect_dma_start(result, bass.IndirectOffsetOnAxis(ap=place[w][:, :], axis=0),
                                        y[w][:, :], None, bounds_check=last_place,
                                        oob_is_err=False).then_inc(out[w], 16)

            software_pipeline(pool, [None] * 7 + [send], NT, WAYS)
            for w in range(WAYS):
                pool.wait_ge(out[w], 16 * NT // WAYS)


def combine(nc, m, X, STATS, result, out):
    with ExitStack() as stack:
        sc = Scope(nc, stack, m.name + "5")
        K, n, tiles = m.top_k, NG // 2, 2 * GT
        part = [sc.sb(f"part{u}", [P, K, tiles, D]) for u in range(2)]
        x_done, part_in, carried, x_out = sc.sem("x_done"), sc.sems("part_in"), sc.sem("carried"), sc.sem("x_out")
        block = stack.enter_context(nc.Block())

        @block.sync
        def _(sp):
            for g in range(n):
                if g >= 2:
                    sp.wait_ge(x_done, K * (g - 1))
                for k in range(K):
                    src = result[bass.ds(k * TOKENS + g * tiles * P, tiles * P), :]
                    sp.dma_start(part[g % 2][:, k, :, :], src.rearrange("(t p) d -> p t d", p=P)).then_inc(part_in[g % 2], 16)

        @block.vector
        def _(dve):
            for g in range(n):
                dve.wait_ge(part_in[g % 2], 16 * K * (g // 2 + 1))
                xs = X[:, g * tiles:(g + 1) * tiles, :]
                for k in range(K):
                    dve.tensor_tensor(xs, xs, part[g % 2][:, k, :, :], ALU.add).then_inc(x_done, 1)
                    dve.wait_ge(x_done, K * g + k + 1)
                if out is None:
                    dve.sem_inc(carried, 1)
                    for t in range(g * tiles, (g + 1) * tiles):
                        tile_stats(dve, STATS, X, t)

        @block.scalar
        def _(act):
            if out is not None:
                for g in range(n):
                    act.wait_ge(x_done, K * (g + 1))
                    dst = out[g * tiles * P:(g + 1) * tiles * P, :].rearrange("(t p) d -> p t d", p=P)
                    act.dma_start(dst, X[:, g * tiles:(g + 1) * tiles, :]).then_inc(x_out, 16)
                act.wait_ge(x_out, 16 * n)


def experts_layer(nc, m, g_in, X, XN, STATS, MEAN, R, ident, banks, rows, result, filled, fills, out):
    layer_norm(nc, "ln" + m.name, STATS, MEAN, R, twice=(m.act == "gelu"))
    with ExitStack() as stack:
        sc = Scope(nc, stack, m.name)
        LOG = sc.sb("logits", [P, T, E])
        META = sc.sb("meta", [P, T, m.top_k, 2])
        ROWS = sc.sb("rows", [P, T, m.top_k], U32)
        TILE_E = sc.sb("tile_e", [1, 2, TURNS], I32)
        weights = load_weights(nc, sc, m, g_in)
        expert_logits(nc, m, g_in, X, XN, MEAN, R, LOG, ident, banks)
        route(nc, m, g_in, LOG, META, ROWS, TILE_E, banks)
        dispatch(nc, m, XN, META, ROWS, rows, filled, fills)
        run_experts(nc, m, g_in, TILE_E, rows, result, ident, banks, *weights)
    combine(nc, m, X, STATS, result, out)


def program(nc, g_in, out):
    with ExitStack() as stack:
        sc = Scope(nc, stack, "all")
        X = sc.sb("X", [P, T, D])
        XN = sc.sb("XN", [P, T, D])
        MEAN = sc.sb("MEAN", [P, T])
        R = sc.sb("R", [P, T])
        STATS = sc.sb("STATS", [P, T, 6])
        ident = sc.sb("ident", [P, P])
        banks = [stack.enter_context(nc.psum_tensor(f"bank{i}", [P, 512], F32)) for i in range(8)]
        x_in, x_out, const_in, carried = sc.sems("x_in", NCH), sc.sem("x_out"), sc.sem("const_in"), sc.sem("carried")
        out_bias = {name: sc.sb(name, [P, D]) for name in ("L0_gnn_bo", "L1_ffn_bo")}
        scratch = {
            name: (nc.dram_tensor(f"dram_{name}_rows", (m.tiles * P, ROW), F32).ap(),
                   nc.dram_tensor(f"dram_{name}_result", (m.top_k * TOKENS, D), F32).ap())
            for name, m in EXPERTS.items() if name in STAGES
        }

        blank = sc.sb("blank", [P, ROW])
        early = stack.enter_context(ExitStack())
        adj_in = sc.sem("adj_in")
        adj = early.enter_context(nc.sbuf_tensor("A_adj", [P, T, NODES], F32))
        with nc.Block() as block:
            @block.sync
            def _(sp):
                for c in range(NCH):
                    src = g_in["x"][c * CH * P:(c + 1) * CH * P, :].rearrange("(t p) d -> p t d", p=P)
                    sp.dma_start(X[:, c * CH:(c + 1) * CH, :], src).then_inc(x_in[c], 16)
                sp.dma_start(adj[:, :, :], g_in["adj"].rearrange("(t p) j -> p t j", p=P)).then_inc(adj_in, 16)
                sp.dma_start(ident[:, :], g_in["c_ident"]).then_inc(const_in, 16)
                for name, buf in out_bias.items():
                    sp.dma_start(buf[:, :], bcast(g_in[name], [P, D])).then_inc(const_in, 16)
                sp.wait_ge(const_in, 48)

            @block.vector
            def _(dve):
                for c in range(NCH):
                    dve.wait_ge(x_in[c], 16)
                    dve.sem_inc(carried, 1)
                    for t in range(c * CH, (c + 1) * CH):
                        tile_stats(dve, STATS, X, t)

        filled, fills = prefill(nc, stack, scratch, blank)
        for stage in STAGES:
            if stage in EXPERTS:
                experts_layer(nc, EXPERTS[stage], g_in, X, XN, STATS, MEAN, R, ident, banks, *scratch[stage], filled, fills,
                              out if stage == STAGES[-1] else None)
            if stage == "A":
                layer_norm(nc, "lnA", STATS, MEAN, R)
                graph_attention(nc, g_in, X, XN, STATS, MEAN, R, ident, banks, out_bias["L0_gnn_bo"], adj, adj_in)
                early.close()
            if stage == "C":
                layer_norm(nc, "lnC", STATS, MEAN, R)
                group_gcns(nc, g_in, X, XN, STATS, MEAN, R, ident, banks)
            if stage == "D":
                layer_norm(nc, "lnD", STATS, MEAN, R)
                routed_mlp(nc, g_in, X, XN, STATS, MEAN, R, ident, banks, out_bias["L1_ffn_bo"])
            if stage == "E":
                layer_norm(nc, "lnE", STATS, MEAN, R)
                edge_attention(nc, g_in, X, XN, STATS, MEAN, R, ident, banks)
            if stage == "G":
                layer_norm(nc, "lnG", STATS, MEAN, R)
                dense_gcn(nc, g_in, X, XN, STATS, MEAN, R, ident, banks)

        if STAGES[-1] not in EXPERTS:
            with nc.Block() as block:
                @block.sync
                def _(sp):
                    sp.dma_start(out.rearrange("(t p) d -> p t d", p=P), X[:, :, :]).then_inc(x_out, 16)
                    sp.wait_ge(x_out, 16)


def kernel(**inputs):
    import numpy as np
    import concourse.bacc as bacc
    from concourse.bass_utils import run_bass_kernel_spmd

    a = {n: np.asarray(v) for n, v in inputs.items()}
    slot_adj = np.zeros((128, NODES, NODES), np.float32)
    slot_b2 = np.zeros((P, D), np.float32)
    slot_group = np.zeros((P, len(GROUPS)), np.float32)
    pick = np.zeros((P, P), np.float32)
    for g, nodes in enumerate(GROUPS):
        sl = slice(SLOT0[g], SLOT0[g] + len(nodes))
        slot_adj[:, sl, sl] = a["adj"][:, nodes][:, :, nodes]
        for b in range(2):
            rows = NODES * b + np.arange(sl.start, sl.stop)
            slot_b2[rows] = a["L1_gnn_b2"][g]
            slot_group[rows, g] = 1
            pick[NODES * b + np.array(nodes), rows] = 1
    lay = {
        "x": a["x"].reshape(TOKENS, D),
        "adj": a["adj"].reshape(TOKENS, NODES),
        "adjT": a["adj"].transpose(0, 2, 1).reshape(TOKENS, NODES),
        "nodemask": a["nodemask"].reshape(T, P).T,
        "L3_gnn_W": a["L3_gnn_W"].T,
        "L3_gnn_b": a["L3_gnn_b"].reshape(1, D),
        "L0_gnn_Wq": a["L0_gnn_Wq"].T, "L0_gnn_Wk": a["L0_gnn_Wk"].T, "L0_gnn_Wv": a["L0_gnn_Wv"].T,
        "L0_gnn_Wo": a["L0_gnn_Wo"].T, "L0_gnn_bo": a["L0_gnn_bo"].reshape(1, D),
        "c_head_of": np.repeat(np.eye(HEADS, dtype=np.float32), HD, axis=0),
        "slot_adj": slot_adj.reshape(TOKENS, NODES), "slot_adjT": slot_adj.transpose(0, 2, 1).reshape(TOKENS, NODES),
        "L1_gnn_W1": a["L1_gnn_W1"], "L1_gnn_W2": a["L1_gnn_W2"],
        "L1_gnn_b1": a["L1_gnn_b1"].reshape(len(GROUPS), 2, P).transpose(2, 0, 1),
        "L1_gnn_b2": slot_b2, "L1_gnn_fusion_w": a["L1_gnn_fusion_w"].reshape(1, -1),
        "c_slot_group": slot_group, "c_pick": pick, "c_spread": pick.T,
        "L1_ffn_route_id": a["L1_ffn_route_id"].reshape(1, T),
        "c_hex_digits": (float(ROUTES) ** np.arange(D_WAYS)).astype(np.float32).reshape(1, D_WAYS),
        "L1_ffn_Wr": a["L1_ffn_Wr"].reshape(LAYERS, ROUTES, MID, 2, P).transpose(4, 0, 1, 3, 2),
        "L1_ffn_Ws": a["L1_ffn_Ws"].reshape(LAYERS, MID, 2, P).transpose(3, 0, 2, 1),
        "c_eye2": np.eye(MID, dtype=np.float32).reshape(2, P, MID).transpose(1, 0, 2),
        "L1_ffn_br": a["L1_ffn_br"].reshape(1, -1), "L1_ffn_bs": a["L1_ffn_bs"].reshape(1, -1),
        "L1_ffn_Wi": a["L1_ffn_Wi"].T, "L1_ffn_bi": a["L1_ffn_bi"].reshape(2, P).T,
        "L1_ffn_Wo": a["L1_ffn_Wo"].reshape(D, 2, P).transpose(2, 1, 0), "L1_ffn_bo": a["L1_ffn_bo"].reshape(1, D),
        "L2_gnn_W1": a["L2_gnn_W1"].T, "L2_gnn_W2": a["L2_gnn_W2"].T, "L2_gnn_w3": a["L2_gnn_w3"].reshape(2, P).T,
        "c_ident": np.eye(P, dtype=np.float32),
        "c_tri": np.triu(np.ones((P, P), np.float32)),
        "c_digits": (float(E) ** np.arange(WAYS)).astype(np.float32).reshape(1, WAYS),
        "c_ones": np.ones((P, P), np.float32),
        "c_steps": (np.arange(T, dtype=np.float32) * P).reshape(1, T),
        "c_tile_no": np.arange(2 * T + SPARE, dtype=np.float32).reshape(1, -1),
        "c_places": (np.arange(P)[:, None, None] + np.arange(T)[None, :, None] * P
                     + np.arange(2)[None, None, :] * TOKENS).astype(np.uint32),
        "L0_ffn_gate": a["L0_ffn_gate_w"],
        "L0_ffn_gate_b": a["L0_ffn_gate_b"].reshape(1, E),
        "L0_ffn_up": a["L0_ffn_w1"],
        "L0_ffn_b_up": a["L0_ffn_b1"].reshape(1, -1),
        "L0_ffn_down": a["L0_ffn_w2"],
        "L0_ffn_b_down": a["L0_ffn_b2"].reshape(1, -1),
        "L2_ffn_gate": a["L2_ffn_router_w"].T,
        "L2_ffn_up": a["L2_ffn_w1"].transpose(0, 2, 1),
        "L2_ffn_up3": a["L2_ffn_w3"].transpose(0, 2, 1),
        "L2_ffn_down": a["L2_ffn_w2"].transpose(0, 2, 1),
        "L3_ffn_gate": a["L3_ffn_Wr"],
        "L3_ffn_gate_b": a["L3_ffn_br"].reshape(1, E),
        "L3_ffn_gamma": a["L3_ffn_gamma"].reshape(1, D),
        "L3_ffn_beta": a["L3_ffn_beta"].reshape(1, D),
        "L3_ffn_up": a["L3_ffn_W1"],
        "L3_ffn_b_up": a["L3_ffn_b1"].reshape(1, -1),
        "L3_ffn_down": a["L3_ffn_W2"],
        "L3_ffn_b_down": a["L3_ffn_b2"].reshape(1, -1),
    }
    nc = bacc.Bacc("TRN2", target_bir_lowering=False, num_devices=1)
    arrays, g_in = {}, {}
    for name, v in lay.items():
        v = np.ascontiguousarray(v)
        arrays[f"in_{name}"] = v
        g_in[name] = nc.dram_tensor(f"in_{name}", v.shape, mybir.dt.from_np(v.dtype), kind="ExternalInput").ap()
    out = nc.dram_tensor("out_x", (TOKENS, D), F32, kind="ExternalOutput").ap()
    program(nc, g_in, out)
    r = run_bass_kernel_spmd(nc, [arrays], core_ids=[0])
    return r.results[0]["out_x"].reshape(128, NODES, D)
```

```python
from contextlib import ExitStack

import concourse.bass as bass
from concourse import mybir

STAGES = 'ABCDEFGH'

F32 = mybir.dt.float32
I32 = mybir.dt.int32
U32 = mybir.dt.uint32
ALU = mybir.AluOpType
ACT = mybir.ActivationFunctionType
AX = mybir.AxisListType

P = 128
NODES = 64
D = 128
TOKENS = 128 * NODES
T = TOKENS // P
GT = 4
NG = T // GT
CH = 16
NCH = T // CH
LN_EPS = 1e-5


def software_pipeline(eng, phases, n, ways=2, at_turn=None):
    depth = len(phases) - 1
    first = -(-(depth + 2) // ways) * ways

    def step(s, slot):
        for p in range(depth, -1, -1):
            if phases[p] is not None and (not isinstance(s, int) or 0 <= s - p < n):
                phases[p](s - p, (slot - p) % ways)

    steady = (n - first) // ways
    at_turn = at_turn or (lambda turn: None)
    for s in range(first):
        if s % ways == 0:
            at_turn(s // ways)
        step(s, s % ways)
    with eng.Fori(0, steady) as i:
        at_turn(i + first // ways)
        for k in range(ways):
            step(i * ways + (first + k), k)
    for s in range(first + ways * steady, n + depth):
        if s % ways == 0:
            at_turn(s // ways)
        step(s, s % ways)


def has(item, back):
    return not isinstance(item, int) or item >= back


class Chain:

    def __init__(self, eng, sem, length):
        self.eng, self.sem, self.length = eng, sem, length

    def start(self, item):
        self.base, self.n = item * self.length, 0

    def link(self, ins):
        self.n += 1
        ins.then_inc(self.sem, 1)
        self.eng.wait_ge(self.sem, self.base + self.n)


class Scope:

    def __init__(self, nc, stack, name):
        self.nc, self.stack, self.name, self.held = nc, stack, name, []
        stack.callback(self.release)

    def release(self):
        if self.held:
            self.nc.clear_and_free_semaphores(self.held)
            self.nc.all_engine_barrier()

    def sb(self, name, shape, dt=F32):
        return self.stack.enter_context(self.nc.sbuf_tensor(f"{self.name}_{name}", shape, dt))

    def sem(self, name):
        self.held.append(self.nc.alloc_semaphore(f"{self.name}_{name}"))
        return self.held[-1]

    def sems(self, name, n=2):
        return [self.sem(f"{name}{i}") for i in range(n)]


def bcast(ap, shape):
    return ap.to_broadcast(shape)


def group(buf, g):
    return buf[:, bass.ds(g * GT, GT), :]


def tile_of(buf, t):
    return buf[:, bass.ds(t, 1), :].rearrange("p o d -> p (o d)")


def tile_stats(dve, STATS, X, t):
    return dve.bn_stats(STATS[:, bass.ds(t, 1), :].rearrange("p o s -> p (o s)"), tile_of(X, t))


def normalise_tile(dve, dst, X, MEAN, R, t):
    return dve.tensor_scalar(dst, tile_of(X, t), MEAN[:, bass.ds(t, 1)], R[:, bass.ds(t, 1)], ALU.subtract, ALU.mult)


def normalise_group(dve, dst, X, MEAN, R, g):
    for j in range(GT):
        last = normalise_tile(dve, dst[:, j, :], X, MEAN, R, g * GT + j)
    return last


def act_normalise_group(nc, dst, X, SHIFT, R, g):
    for j in range(GT):
        t = g * GT + j
        last = nc.scalar.activation(dst[:, j, :], tile_of(X, t), ACT.Identity, bias=SHIFT[:, bass.ds(t, 1)],
                                    scale=R[:, bass.ds(t, 1)])
    return last


def group_stats(dve, STATS, X, g, x_done, carried):
    dve.wait_ge(x_done, g + 1)
    dve.sem_inc(carried, 1)
    for j in range(GT):
        tile_stats(dve, STATS, X, g * GT + j)


def layer_norm(nc, name, STATS, MEAN, R, twice=False, SHIFT=None):
    with ExitStack() as stack:
        sc = Scope(nc, stack, name)
        half = sc.sb("half", [P, T])
        var = sc.sb("var", [P, T])
        var0 = sc.sb("var0", [P, T])
        ln_chain, std_ready = sc.sem("chain"), sc.sem("std_ready")
        links = 6 + 2 * twice
        block = stack.enter_context(nc.Block())

        @block.vector
        def _(dve):
            chain = Chain(dve, ln_chain, 0)
            chain.start(0)
            link = chain.link
            even, odd = STATS[:, :, 1], STATS[:, :, 4]
            dve.tensor_tensor(half[:, :], even, odd, ALU.subtract)
            dve.tensor_tensor(var[:, :], STATS[:, :, 2], STATS[:, :, 5], ALU.add)
            link(dve.tensor_tensor(MEAN[:, :], even, odd, ALU.add))
            link(dve.tensor_scalar(MEAN[:, :], MEAN[:, :], 0.5, None, ALU.mult))
            link(dve.tensor_scalar(half[:, :], half[:, :], 0.5, None, ALU.mult))
            link(dve.tensor_tensor(half[:, :], half[:, :], half[:, :], ALU.mult))
            link(dve.scalar_tensor_tensor(var0[:, :], var[:, :], 1.0 / D, half[:, :], ALU.mult, ALU.add))
            link(dve.tensor_scalar(var[:, :], var0[:, :], LN_EPS, None, ALU.add))
            if twice:
                link(dve.tensor_scalar(var[:, :], var[:, :], LN_EPS, None, ALU.mult))
                link(dve.tensor_tensor(var[:, :], var[:, :], var0[:, :], ALU.add))
            dve.wait_ge(std_ready, 1)
            link(dve.reciprocal(R[:, :], var[:, :]))
            if SHIFT is not None:
                dve.scalar_tensor_tensor(SHIFT[:, :], MEAN[:, :], -1.0, R[:, :], ALU.mult, ALU.mult)

        @block.scalar
        def _(act):
            act.wait_ge(ln_chain, links)
            nc.scalar.activation(var[:, :], var[:, :], ACT.Sqrt).then_inc(std_ready, 1)


def dense_gcn(nc, g_in, X, STATS, SHIFT, R, ident, banks, adj):
    with ExitStack() as stack:
        sc = Scope(nc, stack, "G")
        wt = sc.sb("wt", [P, D])
        bias = sc.sb("bias", [P, D])
        mask = sc.sb("mask", [P, T])
        deg = sc.sb("deg", [P, T])
        dis = sc.sb("dis", [P, T])
        dism = sc.sb("dism", [P, T])
        lnb = [sc.sb(f"lnb{u}", [P, GT, D]) for u in range(2)]
        lnT = [sc.sb(f"lnT{u}", [P, GT, P]) for u in range(2)]
        adjT = [sc.sb(f"adjT{u}", [P, GT, P]) for u in range(2)]
        dh = [sc.sb(f"dh{u}", [P, GT, D]) for u in range(2)]
        agg = [sc.sb(f"agg{u}", [P, GT, D]) for u in range(2)]
        loaded, setup_done, deg_sem = sc.sem("loaded"), sc.sem("setup"), sc.sem("deg")
        zeroed, adjT_in = sc.sem("zeroed"), sc.sems("adjT_in")
        ln_ready, turned, lnT_ready = sc.sem("ln_ready"), sc.sem("turned"), sc.sem("lnT_ready")
        lin_done, dh_ready, agg_done = sc.sem("lin_done"), sc.sem("dh_ready"), sc.sem("agg_done")
        x_done, lin_chain, out_chain = sc.sem("x_done"), sc.sem("lin_chain"), sc.sem("out_chain")
        agg_read, carried = sc.sem("agg_read"), sc.sem("carried")
        pT, pL, pA = banks[0], banks[1:3], banks[3:5]
        block = stack.enter_context(nc.Block())

        @block.sync
        def _(sp):
            sp.dma_start(wt[:, :], g_in["L3_gnn_W"]).then_inc(loaded, 16)
            sp.dma_start(bias[:, :], bcast(g_in["L3_gnn_b"], [P, D])).then_inc(loaded, 16)
            sp.dma_start(mask[:, :], g_in["nodemask"]).then_inc(loaded, 16)
            sp.wait_ge(zeroed, 2)

            def load_adjT(g, u):
                if has(g, 2):
                    sp.wait_ge(agg_done, g - 1)
                for b in range(2):
                    h = slice(b * NODES, (b + 1) * NODES)
                    src = g_in["adjT"][bass.ds(g * GT * P, GT * P), :].rearrange("(t p) j -> p t j", p=P)
                    sp.dma_start(adjT[u][h, :, h], src[h, :, :]).then_inc(adjT_in[u], 16)

            software_pipeline(sp, [load_adjT] + [None] * 5, NG)

        @block.gpsimd
        def _(pool):
            for u in range(2):
                nc.gpsimd.memset(adjT[u][:, :, :], 0.0).then_inc(zeroed, 1)

        @block.scalar
        def _(act):
            act.wait_ge(deg_sem, 3)
            nc.scalar.activation(deg[:, :], deg[:, :], ACT.Sqrt).then_inc(deg_sem, 1)

            def normalise(g, u):
                if has(g, 2):
                    act.wait_ge(turned, g - 1)
                act_normalise_group(nc, lnb[u], X, SHIFT, R, g).then_inc(ln_ready, 1)

            def turn(g, u):
                act.wait_ge(turned, g + 1)
                if has(g, 2):
                    act.wait_ge(lin_done, g - 1)
                nc.scalar.activation(lnT[u][:, :, :], pT[:, :].rearrange("p (t d) -> p t d", t=GT),
                                     ACT.Copy).then_inc(lnT_ready, 1)

            software_pipeline(act, [normalise, turn] + [None] * 4, NG)

        @block.tensor
        def _(pe):
            def turn(g, u):
                pe.wait_ge(ln_ready, g + 1)
                if has(g, 1):
                    pe.wait_ge(lnT_ready, g)
                for j in range(GT):
                    last = nc.tensor.transpose(pT[:, j * P:(j + 1) * P], lnb[u][:, j, :], ident[:, :])
                last.then_inc(turned, 1)

            def linear(g, u):
                pe.wait_ge(lnT_ready, g + 1)
                if has(g, 2):
                    pe.wait_ge(dh_ready, g - 1)
                for j in range(GT):
                    last = nc.tensor.matmul(pL[u][:, j * D:(j + 1) * D], lnT[u][:, j, :], wt[:, :], start=True, stop=True)
                last.then_inc(lin_done, 1)

            def aggregate(g, u):
                pe.wait_ge(dh_ready, g + 1)
                pe.wait_ge(adjT_in[u], g * 16 + (32 - 16 * u))
                if has(g, 2):
                    pe.wait_ge(agg_read, g - 1)
                for j in range(GT):
                    last = nc.tensor.matmul(pA[u][:, j * D:(j + 1) * D], adjT[u][:, j, :], dh[u][:, j, :],
                                            start=True, stop=True)
                last.then_inc(agg_done, 1)

            pe.wait_ge(loaded, 48)
            software_pipeline(pe, [None, turn, linear, None, aggregate, None], NG)

        @block.vector
        def _(dve):
            dve.wait_ge(loaded, 48)
            dve.tensor_reduce(deg[:, :], adj[:, :, :], AX.X, ALU.add).then_inc(deg_sem, 1)
            dve.wait_ge(deg_sem, 1)
            dve.tensor_scalar(deg[:, :], deg[:, :], 1.0, None, ALU.add).then_inc(deg_sem, 1)
            dve.wait_ge(deg_sem, 2)
            dve.tensor_scalar(deg[:, :], deg[:, :], 1e-8, None, ALU.add).then_inc(deg_sem, 1)
            dve.wait_ge(deg_sem, 4)
            dve.reciprocal(dis[:, :], deg[:, :]).then_inc(setup_done, 1)
            dve.wait_ge(setup_done, 1)
            dve.tensor_tensor(dism[:, :], dis[:, :], mask[:, :], ALU.mult).then_inc(setup_done, 1)
            dve.wait_ge(setup_done, 2)

            def scale_linear(g, u):
                dve.wait_ge(lin_done, g + 1)
                if has(g, 2):
                    dve.wait_ge(agg_done, g - 1)
                dve.tensor_tensor(dh[u][:, :, :], pL[u][:, :].rearrange("p (t d) -> p t d", t=GT),
                                  bcast(bias[:, :].unsqueeze(1), [P, GT, D]), ALU.add).then_inc(lin_chain, 1)
                dve.wait_ge(lin_chain, g + 1)
                dve.tensor_tensor(dh[u][:, :, :], dh[u][:, :, :],
                                  bcast(dis[:, bass.ds(g * GT, GT)].unsqueeze(2), [P, GT, D]),
                                  ALU.mult).then_inc(dh_ready, 1)

            def finish(g, u):
                dve.wait_ge(agg_done, g + 1)
                dve.wait_ge(dh_ready, g + 1)
                dve.tensor_tensor(agg[u][:, :, :], pA[u][:, :].rearrange("p (t d) -> p t d", t=GT), dh[u][:, :, :],
                                  ALU.add).then_inc(agg_read, 1)
                dve.wait_ge(agg_read, g + 1)
                dve.tensor_tensor(agg[u][:, :, :], agg[u][:, :, :],
                                  bcast(dism[:, bass.ds(g * GT, GT)].unsqueeze(2), [P, GT, D]),
                                  ALU.mult).then_inc(out_chain, 1)
                dve.wait_ge(out_chain, g + 1)
                dve.scalar_tensor_tensor(group(X, g), agg[u][:, :, :], 0.0, group(X, g), ALU.max,
                                         ALU.add).then_inc(x_done, 1)
                group_stats(dve, STATS, X, g, x_done, carried)

            software_pipeline(dve, [None, None, None, scale_linear, None, finish], NG)


HEADS = 8
HD = D // HEADS
PAIRS = HEADS // 2
VW = HD + 1


def graph_attention(nc, g_in, X, STATS, MEAN, R, ident, banks, out_bias, raw_adj, adj_in, adj, wq, wk, wv, wo, head_of):
    with ExitStack() as stack:
        sc = Scope(nc, stack, "A")
        lnb = [sc.sb(f"lnb{u}", [P, D]) for u in range(2)]
        lnT = [sc.sb(f"lnT{u}", [P, 2, 2, NODES]) for u in range(4)]
        qk = [sc.sb(f"qk{u}", [P, 2, P]) for u in range(4)]
        k_wide = [sc.sb(f"k_wide{u}", [P, HEADS, P]) for u in range(2)]
        v_wide = [sc.sb(f"v_wide{u}", [P, 2, PAIRS, 2, VW]) for u in range(4)]
        top = [sc.sb(f"top{u}", [P, HEADS]) for u in range(2)]
        s = [sc.sb(f"s{u}", [P, HEADS, NODES]) for u in range(4)]
        pT = [sc.sb(f"pT{u}", [P, PAIRS, P]) for u in range(2)]
        inv = [sc.sb(f"inv{u}", [P, HEADS]) for u in range(2)]
        o = [sc.sb(f"o{u}", [P, D]) for u in range(2)]
        oT = [sc.sb(f"oT{u}", [P, P]) for u in range(2)]
        (adj_ready, zeroed, v_preset, ln_ready, turned, lnT_ready, qk_done, v_done, qk_ready, k_ready, v_ready,
         scores_done, top_ready, shifted, exp_done, p_ready, p_turned, pT_ready, av_done, inv_ready, o_ready, o_turned,
         oT_ready, proj_done, x_done) = (sc.sem(n) for n in (
             "adj_ready", "zeroed", "v_preset", "ln_ready", "turned", "lnT_ready", "qk_done", "v_done",
             "qk_ready", "k_ready", "v_ready", "scores_done", "top_ready", "shifted", "exp_done", "p_ready",
             "p_turned", "pT_ready", "av_done", "inv_ready", "o_ready", "o_turned", "oT_ready", "proj_done", "x_done"))
        carried, biased = sc.sem("carried"), sc.sem("biased")
        bX, bQK, bV, bS, bP, bO, bOT, bY = banks
        block = stack.enter_context(nc.Block())

        @block.tensor
        def _(pe):
            def turn(t, w):
                pe.wait_ge(ln_ready, t + 1)
                if has(t, 1):
                    pe.wait_ge(lnT_ready, t)
                nc.tensor.transpose(bX[:, 0:P], lnb[w % 2][:, :], ident[:, :]).then_inc(turned, 1)

            def project(t, w):
                pe.wait_ge(lnT_ready, t + 1)
                if has(t, 1):
                    pe.wait_ge(qk_ready, t)
                nc.tensor.matmul(bQK[:, 0:P], wq[:, :], lnT[w][:, :, 0, :], start=True, stop=True)
                nc.tensor.matmul(bQK[:, P:2 * P], wk[:, :], lnT[w][:, :, 0, :], start=True, stop=True).then_inc(qk_done, 1)

            def project_v(t, w):
                if has(t, 1):
                    pe.wait_ge(v_ready, t)
                for b in range(2):
                    last = nc.tensor.matmul(bV[:, b * D:(b + 1) * D], lnT[w][:, b, :, :].rearrange("p a k -> p (a k)"),
                                            wv[:, :], start=True, stop=True)
                last.then_inc(v_done, 1)

            def scores(t, w):
                pe.wait_ge(qk_ready, t + 1)
                pe.wait_ge(k_ready, t + 1)
                if has(t, 1):
                    pe.wait_ge(shifted, t)
                for b in range(2):
                    h = slice(b * NODES, (b + 1) * NODES)
                    last = nc.tensor.matmul(bS[h, :], qk[w][:, 0, h], k_wide[w % 2][:, :, h], start=True, stop=True)
                last.then_inc(scores_done, 1)

            def turn_p(t, w):
                pe.wait_ge(p_ready, t + 1)
                if has(t, 1):
                    pe.wait_ge(pT_ready, t)
                for c in range(PAIRS):
                    last = nc.tensor.transpose(bP[:, c * P:(c + 1) * P],
                                               s[w][:, 2 * c:2 * c + 2, :].rearrange("p h k -> p (h k)"), ident[:, :])
                last.then_inc(p_turned, 1)

            def values(t, w):
                pe.wait_ge(pT_ready, t + 1)
                pe.wait_ge(v_ready, t + 1)
                if has(t, 1):
                    pe.wait_ge(o_ready, t)
                for b in range(2):
                    h = slice(b * NODES, (b + 1) * NODES)
                    for c in range(PAIRS):
                        last = nc.tensor.matmul(bO[h, c * 2 * VW:(c + 1) * 2 * VW], pT[w % 2][:, c, h],
                                                v_wide[w][:, b, c, :, :].rearrange("p s d -> p (s d)"),
                                                start=True, stop=True)
                last.then_inc(av_done, 1)

            def turn_o(t, w):
                pe.wait_ge(o_ready, t + 1)
                if has(t, 1):
                    pe.wait_ge(oT_ready, t)
                nc.tensor.transpose(bOT[:, 0:P], o[w % 2][:, :], ident[:, :]).then_inc(o_turned, 1)

            def project_out(t, w):
                pe.wait_ge(oT_ready, t + 1)
                if has(t, 1):
                    pe.wait_ge(x_done, t)
                nc.tensor.matmul(bY[:, 0:D], oT[w % 2][:, :], wo[:, :], start=True, stop=True).then_inc(proj_done, 1)

            software_pipeline(pe, [None, turn, project, None, scores, project_v, None, turn_p, values, turn_o,
                                   project_out], T, 4)

        @block.scalar
        def _(act):
            def turn(t, w):
                act.wait_ge(turned, t + 1)
                if has(t, 4):
                    act.wait_ge(v_done, t - 3)
                src = bX[:, 0:P].rearrange("p (b k) -> p b k", b=2).unsqueeze(2)
                nc.scalar.activation(lnT[w][:, :, :, :], bcast(src, [P, 2, 2, NODES]), ACT.Copy).then_inc(lnT_ready, 1)

            def project(t, w):
                act.wait_ge(qk_done, t + 1)
                if has(t, 4):
                    act.wait_ge(scores_done, t - 3)
                    act.wait_ge(k_ready, t - 3)
                nc.scalar.activation(qk[w][:, :, :], bQK[:, 0:2 * P].rearrange("p (a q) -> p a q", a=2),
                                     ACT.Copy).then_inc(qk_ready, 1)

            def exponentials(t, w):
                act.wait_ge(shifted, t + 1)
                nc.scalar.activation(s[w][:, :, :], s[w][:, :, :], ACT.Exp,
                                     scale=HD ** -0.5).then_inc(exp_done, 1)

            def turn_p(t, w):
                act.wait_ge(p_turned, t + 1)
                if has(t, 2):
                    act.wait_ge(av_done, t - 1)
                nc.scalar.activation(pT[w % 2][:, :, :], bP[:, :].rearrange("p (c q) -> p c q", c=PAIRS),
                                     ACT.Copy).then_inc(pT_ready, 1)

            def turn_o(t, w):
                act.wait_ge(o_turned, t + 1)
                if has(t, 2):
                    act.wait_ge(proj_done, t - 1)
                nc.scalar.activation(oT[w % 2][:, :], bOT[:, 0:P], ACT.Copy).then_inc(oT_ready, 1)

            software_pipeline(act, [None, turn, project, None, None, exponentials, None, turn_p, None, turn_o, None],
                              T, 4)

        @block.gpsimd
        def _(pool):
            for u in range(4):
                nc.gpsimd.memset(v_wide[u][:, :, :, :, :], 0.0).then_inc(zeroed, 1)
            pool.wait_ge(zeroed, 4)
            for u in range(4):
                for s2 in range(2):
                    h = slice(s2 * NODES, (s2 + 1) * NODES)
                    ones = v_wide[u][h, :, :, s2, HD:VW].rearrange("p b c d -> p (b c) d")
                    nc.gpsimd.memset(ones, 1.0).then_inc(v_preset, 1)
            pool.wait_ge(v_preset, 8)
            pool.wait_ge(adj_ready, 1)

            def widen_k(t, w):
                pool.wait_ge(qk_ready, t + 1)
                if has(t, 2):
                    pool.wait_ge(scores_done, t - 1)
                nc.gpsimd.tensor_tensor(k_wide[w % 2][:, :, :], bcast(qk[w][:, 1:2, :], [P, HEADS, P]),
                                        bcast(head_of[:, :].unsqueeze(2), [P, HEADS, P]), ALU.mult).then_inc(k_ready, 1)

            def weigh(t, w):
                pool.wait_ge(exp_done, t + 1)
                nc.gpsimd.tensor_tensor(s[w][:, :, :], s[w][:, :, :],
                                        bcast(adj[:, bass.ds(t, 1), :], [P, HEADS, NODES]), ALU.mult).then_inc(p_ready, 1)

            def add_bias(t, w):
                pool.wait_ge(ln_ready, t + 1)
                nc.gpsimd.tensor_tensor(tile_of(X, t), tile_of(X, t), out_bias[:, :], ALU.add).then_inc(biased, 1)

            software_pipeline(pool, [None, add_bias, None, widen_k, None, None, weigh, None, None, None, None], T, 4)

        @block.vector
        def _(dve):
            dve.wait_ge(v_preset, 8)
            dve.wait_ge(adj_in, 16)
            dve.tensor_scalar(adj[:, :, :], raw_adj[:, :, :], 1e-6, None, ALU.add).then_inc(adj_ready, 1)

            def normalise(t, w):
                if has(t, 2):
                    dve.wait_ge(turned, t - 1)
                normalise_tile(dve, lnb[w % 2][:, :], X, MEAN, R, t).then_inc(ln_ready, 1)

            def widen_v(t, w):
                dve.wait_ge(v_done, t + 1)
                if has(t, 4):
                    dve.wait_ge(av_done, t - 3)
                for s2 in range(2):
                    h = slice(s2 * NODES, (s2 + 1) * NODES)
                    src = bV[h, 0:2 * D].rearrange("p (c s d) -> p c s d", s=2, d=HD)[:, :, s2, :]
                    last = dve.tensor_copy(v_wide[w][h, :, :, s2, 0:HD].rearrange("p b c d -> p (b c) d"), src)
                last.then_inc(v_ready, 1)

            def shift(t, w):
                dve.wait_ge(scores_done, t + 1)
                src = bS[:, :].rearrange("p (h k) -> p h k", h=HEADS)
                dve.tensor_reduce(top[w % 2][:, :], src, AX.X, ALU.max).then_inc(top_ready, 1)
                dve.wait_ge(top_ready, t + 1)
                if has(t, 4):
                    dve.wait_ge(p_turned, t - 3)
                dve.tensor_tensor(s[w][:, :, :], src, bcast(top[w % 2][:, :].unsqueeze(2), [P, HEADS, NODES]),
                                  ALU.subtract).then_inc(shifted, 1)

            def divide(t, w):
                dve.wait_ge(av_done, t + 1)
                src = bO[:, 0:HEADS * VW].rearrange("p (h d) -> p h d", h=HEADS)
                dve.reciprocal(inv[w % 2][:, :].unsqueeze(2), src[:, :, HD:VW]).then_inc(inv_ready, 1)
                dve.wait_ge(inv_ready, t + 1)
                if has(t, 2):
                    dve.wait_ge(o_turned, t - 1)
                dve.tensor_tensor(o[w % 2][:, :].rearrange("p (h d) -> p h d", h=HEADS), src[:, :, 0:HD],
                                  bcast(inv[w % 2][:, :].unsqueeze(2), [P, HEADS, HD]), ALU.mult).then_inc(o_ready, 1)

            def add(t, w):
                dve.wait_ge(proj_done, t + 1)
                dve.wait_ge(biased, t + 1)
                dve.tensor_tensor(tile_of(X, t), bY[:, 0:D], tile_of(X, t), ALU.add).then_inc(x_done, 1)
                dve.wait_ge(x_done, t + 1)
                dve.sem_inc(carried, 1)
                tile_stats(dve, STATS, X, t)

            software_pipeline(dve, [normalise, None, None, None, shift, widen_v, None, None, divide, None, add], T, 4)


GROUPS = [list(range(25)), [0, 1, 2, 3, 4, 5, 6, 7, 8], [0, 9, 10, 11, 12, 13, 14], [6, 7, 8, 12, 13, 14],
          [3, 4, 5, 9, 10, 11]]
SLOT0 = [sum(len(n) for n in GROUPS[:g]) for g in range(len(GROUPS))]
SLOTS = sum(len(n) for n in GROUPS)
MID = 256


def load_gcn_weights(nc, sc, g_in):
    NGR = len(GROUPS)
    adj = sc.sb("adj", [P, T, NODES])
    w1 = sc.sb("w1", [P, NGR, MID])
    w2 = sc.sb("w2", [P, NGR, 2, D])
    b1 = sc.sb("b1", [P, NGR, 2])
    b2 = sc.sb("b2", [P, D])
    fusion = sc.sb("fusion", [P, NGR])
    slot_group = sc.sb("slot_group", [P, NGR])
    pick = sc.sb("pick", [P, P])
    spread = sc.sb("spread", [P, P])
    loaded = sc.sem("loaded")
    with nc.Block() as block:
        @block.sync
        def _(sp):
            for buf, src in ((adj[:, :, :], g_in["slot_adj"].rearrange("(t p) j -> p t j", p=P)),
                             (w1[:, :, :], g_in["L1_gnn_W1"].rearrange("g d f -> d g f")),
                             (w2[:, :, :, :], g_in["L1_gnn_W2"].rearrange("g (c f) d -> f g c d", f=P)),
                             (b1[:, :, :], g_in["L1_gnn_b1"]), (b2[:, :], g_in["L1_gnn_b2"]),
                             (fusion[:, :], bcast(g_in["L1_gnn_fusion_w"], [P, NGR])),
                             (slot_group[:, :], g_in["c_slot_group"]),
                             (pick[:, :], g_in["c_pick"]), (spread[:, :], g_in["c_spread"])):
                sp.dma_start(buf, src).then_inc(loaded, 16)
    return adj, w1, w2, b1, b2, fusion, slot_group, pick, spread, loaded


def group_gcns(nc, g_in, X, STATS, SHIFT, R, ident, banks, weights, combine_next):
    with ExitStack() as stack:
        sc = Scope(nc, stack, "C")
        adj, w1, w2, b1, b2, fusion, slot_group, pick, spread, loaded = weights
        fmax, fsum, finv, slot_w = (sc.sb(n, [P, 1]) for n in ("fmax", "fsum", "finv", "slot_w"))
        deg, zero, dinv = (sc.sb(n, [P, T]) for n in ("deg", "zero", "dinv"))
        ring = lambda name, shape: [sc.sb(f"{name}{u}", shape) for u in range(2)]
        lnb, xs, z, ys, f = (ring(n, [P, GT, D]) for n in ("lnb", "xs", "z", "ys", "f"))
        adj1, adj2 = ring("adj1", [P, GT, P]), ring("adj2", [P, GT, P])
        zT, sT = ring("zT", [P, 2 * GT, NODES]), ring("sT", [P, 2 * GT, NODES])
        hT = ring("hT", [P, 2, 2 * GT, NODES])
        (zeroed, chain_sem, exp_done, sqrt_done, ln_ready, picked, xs_ready, conv1_done, z_sum, z_scaled, z_turned,
         zT_ready, up_done, hT_ready, down_done, sT_ready, s_turned, ys_ready, conv2_done, bank7_read, spread_done,
         x_done, f_chain, f_ready) = (sc.sem(n) for n in (
             "zeroed", "chain", "exp_done", "sqrt_done", "ln_ready", "picked", "xs_ready", "conv1_done",
             "z_sum", "z_scaled", "z_turned", "zT_ready", "up_done", "hT_ready", "down_done", "sT_ready", "s_turned",
             "ys_ready", "conv2_done", "bank7_read", "spread_done", "x_done", "f_chain", "f_ready"))
        adj1_in, adj2_in = sc.sems("adj1_in"), sc.sems("adj2_in")
        carried = sc.sem("carried")
        bPick, bA1, bZT, bH0, bH1, bS, bST, bA2 = banks
        bSpread = bS
        DOWN_STEP, SPREAD_STEP = 5, 8
        BEHIND = SPREAD_STEP - DOWN_STEP
        cols = lambda bank: bank[:, :].rearrange("p (a s) -> p a s", s=NODES)
        tiles = lambda bank: bank[:, :].rearrange("p (t d) -> p t d", t=GT)
        block = stack.enter_context(nc.Block())

        @block.sync
        def _(sp):
            sp.wait_ge(zeroed, 6)

            def load(dst, arrived, readers):
                def run(g, u):
                    if has(g, 2):
                        sp.wait_ge(readers, g - 1)
                    src = g_in["slot_adjT"][bass.ds(g * GT * P, GT * P), :].rearrange("(t p) j -> p t j", p=P)
                    for b in range(2):
                        h = slice(b * NODES, (b + 1) * NODES)
                        sp.dma_start(dst[u][h, :, h], src[h, :, :]).then_inc(arrived[u], 16)
                return run

            software_pipeline(sp, [None, load(adj1, adj1_in, conv1_done), None, None, None, None,
                                   load(adj2, adj2_in, conv2_done), None, None], NG)

        @block.gpsimd
        def _(pool):
            for buf in adj1 + adj2 + sT:
                nc.gpsimd.memset(buf[:, :, :], 0.0).then_inc(zeroed, 1)
            if combine_next is not None:
                combine_next(pool)

        @block.tensor
        def _(pe):
            def pick_slots(g, u):
                pe.wait_ge(ln_ready, g + 1)
                if has(g, 1):
                    pe.wait_ge(xs_ready, g)
                nc.tensor.matmul(bPick[:, :], pick[:, :], lnb[u][:, :, :].rearrange("p t d -> p (t d)"),
                                 start=True, stop=True).then_inc(picked, 1)

            def conv1(g, u):
                pe.wait_ge(xs_ready, g + 1)
                pe.wait_ge(adj1_in[u], g * 16 + (32 - 16 * u))
                if has(g, 1):
                    pe.wait_ge(z_sum, g)
                for j in range(GT):
                    last = nc.tensor.matmul(bA1[:, j * D:(j + 1) * D], adj1[u][:, j, :], xs[u][:, j, :],
                                            start=True, stop=True)
                last.then_inc(conv1_done, 1)

            def turn_z(g, u):
                pe.wait_ge(z_scaled, g + 1)
                if has(g, 1):
                    pe.wait_ge(zT_ready, g)
                for j in range(GT):
                    last = nc.tensor.transpose(bZT[:, j * P:(j + 1) * P], z[u][:, j, :], ident[:, :])
                last.then_inc(z_turned, 1)

            def up(g, u):
                pe.wait_ge(zT_ready, g + 1)
                if has(g, 1):
                    pe.wait_ge(hT_ready, g)
                for c, bank in enumerate((bH0, bH1)):
                    for i, nodes in enumerate(GROUPS):
                        sl = slice(SLOT0[i], SLOT0[i] + len(nodes))
                        last = nc.tensor.matmul(cols(bank)[:, :, sl], w1[:, i, c * P:(c + 1) * P], zT[u][:, :, sl],
                                                start=True, stop=True)
                last.then_inc(up_done, 1)

            def down(g, u):
                pe.wait_ge(hT_ready, g + 1)
                if has(g, 1):
                    pe.wait_ge(sT_ready, g)
                if has(g, BEHIND):
                    pe.wait_ge(x_done, g - (BEHIND - 1))
                for i, nodes in enumerate(GROUPS):
                    sl = slice(SLOT0[i], SLOT0[i] + len(nodes))
                    for c in range(2):
                        last = nc.tensor.matmul(cols(bS)[:, :, sl], w2[:, i, c, :], hT[u][:, c, :, sl],
                                                start=(c == 0), stop=(c == 1))
                last.then_inc(down_done, 1)

            def turn_s(g, u):
                pe.wait_ge(sT_ready, g + 1)
                if has(g, 1):
                    pe.wait_ge(ys_ready, g)
                for j in range(GT):
                    last = nc.tensor.transpose(bST[:, j * P:(j + 1) * P],
                                               sT[u][:, 2 * j:2 * j + 2, :].rearrange("p b s -> p (b s)"), ident[:, :])
                last.then_inc(s_turned, 1)

            def conv2(g, u):
                pe.wait_ge(ys_ready, g + 1)
                pe.wait_ge(adj2_in[u], g * 16 + (32 - 16 * u))
                if has(g, 1):
                    pe.wait_ge(bank7_read, g)
                for j in range(GT):
                    last = nc.tensor.matmul(bA2[:, j * D:(j + 1) * D], adj2[u][:, j, :], ys[u][:, j, :],
                                            start=True, stop=True)
                last.then_inc(conv2_done, 1)

            def spread_slots(g, u):
                pe.wait_ge(f_ready, g + 1)
                n = g + BEHIND
                pe.wait_ge(sT_ready, min(n, NG) if isinstance(n, int) else n)
                if has(g, 1):
                    pe.wait_ge(x_done, g)
                nc.tensor.matmul(bSpread[:, :], spread[:, :], f[u][:, :, :].rearrange("p t d -> p (t d)"),
                                 start=True, stop=True).then_inc(spread_done, 1)

            pe.wait_ge(loaded, 144)
            software_pipeline(pe, [None, pick_slots, conv1, turn_z, up, down, turn_s, conv2, spread_slots], NG)

        @block.scalar
        def _(act):
            act.wait_ge(chain_sem, 2)
            nc.scalar.activation(fusion[:, :], fusion[:, :], ACT.Exp).then_inc(exp_done, 1)
            act.wait_ge(chain_sem, 12)
            nc.scalar.activation(deg[:, :], deg[:, :], ACT.Sqrt).then_inc(sqrt_done, 1)

            def normalise(g, u):
                if has(g, 2):
                    act.wait_ge(picked, g - 1)
                act_normalise_group(nc, lnb[u], X, SHIFT, R, g).then_inc(ln_ready, 1)

            def turn_z(g, u):
                act.wait_ge(z_turned, g + 1)
                if has(g, 2):
                    act.wait_ge(up_done, g - 1)
                nc.scalar.activation(zT[u][:, :, :], cols(bZT), ACT.Copy).then_inc(zT_ready, 1)

            def up(g, u):
                act.wait_ge(up_done, g + 1)
                if has(g, 2):
                    act.wait_ge(down_done, g - 1)
                for c, bank in enumerate((bH0, bH1)):
                    for i, nodes in enumerate(GROUPS):
                        sl = slice(SLOT0[i], SLOT0[i] + len(nodes))
                        last = nc.scalar.activation(hT[u][:, c, :, sl], cols(bank)[:, :, sl], ACT.Relu,
                                                    bias=b1[:, i, c:c + 1])
                last.then_inc(hT_ready, 1)

            def down(g, u):
                act.wait_ge(down_done, g + 1)
                if has(g, 2):
                    act.wait_ge(s_turned, g - 1)
                nc.scalar.activation(sT[u][:, :, 0:SLOTS], cols(bS)[:, :, 0:SLOTS], ACT.Copy).then_inc(sT_ready, 1)

            software_pipeline(act, [normalise, None, None, turn_z, up, down, None, None, None], NG)

        @block.vector
        def _(dve):
            chain = Chain(dve, chain_sem, 0)
            chain.start(0)
            link = chain.link
            dve.wait_ge(loaded, 144)
            link(dve.tensor_reduce(fmax[:, :], fusion[:, :], AX.X, ALU.max))
            link(dve.tensor_scalar(fusion[:, :], fusion[:, :], fmax[:, :], None, ALU.subtract))
            dve.wait_ge(exp_done, 1)
            link(dve.tensor_reduce(fsum[:, :], fusion[:, :], AX.X, ALU.add))
            link(dve.reciprocal(finv[:, :], fsum[:, :]))
            link(dve.tensor_tensor(fusion[:, :], fusion[:, :], slot_group[:, :], ALU.mult))
            link(dve.tensor_reduce(slot_w[:, :], fusion[:, :], AX.X, ALU.add))
            link(dve.tensor_tensor(slot_w[:, :], slot_w[:, :], finv[:, :], ALU.mult))
            link(dve.tensor_reduce(deg[:, :], adj[:, :, :], AX.X, ALU.add))
            link(dve.tensor_scalar(deg[:, :], deg[:, :], 1.0, None, ALU.add))
            link(dve.tensor_scalar(zero[:, :], deg[:, :], 0.0, None, ALU.is_equal))
            link(dve.tensor_tensor(deg[:, :], deg[:, :], zero[:, :], ALU.add))
            link(dve.tensor_scalar(zero[:, :], zero[:, :], -1.0, 1.0, ALU.mult, ALU.add))
            dve.wait_ge(sqrt_done, 1)
            link(dve.reciprocal(dinv[:, :], deg[:, :]))
            link(dve.tensor_tensor(dinv[:, :], dinv[:, :], zero[:, :], ALU.mult))

            def dinv_of(g):
                return bcast(dinv[:, bass.ds(g * GT, GT)].unsqueeze(2), [P, GT, D])

            def pick_slots(g, u):
                dve.wait_ge(picked, g + 1)
                if has(g, 2):
                    dve.wait_ge(conv1_done, g - 1)
                    dve.wait_ge(z_sum, g - 1)
                dve.tensor_tensor(xs[u][:, :, :], tiles(bPick), dinv_of(g), ALU.mult).then_inc(xs_ready, 1)

            def conv1(g, u):
                dve.wait_ge(conv1_done, g + 1)
                if has(g, 2):
                    dve.wait_ge(z_turned, g - 1)
                dve.tensor_tensor(z[u][:, :, :], tiles(bA1), xs[u][:, :, :], ALU.add).then_inc(z_sum, 1)
                dve.wait_ge(z_sum, g + 1)
                dve.tensor_tensor(z[u][:, :, :], z[u][:, :, :], dinv_of(g), ALU.mult).then_inc(z_scaled, 1)

            def turn_s(g, u):
                dve.wait_ge(s_turned, g + 1)
                if has(g, 2):
                    dve.wait_ge(conv2_done, g - 1)
                dve.tensor_tensor(ys[u][:, :, :], tiles(bST), dinv_of(g), ALU.mult).then_inc(ys_ready, 1)

            def conv2(g, u):
                dve.wait_ge(conv2_done, g + 1)
                if has(g, 2):
                    dve.wait_ge(spread_done, g - 1)
                dve.tensor_tensor(f[u][:, :, :], tiles(bA2), ys[u][:, :, :], ALU.add).then_inc(bank7_read, 1)
                dve.wait_ge(bank7_read, g + 1)
                dve.tensor_tensor(f[u][:, :, :], f[u][:, :, :], dinv_of(g), ALU.mult).then_inc(f_chain, 1)
                dve.wait_ge(f_chain, g * 2 + 1)
                dve.tensor_tensor(f[u][:, :, :], f[u][:, :, :], bcast(b2[:, :].unsqueeze(1), [P, GT, D]),
                                  ALU.add).then_inc(f_chain, 1)
                dve.wait_ge(f_chain, g * 2 + 2)
                dve.tensor_scalar(f[u][:, :, :], f[u][:, :, :], 0.0, slot_w[:, :], ALU.max, ALU.mult).then_inc(f_ready, 1)

            def add(g, u):
                dve.wait_ge(spread_done, g + 1)
                dve.tensor_tensor(group(X, g), tiles(bSpread), group(X, g), ALU.add).then_inc(x_done, 1)
                group_stats(dve, STATS, X, g, x_done, carried)

            software_pipeline(dve, [None, pick_slots, conv1, None, None, None, turn_s, conv2, add], NG)


ROUTES = 16
LAYERS = 2
D_WAYS = 4
FIRST, SECOND = 3, 5
D_TURNS = (T + 7 - 1) // D_WAYS + 1


W_CUTS = 4


class RoutedWeights:

    def __init__(self, sc, g_in):
        self.g_in = g_in
        self.w = sc.sb("w", [P, LAYERS, ROUTES, 2, MID])
        self.ws = sc.sb("ws", [P, LAYERS, 2, MID])
        self.eye2 = sc.sb("eye2", [P, 2, MID])
        self.shared_in, self.w_in = sc.sem("shared_in"), sc.sems("w_in")
        self.shared_ready, self.combined = sc.sem("shared_ready"), sc.sem("combined")

    def combine(self, pool):
        w, ws, eye2 = self.w, self.ws, self.eye2
        n = ROUTES // W_CUTS
        pieces = [(layer, c) for layer in range(LAYERS) for c in range(W_CUTS)]

        def load(i):
            layer, c = pieces[i]
            pool.dma_start(w[:, layer, c * n:(c + 1) * n, :, :],
                           self.g_in["L1_ffn_Wr"][:, layer, c * n:(c + 1) * n, :, :]).then_inc(self.w_in[i % 2], 16)

        pool.dma_start(ws[:, :, :, :], self.g_in["L1_ffn_Ws"]).then_inc(self.shared_in, 16)
        pool.dma_start(eye2[:, :, :], self.g_in["c_eye2"]).then_inc(self.shared_in, 16)
        load(0)
        pool.wait_ge(self.shared_in, 32)
        pool.tensor_tensor(ws[:, :, :, :], ws[:, :, :, :], bcast(eye2[:, :, :].unsqueeze(1), [P, LAYERS, 2, MID]),
                           ALU.add).then_inc(self.shared_ready, 1)
        pool.wait_ge(self.shared_ready, 1)
        for i, (layer, c) in enumerate(pieces):
            if i + 1 < len(pieces):
                load(i + 1)
            pool.wait_ge(self.w_in[i % 2], 16 * (i // 2 + 1))
            ww = w[:, layer, c * n:(c + 1) * n, :, :].rearrange("p e c f -> p e (c f)")
            shared = ws[:, layer, :, :].rearrange("p c f -> p (c f)").unsqueeze(1)
            pool.tensor_tensor(ww, ww, bcast(shared, [P, n, 2 * MID]), ALU.add).then_inc(self.combined, 1)


def routed_mlp(nc, g_in, X, STATS, MEAN, R, ident, banks, out_bias, w):
    with ExitStack() as stack:
        sc = Scope(nc, stack, "D")
        br = sc.sb("br", [P, LAYERS, ROUTES, MID])
        bs = sc.sb("bs", [P, LAYERS, MID])
        wi = sc.sb("wi", [P, MID])
        bi = sc.sb("bi", [P, 2])
        wo = sc.sb("wo", [P, 2, D])
        route = sc.sb("route", [1, T], I32)
        route_f = sc.sb("route_f", [1, SECOND + D_WAYS * D_TURNS])
        digits = sc.sb("digits", [1, D_WAYS])
        words = sc.sb("words", [1, 2, D_TURNS, D_WAYS])
        word_sum = sc.sb("word_sum", [1, 2, D_TURNS])
        packed = sc.sb("packed", [1, 2, D_TURNS], I32)
        ring = lambda name, shape: [sc.sb(f"{name}{u}", shape) for u in range(2)]
        lnb, lnT = ring("lnb", [P, D]), ring("lnT", [P, P])
        h0T, h1T, h2T = (ring(n, [P, 2, P]) for n in ("h0T", "h1T", "h2T"))
        h1, h2 = ring("h1", [P, MID]), ring("h2", [P, MID])
        (loaded, biases_in, chain_sem, words_ready, biases_ready, ln_ready, turned, lnT_ready, in_done, h0_ready, mm1_done,
         h1_ready, turned1, h1T_ready, mm2_done, h2_ready, turned2, h2T_ready, out_done, x_done) = (
             sc.sem(n) for n in (
                 "loaded", "biases_in", "chain", "words_ready", "biases_ready", "ln_ready", "turned", "lnT_ready", "in_done",
                 "h0_ready", "mm1_done", "h1_ready", "turned1", "h1T_ready", "mm2_done", "h2_ready", "turned2",
                 "h2T_ready", "out_done", "x_done"))
        carried, biased = sc.sem("carried"), sc.sem("biased")
        bX, b0, b1, bT1, b2, bT2, bY = banks[0:7]
        block = stack.enter_context(nc.Block())

        @block.sync
        def _(sp):
            for buf, src in ((route[:, :], g_in["L1_ffn_route_id"]), (digits[:, :], g_in["c_hex_digits"]),
                             (wi[:, :], g_in["L1_ffn_Wi"]), (bi[:, :], g_in["L1_ffn_bi"]), (wo[:, :, :], g_in["L1_ffn_Wo"])):
                sp.dma_start(buf, src).then_inc(loaded, 16)
            for buf, src in ((bs[:, :, :].rearrange("p l f -> p (l f)"), bcast(g_in["L1_ffn_bs"], [P, LAYERS * MID])),
                             (br[:, :, :, :].rearrange("p l e f -> p (l e f)"),
                              bcast(g_in["L1_ffn_br"], [P, LAYERS * ROUTES * MID]))):
                sp.dma_start(buf, src).then_inc(biases_in, 16)

        @block.gpsimd
        def _(pool):
            def add_bias(t, k):
                pool.wait_ge(ln_ready, t + 1)
                nc.gpsimd.tensor_tensor(tile_of(X, t), tile_of(X, t), out_bias[:, :], ALU.add).then_inc(biased, 1)

            software_pipeline(pool, [None, add_bias] + [None] * 6, T, D_WAYS)

        class Routes:

            def __init__(self, eng):
                self.eng = eng

            def turn(self, j):
                self.words = [self.eng.value_load(packed[:, i, bass.ds(j, 1)], min_val=0, max_val=ROUTES ** D_WAYS - 1)
                              for i in range(2)]

            def of(self, slot, phase):
                return (self.words[phase == SECOND] >> (4 * ((slot + phase) % D_WAYS))) & (ROUTES - 1)

        @block.tensor
        def _(pe):
            routes = Routes(pe)

            def turn(t, k):
                pe.wait_ge(ln_ready, t + 1)
                if has(t, 1):
                    pe.wait_ge(lnT_ready, t)
                nc.tensor.transpose(bX[:, 0:P], lnb[k % 2][:, :], ident[:, :]).then_inc(turned, 1)

            def project_in(t, k):
                pe.wait_ge(lnT_ready, t + 1)
                if has(t, 1):
                    pe.wait_ge(h0_ready, t)
                for c in range(2):
                    last = nc.tensor.matmul(b0[:, c * P:(c + 1) * P], wi[:, c * P:(c + 1) * P], lnT[k % 2][:, :],
                                            start=True, stop=True)
                last.then_inc(in_done, 1)

            def layer(n, phase, bank, src, src_ready, bank_read, done):
                def run(t, k):
                    e = routes.of(k, phase)
                    pe.wait_ge(src_ready, t + 1)
                    if has(t, 1):
                        pe.wait_ge(bank_read, t)
                    for c in range(2):
                        last = nc.tensor.matmul(bank[:, 0:MID], src[k % 2][:, c, :],
                                                w[:, n, bass.ds(e, 1), c, :].rearrange("p o f -> p (o f)"),
                                                start=(c == 0), stop=(c == 1))
                    last.then_inc(done, 1)
                return run

            def turn_h(bank, src, src_ready, bank_read, done):
                def run(t, k):
                    pe.wait_ge(src_ready, t + 1)
                    if has(t, 1):
                        pe.wait_ge(bank_read, t)
                    for c in range(2):
                        last = nc.tensor.transpose(bank[:, c * P:(c + 1) * P], src[k % 2][:, c * P:(c + 1) * P], ident[:, :])
                    last.then_inc(done, 1)
                return run

            def project_out(t, k):
                pe.wait_ge(h2T_ready, t + 1)
                if has(t, 1):
                    pe.wait_ge(x_done, t)
                for c in range(2):
                    last = nc.tensor.matmul(bY[:, 0:D], h2T[k % 2][:, c, :], wo[:, c, :], start=(c == 0), stop=(c == 1))
                last.then_inc(out_done, 1)

            pe.wait_ge(loaded, 80)
            pe.wait_ge(words_ready, 1)
            software_pipeline(pe, [None, turn, project_in, layer(0, FIRST, b1, h0T, h0_ready, h1_ready, mm1_done),
                                   turn_h(bT1, h1, h1_ready, h1T_ready, turned1),
                                   layer(1, SECOND, b2, h1T, h1T_ready, h2_ready, mm2_done),
                                   turn_h(bT2, h2, h2_ready, h2T_ready, turned2), project_out],
                              T, D_WAYS, routes.turn)

        @block.scalar
        def _(act):
            act.wait_ge(loaded, 80)

            def turn(t, k):
                act.wait_ge(turned, t + 1)
                if has(t, 2):
                    act.wait_ge(in_done, t - 1)
                nc.scalar.activation(lnT[k % 2][:, :], bX[:, 0:P], ACT.Copy).then_inc(lnT_ready, 1)

            def project_in(t, k):
                act.wait_ge(in_done, t + 1)
                if has(t, 2):
                    act.wait_ge(mm1_done, t - 1)
                for c in range(2):
                    last = nc.scalar.activation(h0T[k % 2][:, c, :], b0[:, c * P:(c + 1) * P], ACT.Relu, bias=bi[:, c:c + 1])
                last.then_inc(h0_ready, 1)

            def turn_h(bank, dst, done, readers, ready):
                def run(t, k):
                    act.wait_ge(done, t + 1)
                    if has(t, 2):
                        act.wait_ge(readers, t - 1)
                    nc.scalar.activation(dst[k % 2][:, :, :], bank[:, 0:2 * P].rearrange("p (c q) -> p c q", c=2),
                                         ACT.Relu).then_inc(ready, 1)
                return run

            software_pipeline(act, [None, turn, project_in, None, turn_h(bT1, h1T, turned1, mm2_done, h1T_ready), None,
                                    turn_h(bT2, h2T, turned2, out_done, h2T_ready), None], T, D_WAYS)

        @block.vector
        def _(dve):
            chain = Chain(dve, chain_sem, 0)
            chain.start(0)
            link = chain.link
            routes = Routes(dve)
            dve.wait_ge(loaded, 80)
            link(dve.memset(route_f[:, :], 0.0))
            link(dve.tensor_copy(route_f[:, SECOND:SECOND + T], route[:, :]))
            for i, first in enumerate((SECOND - FIRST, 0)):
                part = route_f[:, first:first + D_WAYS * D_TURNS].rearrange("p (j k) -> p j k", k=D_WAYS)
                link(dve.tensor_tensor(words[:, i, :, :], part, bcast(digits[:, :].unsqueeze(1), [1, D_TURNS, D_WAYS]),
                                       ALU.mult))
            link(dve.tensor_reduce(word_sum[:, :, :], words[:, :, :, :], AX.X, ALU.add))
            dve.tensor_copy(packed[:, :, :], word_sum[:, :, :]).then_inc(words_ready, 1)
            dve.wait_ge(words_ready, 1)

            def normalise(t, k):
                if has(t, 2):
                    dve.wait_ge(turned, t - 1)
                normalise_tile(dve, lnb[k % 2][:, :], X, MEAN, R, t).then_inc(ln_ready, 1)

            def combine_biases():
                dve.wait_ge(biases_in, 32)
                for n in range(LAYERS):
                    bb = br[:, n, :, :]
                    dve.tensor_tensor(bb, bb, bcast(bs[:, n:n + 1, :], [P, ROUTES, MID]), ALU.add).then_inc(biases_ready, 1)
                dve.wait_ge(biases_ready, LAYERS)

            def layer(n, phase, bank, dst, done, readers, ready):
                def run(t, k):
                    e = routes.of(k, phase)
                    dve.wait_ge(done, t + 1)
                    if has(t, 2):
                        dve.wait_ge(readers, t - 1)
                    if isinstance(t, int) and t == 0 and n == 0:
                        combine_biases()
                    dve.tensor_tensor(dst[k % 2][:, :], bank[:, 0:MID],
                                      br[:, n, bass.ds(e, 1), :].rearrange("p o f -> p (o f)"), ALU.add).then_inc(ready, 1)
                return run

            def add(t, k):
                dve.wait_ge(out_done, t + 1)
                dve.wait_ge(biased, t + 1)
                dve.tensor_tensor(tile_of(X, t), bY[:, 0:D], tile_of(X, t), ALU.add).then_inc(x_done, 1)
                dve.wait_ge(x_done, t + 1)
                dve.sem_inc(carried, 1)
                tile_stats(dve, STATS, X, t)

            software_pipeline(dve, [normalise, None, None, layer(0, FIRST, b1, h1, mm1_done, turned1, h1_ready), None,
                                    layer(1, SECOND, b2, h2, mm2_done, turned2, h2_ready), None, add],
                              T, D_WAYS, routes.turn)


def edge_attention(nc, g_in, X, STATS, SHIFT, R, ident, banks, adj):
    with ExitStack() as stack:
        sc = Scope(nc, stack, "E")
        SLOPE, FAR = 0.2, 9e15
        XN = sc.sb("XN", [P, T, D])
        w1, w2 = sc.sb("w1", [P, D]), sc.sb("w2", [P, D])
        w3 = sc.sb("w3", [P, 2])
        v1, v2 = sc.sb("v1", [P, P]), sc.sb("v2", [P, P])
        deg, some, rdeg = (sc.sb(n, [P, T]) for n in ("deg", "some", "rdeg"))
        ring = lambda name, shape: [sc.sb(f"{name}{u}", shape) for u in range(2)]
        lnb, lnT, pD, pT = (ring(n, [P, GT, P]) for n in ("lnb", "lnT", "pD", "pT"))
        s1, s2j, e, a = (ring(n, [P, GT, NODES]) for n in ("s1", "s2j", "e", "a"))
        mask = sc.sb("mask", [P, T, NODES])
        far = sc.sb("far", [P, T, NODES])
        s2, top, inv = (ring(n, [P, GT]) for n in ("s2", "top", "inv"))
        (loaded, zeroed, v_done, chain_sem, setup, ln_ready, kept, turned, lnT_ready, sums_done, s1_ready, s2_read,
         pre_ready, alpha_ready, e_chain, a_chain, shifted, exp_done, inv_ready, pD_ready, p_turned,
         pT_ready, edge_done, x_done) = (sc.sem(n) for n in (
             "loaded", "zeroed", "v_done", "chain", "setup", "ln_ready", "kept", "turned", "lnT_ready", "sums_done",
             "s1_ready", "s2_read", "pre_ready", "alpha_ready", "e_chain", "a_chain", "shifted",
             "exp_done", "inv_ready", "pD_ready", "p_turned", "pT_ready", "edge_done", "x_done"))
        begun, carried = sc.sem("begun"), sc.sem("carried")
        bX, b1, b2, bP, bY = banks[0:5]
        halves = [slice(0, NODES), slice(NODES, P)]
        tiles = lambda bank: bank[:, :].rearrange("p (t d) -> p t d", t=GT)
        block = stack.enter_context(nc.Block())

        @block.sync
        def _(sp):
            for buf, name in ((w1, "L2_gnn_W1"), (w2, "L2_gnn_W2"), (w3, "L2_gnn_w3")):
                sp.dma_start(buf[:, :], g_in[name]).then_inc(loaded, 16)

        @block.tensor
        def _(pe):
            pe.wait_ge(loaded, 48)
            nc.tensor.matmul(b1[:, 0:1], w1[:, :], w3[:, 0:1], start=True, stop=True)
            nc.tensor.matmul(b1[:, 1:2], w2[:, :], w3[:, 1:2], start=True, stop=True).then_inc(v_done, 1)

            def turn(g, u):
                pe.wait_ge(ln_ready, g + 1)
                if has(g, 1):
                    pe.wait_ge(lnT_ready, g)
                for j in range(GT):
                    last = nc.tensor.transpose(bX[:, j * P:(j + 1) * P], lnb[u][:, j, :], ident[:, :])
                last.then_inc(turned, 1)

            def sums(g, u):
                pe.wait_ge(lnT_ready, g + 1)
                if has(g, 1):
                    pe.wait_ge(s1_ready, g)
                    pe.wait_ge(s2_read, g)
                rhs = lnT[u][:, :, :].rearrange("p t q -> p (t q)")
                nc.tensor.matmul(b1[:, :], v1[:, :], rhs, start=True, stop=True)
                nc.tensor.matmul(b2[:, :], v2[:, :], rhs, start=True, stop=True).then_inc(sums_done, 1)

            def turn_p(g, u):
                pe.wait_ge(pD_ready, g + 1)
                if has(g, 1):
                    pe.wait_ge(pT_ready, g)
                for j in range(GT):
                    last = nc.tensor.transpose(bP[:, j * P:(j + 1) * P], pD[u][:, j, :], ident[:, :])
                last.then_inc(p_turned, 1)

            def edges(g, u):
                pe.wait_ge(pT_ready, g + 1)
                pe.wait_ge(kept, g + 1)
                if has(g, 1):
                    pe.wait_ge(x_done, g)
                for j in range(GT):
                    last = nc.tensor.matmul(bY[:, j * D:(j + 1) * D], pT[u][:, j, :],
                                            XN[:, bass.ds(g * GT + j, 1), :].rearrange("p o d -> p (o d)"),
                                            start=True, stop=True)
                last.then_inc(edge_done, 1)

            pe.wait_ge(setup, 1)
            software_pipeline(pe, [None, turn, sums, None, turn_p, edges], NG)

        @block.scalar
        def _(act):
            def normalise(g, u):
                if has(g, 2):
                    act.wait_ge(turned, g - 1)
                    act.wait_ge(kept, g - 1)
                act_normalise_group(nc, lnb[u], X, SHIFT, R, g).then_inc(ln_ready, 1)

            def turn(g, u):
                act.wait_ge(ln_ready, g + 1)
                nc.scalar.activation(group(XN, g), lnb[u][:, :, :], ACT.Copy).then_inc(kept, 1)
                act.wait_ge(turned, g + 1)
                if has(g, 2):
                    act.wait_ge(sums_done, g - 1)
                nc.scalar.activation(lnT[u][:, :, :], tiles(bX), ACT.Copy).then_inc(lnT_ready, 1)

            def sums(g, u):
                act.wait_ge(sums_done, g + 1)
                if has(g, 2):
                    act.wait_ge(e_chain, (g - 1) * 3)
                for b, h in enumerate(halves):
                    last = nc.scalar.activation(s1[u][h, :, :], tiles(b1)[h, :, h], ACT.Copy)
                last.then_inc(s1_ready, 1)

            def alpha(g, u):
                act.wait_ge(pre_ready, g + 1)
                nc.scalar.activation(e[u][:, :, :], e[u][:, :, :], ACT.Exp).then_inc(alpha_ready, 1)

            def second(g, u):
                act.wait_ge(shifted, g + 1)
                nc.scalar.activation(a[u][:, :, :], a[u][:, :, :], ACT.Exp).then_inc(exp_done, 1)

            def turn_p(g, u):
                act.wait_ge(p_turned, g + 1)
                if has(g, 2):
                    act.wait_ge(edge_done, g - 1)
                nc.scalar.activation(pT[u][:, :, :], tiles(bP), ACT.Copy).then_inc(pT_ready, 1)

            def sums_and_alpha(g, u):
                sums(g, u)
                alpha(g, u)

            software_pipeline(act, [normalise, turn, sums_and_alpha, second, turn_p, None], NG)

        @block.gpsimd
        def _(pool):
            for u in range(2):
                nc.gpsimd.memset(pD[u][:, :, :], 0.0).then_inc(zeroed, 1)
            pool.wait_ge(zeroed, 2)

            def place(g, u):
                pool.wait_ge(exp_done, g + 1)
                if has(g, 2):
                    pool.wait_ge(p_turned, g - 1)
                pool.sem_inc(begun, 1)
                for b, h in enumerate(halves):
                    last = nc.gpsimd.tensor_copy(pD[u][h, :, h], a[u][h, :, :])
                last.then_inc(pD_ready, 1)

            software_pipeline(pool, [None, None, None, place, None, None], NG)

        @block.vector
        def _(dve):
            chain = Chain(dve, chain_sem, 0)
            chain.start(0)
            link = chain.link
            dve.wait_ge(loaded, 48)
            dve.wait_ge(v_done, 1)
            link(dve.tensor_copy(v1[:, :], bcast(b1[:, 0:1], [P, P])))
            link(dve.tensor_copy(v2[:, :], bcast(b1[:, 1:2], [P, P])))
            link(dve.tensor_reduce(deg[:, :], adj[:, :, :], AX.X, ALU.add))
            link(dve.tensor_scalar(some[:, :], deg[:, :], 0.0, None, ALU.is_gt))
            link(dve.tensor_scalar(mask[:, :, :], adj[:, :, :], 0.0, None, ALU.is_gt))
            link(dve.tensor_scalar(far[:, :, :], mask[:, :, :], -1.0, FAR, ALU.add, ALU.mult))
            link(dve.tensor_tensor(deg[:, :], deg[:, :], some[:, :], ALU.mult))
            link(dve.tensor_scalar(some[:, :], some[:, :], -1.0, 1.0, ALU.mult, ALU.add))
            link(dve.tensor_tensor(deg[:, :], deg[:, :], some[:, :], ALU.add))
            dve.reciprocal(rdeg[:, :], deg[:, :]).then_inc(setup, 1)
            dve.wait_ge(setup, 1)
            e_links = Chain(dve, e_chain, 3)
            a_links = Chain(dve, a_chain, 3)

            def wide(ap):
                return bcast(ap.unsqueeze(2), [P, GT, NODES])

            def before_alpha(g, u):
                e_links.start(g)
                dve.wait_ge(sums_done, g + 1)
                for b, h in enumerate(halves):
                    last = dve.tensor_tensor(s2j[u][h, :, :], group(adj, g)[h, :, :], tiles(b2)[h, :, h], ALU.mult)
                last.then_inc(s2_read, 1)
                dve.wait_ge(s2_read, g + 1)
                e_links.link(dve.tensor_reduce(s2[u][:, :], s2j[u][:, :, :], AX.X, ALU.add))
                e_links.link(dve.tensor_tensor(s2[u][:, :], s2[u][:, :], rdeg[:, bass.ds(g * GT, GT)], ALU.mult))
                dve.wait_ge(s1_ready, g + 1)
                for j in range(GT):
                    last = dve.scalar_tensor_tensor(e[u][:, j, :], s1[u][:, j, :], s2[u][:, j:j + 1],
                                                    adj[:, bass.ds(g * GT + j, 1), :].rearrange("p o j -> p (o j)"),
                                                    ALU.add, ALU.mult)
                e_links.link(last)
                dve.scalar_tensor_tensor(e[u][:, :, :], e[u][:, :, :], SLOPE, e[u][:, :, :], ALU.mult,
                                         ALU.max).then_inc(pre_ready, 1)

            def after_alpha(g, u):
                a_links.start(g)
                dve.wait_ge(alpha_ready, g + 1)
                if has(g, 2):
                    dve.wait_ge(pD_ready, g - 1)
                a_links.link(dve.tensor_tensor(a[u][:, :, :], e[u][:, :, :], group(mask, g), ALU.mult))
                a_links.link(dve.tensor_tensor(a[u][:, :, :], a[u][:, :, :], group(far, g), ALU.add))
                a_links.link(dve.tensor_reduce(top[u][:, :], a[u][:, :, :], AX.X, ALU.max))
                dve.tensor_tensor(a[u][:, :, :], a[u][:, :, :], wide(top[u][:, :]), ALU.subtract).then_inc(shifted, 1)

            def totals(g, u):
                dve.wait_ge(exp_done, g + 1)
                dve.tensor_reduce(inv[u][:, :], a[u][:, :, :], AX.X, ALU.add).then_inc(inv_ready, 1)
                dve.wait_ge(inv_ready, g * 2 + 1)
                dve.reciprocal(inv[u][:, :], inv[u][:, :]).then_inc(inv_ready, 1)

            def add(g, u):
                dve.wait_ge(edge_done, g + 1)
                dve.wait_ge(inv_ready, g * 2 + 2)
                for j in range(GT):
                    xt = X[:, bass.ds(g * GT + j, 1), :].rearrange("p o d -> p (o d)")
                    last = dve.scalar_tensor_tensor(xt, bY[:, j * D:(j + 1) * D], inv[u][:, j:j + 1], xt,
                                                    ALU.mult, ALU.add)
                last.then_inc(x_done, 1)
                group_stats(dve, STATS, X, g, x_done, carried)

            software_pipeline(dve, [None, None, before_alpha, after_alpha, totals, add], NG)


class Experts:

    def __init__(self, name, src, top_k, hidden, capacity, act, tiles):
        self.name, self.src, self.top_k, self.hidden = name, src, top_k, hidden
        self.capacity, self.act, self.tiles = capacity, act, tiles
        self.chunks = [(c, min(P, hidden - c)) for c in range(0, hidden, P)]
        self.gated = act == "silu"


E = 8
ROW = D + 2
NO_ROW = 1 << 30
L0_CAPACITY = -(-5 * TOKENS // (4 * E))
WAYS = 4
UP, DOWN = 3, 6
TURNS = ((2 * T + E) // 2 + 7) // WAYS + 1
SPARE = E
EXPERTS = {
    "B": Experts("B", "L0_ffn", 1, 512, L0_CAPACITY, "relu", E * L0_CAPACITY // P),
    "F": Experts("F", "L2_ffn", 2, 341, None, "silu", 2 * T + SPARE),
    "H": Experts("H", "L3_ffn", 2, 256, None, "gelu", 2 * T + SPARE),
}


def prefill(nc, stack, scratch, blank):
    sc = Scope(nc, stack, "fill")
    blank_ready, filled = sc.sem("blank_ready"), sc.sem("filled")
    count = 0
    with nc.Block() as block:
        @block.vector
        def _(dve):
            dve.memset(blank[:, 0:D + 1], 0.0).then_inc(blank_ready, 1)
            dve.memset(blank[:, D + 1:ROW].bitcast(U32), NO_ROW).then_inc(blank_ready, 1)

        @block.sync
        def _(sp):
            sp.wait_ge(blank_ready, 2)
            for name, (rows, result) in scratch.items():
                n = EXPERTS[name].tiles
                sp.dma_start(rows.rearrange("(n p) c -> p n c", p=P),
                             bcast(blank[:, :].unsqueeze(1), [P, n, ROW])).then_inc(filled, 16)
                if name == "B":
                    sp.dma_start(result.rearrange("(n p) c -> p n c", p=P),
                                 bcast(blank[:, 0:D].unsqueeze(1), [P, T, D])).then_inc(filled, 16)
    return filled, 16 * (len(scratch) + ("B" in scratch))


def expert_logits(nc, m, g_in, X, XN, MEAN, R, LOG, ident, banks):
    with ExitStack() as stack:
        sc = Scope(nc, stack, m.name + "1")
        affine, biased = m.act == "gelu", m.act != "silu"
        gate = sc.sb("gate", [P, E])
        gate_b = sc.sb("gate_b", [P, E])
        gamma = sc.sb("gamma", [P, D])
        beta = sc.sb("beta", [P, D])
        lnb = [sc.sb(f"lnb{u}", [P, GT, D]) for u in range(2)]
        lnT = [sc.sb(f"lnT{u}", [P, GT, P]) for u in range(2)]
        loaded, ln_chain, ln_ready = sc.sem("loaded"), sc.sem("ln_chain"), sc.sem("ln_ready")
        turned, lnT_ready, kept = sc.sem("turned"), sc.sem("lnT_ready"), sc.sem("kept")
        logits_done, logits_read = sc.sem("logits_done"), sc.sem("logits_read")
        pT, pL = banks[0:2], banks[2:4]
        loads = 16 * (1 + biased + 2 * affine)
        block = stack.enter_context(nc.Block())

        @block.sync
        def _(sp):
            sp.dma_start(gate[:, :], g_in[m.src + "_gate"]).then_inc(loaded, 16)
            if biased:
                sp.dma_start(gate_b[:, :], bcast(g_in[m.src + "_gate_b"], [P, E])).then_inc(loaded, 16)
            if affine:
                sp.dma_start(gamma[:, :], bcast(g_in[m.src + "_gamma"], [P, D])).then_inc(loaded, 16)
                sp.dma_start(beta[:, :], bcast(g_in[m.src + "_beta"], [P, D])).then_inc(loaded, 16)

        @block.vector
        def _(dve):
            dve.wait_ge(loaded, loads)

            def normalise(g, u):
                if has(g, 2):
                    dve.wait_ge(turned, g - 1)
                    dve.wait_ge(kept, g - 1)
                ins = normalise_group(dve, lnb[u], X, MEAN, R, g)
                if affine:
                    ins.then_inc(ln_chain, 1)
                    dve.wait_ge(ln_chain, g * 2 + 1)
                    dve.tensor_tensor(lnb[u][:, :, :], lnb[u][:, :, :],
                                      bcast(gamma[:, :].unsqueeze(1), [P, GT, D]), ALU.mult).then_inc(ln_chain, 1)
                    dve.wait_ge(ln_chain, g * 2 + 2)
                    ins = dve.tensor_tensor(lnb[u][:, :, :], lnb[u][:, :, :],
                                            bcast(beta[:, :].unsqueeze(1), [P, GT, D]), ALU.add)
                ins.then_inc(ln_ready, 1)

            def logits(g, u):
                dve.wait_ge(logits_done, g + 1)
                src = pL[u][:, 0:GT * E].rearrange("p (t e) -> p t e", t=GT)
                if biased:
                    dve.tensor_tensor(group(LOG, g), src, bcast(gate_b[:, :].unsqueeze(1), [P, GT, E]),
                                      ALU.add).then_inc(logits_read, 1)
                else:
                    dve.tensor_copy(group(LOG, g), src).then_inc(logits_read, 1)

            software_pipeline(dve, [normalise, None, None, logits, None], NG)

        @block.tensor
        def _(pe):
            def turn(g, u):
                pe.wait_ge(ln_ready, g + 1)
                if has(g, 2):
                    pe.wait_ge(lnT_ready, g - 1)
                for j in range(GT):
                    last = nc.tensor.transpose(pT[u][:, j * P:(j + 1) * P], lnb[u][:, j, :], ident[:, :])
                last.then_inc(turned, 1)

            def logits(g, u):
                pe.wait_ge(lnT_ready, g + 1)
                if has(g, 2):
                    pe.wait_ge(logits_read, g - 1)
                for j in range(GT):
                    last = nc.tensor.matmul(pL[u][:, j * E:(j + 1) * E], lnT[u][:, j, :], gate[:, :],
                                            start=True, stop=True)
                last.then_inc(logits_done, 1)

            pe.wait_ge(loaded, loads)
            software_pipeline(pe, [None, turn, None, logits, None], NG)

        @block.scalar
        def _(act):
            def turn(g, u):
                act.wait_ge(turned, g + 1)
                if has(g, 2):
                    act.wait_ge(logits_done, g - 1)
                nc.scalar.activation(lnT[u][:, :, :], pT[u][:, :].rearrange("p (t d) -> p t d", t=GT),
                                     ACT.Copy).then_inc(lnT_ready, 1)
                nc.scalar.activation(group(XN, g), lnb[u][:, :, :], ACT.Copy).then_inc(kept, 1)

            software_pipeline(act, [None, turn, None, None, None], NG)


def route(nc, m, g_in, LOG, META, ROWS, TILE_E, banks):
    with ExitStack() as stack:
        sc = Scope(nc, stack, m.name + "2")
        K, NT = m.top_k, m.tiles
        tri = sc.sb("tri", [P, P])
        ones = sc.sb("ones", [P, P])
        steps = sc.sb("steps", [P, T])
        tile_no = sc.sb("tile_no", [P, NT])
        places = sc.sb("places", [P, T, 2], U32)
        top = [sc.sb(f"top{k}", [P, T]) for k in range(K)]
        masked = sc.sb("masked", [P, T, E])
        equal = sc.sb("equal", [P, T, E])
        taken = sc.sb("taken", [P, 2, T])
        chosen = [sc.sb(f"chosen{k}", [P, T, E]) for k in range(K)]
        any_chosen = sc.sb("any_chosen", [P, T, E])
        z = sc.sb("z", [P, T, E])
        esum = sc.sb("esum", [P, T])
        inv = sc.sb("inv", [P, T])
        e2 = sc.sb("e2", [P, T])
        tot = sc.sb("tot", [P, E, T])
        cum = sc.sb("cum", [P, E, T])
        cmp = sc.sb("cmp", [P, E, T])
        cmp2 = sc.sb("cmp2", [P, NT, E])
        nt = sc.sb("nt", [P, E])
        nt_cum = sc.sb("nt_cum", [P, E])
        off = sc.sb("off", [P, E])
        pos = sc.sb("pos", [P, T, E])
        row = sc.sb("row", [P, T])
        over = sc.sb("over", [P, T])
        tile_e = sc.sb("tile_e", [1, 2 * (DOWN + WAYS * TURNS)])
        digits = sc.sb("digits", [1, 2 * WAYS])
        words = sc.sb("words", [1, 2, TURNS, 2 * WAYS])
        word_sum = sc.sb("word_sum", [1, 2, TURNS])
        loaded, chain_sem = sc.sem("loaded"), sc.sem("chain")
        z_ready, exp_done, chosen_ready = sc.sem("z_ready"), sc.sem("exp_done"), sc.sem("chosen_ready")
        counted = sc.sem("counted")
        pU, pO = banks[0:2]
        block = stack.enter_context(nc.Block())

        @block.sync
        def _(sp):
            sp.dma_start(tri[:, :], g_in["c_tri"]).then_inc(loaded, 16)
            sp.dma_start(digits[:, :], g_in["c_digits"]).then_inc(loaded, 16)
            sp.dma_start(ones[:, :], g_in["c_ones"]).then_inc(loaded, 16)
            sp.dma_start(steps[:, :], bcast(g_in["c_steps"], [P, T])).then_inc(loaded, 16)
            sp.dma_start(tile_no[:, :], bcast(g_in["c_tile_no"][:, 0:NT], [P, NT])).then_inc(loaded, 16)
            sp.dma_start(places[:, :, :], g_in["c_places"]).then_inc(loaded, 16)

        @block.scalar
        def _(act):
            act.wait_ge(z_ready, 1)
            nc.scalar.activation(z[:, :, :], z[:, :, :], ACT.Exp).then_inc(exp_done, 1)
            if K == 2:
                act.wait_ge(z_ready, 2)
                nc.scalar.activation(e2[:, :], e2[:, :], ACT.Exp).then_inc(exp_done, 1)

        @block.tensor
        def _(pe):
            pe.wait_ge(loaded, 96)
            pe.wait_ge(chosen_ready, 1)
            flat = any_chosen[:, :, :].rearrange("p t e -> p (t e)")
            nc.tensor.matmul(pU[:, :], tri[:, :], flat, start=True, stop=True).then_inc(counted, 1)
            nc.tensor.matmul(pO[:, :], ones[:, :], flat, start=True, stop=True).then_inc(counted, 1)

        @block.vector
        def _(dve):
            chain = Chain(dve, chain_sem, 0)
            chain.start(0)
            link = chain.link

            def wide(ap):
                return bcast(ap.unsqueeze(2), [P, T, E])

            dve.wait_ge(loaded, 96)
            for k in range(K):
                src = LOG if k == 0 else masked
                link(dve.tensor_reduce(top[k][:, :], src[:, :, :], AX.X, ALU.max))
                link(dve.tensor_tensor(equal[:, :, :], src[:, :, :], wide(top[k][:, :]), ALU.is_equal))
                link(dve.memset(taken[:, 0, :], 0.0))
                for e in range(E):
                    dve.tensor_tensor(chosen[k][:, :, e], equal[:, :, e], taken[:, e % 2, :], ALU.is_gt)
                    link(dve.tensor_tensor(taken[:, (e + 1) % 2, :], equal[:, :, e], taken[:, e % 2, :], ALU.max))
                if k == 0:
                    dve.tensor_tensor(z[:, :, :], LOG[:, :, :], wide(top[0][:, :]),
                                      ALU.subtract).then_inc(z_ready, 1)
                    if K == 2:
                        link(dve.scalar_tensor_tensor(masked[:, :, :], chosen[0][:, :, :], -1e30, LOG[:, :, :],
                                                      ALU.mult, ALU.add))
            if K == 2:
                dve.tensor_tensor(e2[:, :], top[1][:, :], top[0][:, :], ALU.subtract).then_inc(z_ready, 1)
                dve.tensor_tensor(any_chosen[:, :, :], chosen[0][:, :, :], chosen[1][:, :, :],
                                  ALU.add).then_inc(chosen_ready, 1)
            else:
                dve.tensor_copy(any_chosen[:, :, :], chosen[0][:, :, :]).then_inc(chosen_ready, 1)

            dve.wait_ge(exp_done, K)
            weights = [META[:, :, k, 0] for k in range(K)]
            if m.name == "H":
                link(dve.tensor_scalar(esum[:, :], e2[:, :], 1.0, None, ALU.add))
                link(dve.reciprocal(weights[0], esum[:, :]))
                link(dve.tensor_tensor(weights[1], e2[:, :], weights[0], ALU.mult))
            else:
                link(dve.tensor_reduce(esum[:, :], z[:, :, :], AX.X, ALU.add))
                link(dve.reciprocal(inv[:, :], esum[:, :]))
                if K == 1:
                    link(dve.tensor_copy(weights[0], inv[:, :]))
                else:
                    link(dve.tensor_tensor(e2[:, :], e2[:, :], inv[:, :], ALU.mult))
                    link(dve.tensor_tensor(esum[:, :], e2[:, :], inv[:, :], ALU.add))
                    link(dve.tensor_scalar(esum[:, :], esum[:, :], 1e-9, None, ALU.add))
                    link(dve.reciprocal(over[:, :], esum[:, :]))
                    link(dve.tensor_tensor(weights[0], inv[:, :], over[:, :], ALU.mult))
                    link(dve.tensor_tensor(weights[1], e2[:, :], over[:, :], ALU.mult))
            for k in range(K):
                link(dve.tensor_copy(META[:, :, k, 1].bitcast(U32), places[:, :, k]))

            dve.wait_ge(counted, 2)
            link(dve.tensor_copy(tot[:, :, :], pO[:, :].rearrange("p (t e) -> p e t", e=E)))
            for e in range(E):
                link(dve.tensor_tensor_scan(cum[:, e, :], ones[:, 0:T], tot[:, e, :], 0.0, ALU.mult, ALU.add))
            link(dve.tensor_tensor(tot[:, :, :], cum[:, :, :], tot[:, :, :], ALU.subtract))
            link(dve.tensor_tensor(pos[:, :, :], pU[:, :].rearrange("p (t e) -> p t e", e=E),
                                   tot[:, :, :].rearrange("p e t -> p t e"), ALU.add))
            if m.capacity is None:
                link(dve.tensor_tensor(cmp[:, :, :], bcast(cum[:, :, T - 1:T], [P, E, T]),
                                       bcast(steps[:, :].unsqueeze(1), [P, E, T]), ALU.is_gt))
                link(dve.tensor_reduce(nt[:, :], cmp[:, :, :], AX.X, ALU.add))
                link(dve.tensor_tensor_scan(nt_cum[:, :], ones[:, 0:E], nt[:, :], 0.0, ALU.mult, ALU.add))
                link(dve.tensor_tensor(off[:, :], nt_cum[:, :], nt[:, :], ALU.subtract))
                link(dve.tensor_scalar(off[:, :], off[:, :], float(P), -1.0, ALU.mult, ALU.add))
            else:
                link(dve.tensor_scalar(nt_cum[:, :], tile_no[:, 0:E], 1.0, float(m.capacity // P), ALU.add, ALU.mult))
                link(dve.tensor_scalar(off[:, :], tile_no[:, 0:E], float(m.capacity), -1.0, ALU.mult, ALU.add))
            link(dve.tensor_tensor(cmp2[:, :, 0:E - 1], bcast(nt_cum[:, 0:E - 1].unsqueeze(1), [P, NT, E - 1]),
                                   bcast(tile_no[:, :].unsqueeze(2), [P, NT, E - 1]), ALU.is_le))
            link(dve.memset(tile_e[:, :], 0.0))
            link(dve.tensor_reduce(tile_e[:, 2 * DOWN:2 * DOWN + NT], cmp2[0:1, :, 0:E - 1], AX.X, ALU.add))
            for i, first in enumerate((2 * (DOWN - UP), 0)):
                part = tile_e[:, first:first + 2 * WAYS * TURNS].rearrange("p (j k) -> p j k", k=2 * WAYS)
                link(dve.tensor_tensor(words[:, i, :, :], part, bcast(digits[:, :].unsqueeze(1), [1, TURNS, 2 * WAYS]),
                                       ALU.mult))
            link(dve.tensor_reduce(word_sum[:, :, :], words[:, :, :, :], AX.X, ALU.add))
            link(dve.tensor_copy(TILE_E[:, :, :], word_sum[:, :, :]))
            for k in range(K):
                if m.capacity is not None:
                    link(dve.tensor_tensor(masked[:, :, :], pos[:, :, :], chosen[k][:, :, :], ALU.mult))
                    link(dve.tensor_reduce(over[:, :], masked[:, :, :], AX.X, ALU.add))
                    link(dve.tensor_scalar(over[:, :], over[:, :], float(m.capacity), 1e6, ALU.is_gt, ALU.mult))
                link(dve.tensor_tensor(equal[:, :, :], pos[:, :, :], bcast(off[:, :].unsqueeze(1), [P, T, E]),
                                       ALU.add))
                link(dve.tensor_tensor(equal[:, :, :], equal[:, :, :], chosen[k][:, :, :], ALU.mult))
                link(dve.tensor_reduce(row[:, :], equal[:, :, :], AX.X, ALU.add))
                if m.capacity is not None:
                    link(dve.tensor_tensor(row[:, :], row[:, :], over[:, :], ALU.add))
                link(dve.tensor_copy(ROWS[:, :, k], row[:, :]))


def dispatch(nc, m, XN, META, ROWS, rows, filled, fills, loads):
    SENDS = 8
    with ExitStack() as stack:
        sc = Scope(nc, stack, m.name + "3")
        K, n_rows = m.top_k, m.tiles * P
        stage = [sc.sb(f"stage{u}", [P, K, ROW]) for u in range(SENDS)]
        index = [[sc.sb(f"index{u}_{k}", [P, 1], U32) for k in range(K)] for u in range(SENDS)]
        begun = sc.sem("begun")
        x_staged, meta_staged, sent = sc.sem("x_staged"), sc.sem("meta_staged"), sc.sems("sent", SENDS)
        block = stack.enter_context(nc.Block())

        def free(eng, t, u):
            if has(t, SENDS):
                eng.wait_ge(sent[u], (t - u) * (16 * K // SENDS))

        @block.sync
        def _(sp):
            for i, (dst, src, loaded) in enumerate(loads):
                sp.wait_ge(x_staged, (i + 1) * (T // (len(loads) + 2)))
                sp.dma_start(dst, src).then_inc(loaded, 16)

        @block.scalar
        def _(act):
            def copy_x(t, u):
                free(act, t, u)
                nc.scalar.activation(stage[u][:, :, 0:D], bcast(XN[:, bass.ds(t, 1), :], [P, K, D]),
                                     ACT.Copy).then_inc(x_staged, 1)

            software_pipeline(act, [copy_x, None], T, SENDS)

        @block.vector
        def _(dve):
            def copy_meta(t, u):
                free(dve, t, u)
                dve.tensor_copy(stage[u][:, :, D:ROW].bitcast(U32),
                                META[:, bass.ds(t, 1), :, :].rearrange("p o k c -> p (o k) c").bitcast(U32)
                                ).then_inc(meta_staged, 1)
                for k in range(K):
                    dve.tensor_copy(index[u][k][:, :], ROWS[:, bass.ds(t, 1), k]).then_inc(meta_staged, 1)

            software_pipeline(dve, [copy_meta, None], T, SENDS)

        @block.gpsimd
        def _(pool):
            pool.wait_ge(filled, fills)

            last_row = pool.to_reg(n_rows - 1)

            def send(t, u):
                pool.wait_ge(x_staged, t + 1)
                pool.wait_ge(meta_staged, (t + 1) * (1 + K))
                pool.sem_inc(begun, 1)
                for k in range(K):
                    pool.indirect_dma_start(rows, bass.IndirectOffsetOnAxis(ap=index[u][k][:, :], axis=0),
                                            stage[u][:, k, :], None, bounds_check=last_row,
                                            oob_is_err=False).then_inc(sent[u], 16)

            software_pipeline(pool, [None, send], T, SENDS)
            for u in range(SENDS):
                pool.wait_ge(sent[u], 16 * K * T // SENDS)


def expert_weights(sc, m, g_in):
    H, C = m.hidden, len(m.chunks)
    w_up = sc.sb("w_up", [P, E, H])
    w_gate = sc.sb("w_gate", [P, E, H]) if m.gated else None
    w_down = sc.sb("w_down", [P, E, C, D])
    b_up = None if m.gated else sc.sb("b_up", [P, E, H])
    b_down = None if m.gated else sc.sb("b_down", [P, E, D])
    loaded = sc.sem("loaded")
    half = E // 2
    loads = []
    for e in (slice(0, half), slice(half, E)):
        loads.append((w_up[:, e, :], g_in[m.src + "_up"][e].rearrange("e d f -> d e f")))
        if m.gated:
            loads.append((w_gate[:, e, :], g_in[m.src + "_up3"][e].rearrange("e d f -> d e f")))
        else:
            loads.append((b_up[:, e, :].rearrange("p e f -> p (e f)"),
                          bcast(g_in[m.src + "_b_up"][:, e.start * H:e.stop * H], [P, half * H])))
    for c, (f0, nf) in enumerate(m.chunks):
        loads.append((w_down[0:nf, :, c, :], g_in[m.src + "_down"][:, f0:f0 + nf, :].rearrange("e f d -> f e d")))
    if not m.gated:
        loads.append((b_down[:, :, :].rearrange("p e f -> p (e f)"), bcast(g_in[m.src + "_b_down"], [P, E * D])))
    loads = [(dst, src, loaded) for dst, src in loads]
    return (w_up, w_gate, w_down, b_up, b_down), loaded, loads


def run_experts(nc, m, g_in, TILE_E, rows, result, ident, psum, weights, loaded, loads):
    with ExitStack() as stack:
        sc = Scope(nc, stack, m.name + "4")
        NT, H, C = m.tiles, m.hidden, len(m.chunks)
        NP = NT // 2
        w_up, w_gate, w_down, b_up, b_down = weights
        xt = [sc.sb(f"xt{u}", [P, 2, ROW]) for u in range(WAYS)]
        tail = [sc.sb(f"tail{u}", [P, 2, 2], U32) for u in range(WAYS)]
        place = [sc.sb(f"place{u}", [P, 2], U32) for u in range(WAYS)]
        xT = [sc.sb(f"xT{u}", [P, 2, P]) for u in range(2)]
        h = [sc.sb(f"h{u}", [P, 2, H]) for u in range(2)] if m.act != "relu" else None
        act_h = [sc.sb(f"act_h{u}", [P, 2, H]) for u in range(2)]
        hT = [sc.sb(f"hT{u}", [P, 2, C, P]) for u in range(2)]
        y = [sc.sb(f"y{u}", [P, 2, D]) for u in range(WAYS)]
        yc = [sc.sb(f"yc{u}", [P, 2, D]) for u in range(2)]
        no_number = [sc.sb(f"no_number{u}", [P, 2, D], U32) for u in range(2)]
        finite = [sc.sb(f"finite{u}", [P, 2, D], U32) for u in range(2)]
        zeros = sc.sb("zeros", [P, 2, D])
        x_in, x_read, begun = sc.sems("x_in", WAYS), sc.sem("x_read"), sc.sem("begun")
        turned, xT_ready, up_done, h_ready = sc.sem("turned"), sc.sem("xT_ready"), sc.sem("up_done"), sc.sem("h_ready")
        act_ready, h_turned, hT_ready = sc.sem("act_ready"), sc.sem("h_turned"), sc.sem("hT_ready")
        down_done, down_read, y_ready = sc.sem("down_done"), sc.sem("down_read"), sc.sem("y_ready")
        settled = sc.sem("settled")
        zeroed, chain_sem, out = sc.sem("zeroed"), sc.sem("chain"), sc.sems("out", WAYS)
        up_read = h_ready if m.act == "gelu" else act_ready
        down_bank_read = y_ready if m.gated else down_read
        pX, pY, pH = psum[:, 0, 0:2 * P], psum[:, 1, 0:2 * D], psum[:, 2:4, :]
        pUp = [psum[:, 4:6, :], psum[:, 4:6, :] if m.gated else psum[:, 6:8, :]]
        pGate = psum[:, 6:8, :]
        up_ways = 1 if m.gated else 2
        n_result = m.top_k * TOKENS
        n_loads = 16 * len(loads)
        block = stack.enter_context(nc.Block())

        @block.sync
        def _(sp):
            def load(t, w):
                if has(t, WAYS):
                    sp.wait_ge(x_read, t - (WAYS - 1))
                sp.dma_start(xt[w][:, :, :],
                             rows[bass.ds(t * (2 * P), 2 * P), :].rearrange("(i p) c -> p i c", p=P)).then_inc(x_in[w], 16)

            software_pipeline(sp, [load] + [None] * 7, NP, WAYS)

        class TileExperts:

            def __init__(self, eng):
                self.eng = eng

            def turn(self, j):
                self.words = [self.eng.value_load(TILE_E[:, i, bass.ds(j, 1)], min_val=0, max_val=E ** (2 * WAYS) - 1)
                              for i in range(2)]

            def of(self, w, phase, i):
                return (self.words[phase == DOWN] >> (3 * (2 * ((w + phase) % WAYS) + i))) & (E - 1)

        @block.tensor
        def _(pe):
            pe.wait_ge(loaded, n_loads)
            experts = TileExperts(pe)

            def turn(t, w):
                pe.wait_ge(x_in[w], (t - w) * (16 // WAYS) + 16)
                if has(t, 1):
                    pe.wait_ge(xT_ready, t)
                for i in range(2):
                    last = nc.tensor.transpose(pX[:, i * P:(i + 1) * P], xt[w][:, i, 0:D], ident[:, :])
                last.then_inc(turned, 1)

            def up(t, w):
                e = [experts.of(w, UP, i) for i in range(2)]
                pe.wait_ge(xT_ready, t + 1)
                if has(t, up_ways):
                    pe.wait_ge(up_read, t - (up_ways - 1))
                for i in range(2):
                    mm = nc.tensor.matmul(pUp[w % 2][:, i, 0:H], xT[w % 2][:, i, :],
                                          w_up[:, bass.ds(e[i], 1), :].rearrange("p o f -> p (o f)"),
                                          start=True, stop=True)
                    if m.gated:
                        mm = nc.tensor.matmul(pGate[:, i, 0:H], xT[w % 2][:, i, :],
                                              w_gate[:, bass.ds(e[i], 1), :].rearrange("p o f -> p (o f)"),
                                              start=True, stop=True)
                mm.then_inc(up_done, 1)

            def turn_h(t, w):
                pe.wait_ge(act_ready, t + 1)
                if has(t, 1):
                    pe.wait_ge(hT_ready, t)
                for i in range(2):
                    for c, (f0, nf) in enumerate(m.chunks):
                        last = nc.tensor.transpose(pH[0:nf, i, c * P:(c + 1) * P], act_h[w % 2][:, i, f0:f0 + nf],
                                                   ident[:, :])
                last.then_inc(h_turned, 1)

            def down(t, w):
                e = [experts.of(w, DOWN, i) for i in range(2)]
                pe.wait_ge(hT_ready, t + 1)
                if has(t, 1):
                    pe.wait_ge(down_bank_read, t)
                for i in range(2):
                    for c, (f0, nf) in enumerate(m.chunks):
                        last = nc.tensor.matmul(pY[:, i * D:(i + 1) * D], hT[w % 2][0:nf, i, c, :],
                                                w_down[0:nf, bass.ds(e[i], 1), c, :].rearrange("p o d -> p (o d)"),
                                                start=(c == 0), stop=(c == C - 1))
                last.then_inc(down_done, 1)

            software_pipeline(pe, [None, None, turn, up, None, turn_h, down, None], NP, WAYS, experts.turn)

        @block.scalar
        def _(act):
            def turn(t, w):
                act.wait_ge(turned, t + 1)
                if has(t, 2):
                    act.wait_ge(up_done, t - 1)
                nc.scalar.activation(xT[w % 2][:, :, :], pX.rearrange("p (i q) -> p i q", i=2),
                                     ACT.Copy).then_inc(xT_ready, 1)

            def silu(t, w):
                act.wait_ge(up_done, t + 1)
                if has(t, 2):
                    act.wait_ge(act_ready, t - 1)
                nc.scalar.activation(h[w % 2][:, :, :], pUp[w % 2][:, :, 0:H], ACT.Silu).then_inc(h_ready, 1)

            def gelu(t, w):
                act.wait_ge(h_ready, t + 1)
                if has(t, 2):
                    act.wait_ge(h_turned, t - 1)
                nc.scalar.activation(act_h[w % 2][:, :, :], h[w % 2][:, :, :], ACT.Gelu).then_inc(act_ready, 1)

            def turn_h(t, w):
                act.wait_ge(h_turned, t + 1)
                if has(t, 2):
                    act.wait_ge(down_done, t - 1)
                func = ACT.Relu if m.act == "relu" else ACT.Copy
                full, rest = H // P, H % P
                for i in range(2):
                    ins = nc.scalar.activation(hT[w % 2][:, i, 0:full, :],
                                               pH[:, i, 0:full * P].rearrange("p (c q) -> p c q", q=P), func)
                if rest:
                    ins = nc.scalar.activation(hT[w % 2][0:rest, :, full, :], pH[0:rest, :, full * P:(full + 1) * P], func)
                ins.then_inc(hT_ready, 1)

            software_pipeline(act, [None, None, turn, silu if m.gated else None, gelu if m.act == "gelu" else None,
                                    turn_h, None, None], NP, WAYS)

        @block.vector
        def _(dve):
            dve.wait_ge(loaded, n_loads)
            chain = Chain(dve, chain_sem, 3)
            experts = TileExperts(dve)
            dve.memset(zeros[:, :, :], 0.0).then_inc(zeroed, 1)
            dve.wait_ge(zeroed, 1)

            def activate(t, w):
                e = None if m.gated else [experts.of(w, UP, i) for i in range(2)]
                dve.wait_ge(up_done, t + 1)
                dve.tensor_copy(tail[w][:, :, :], xt[w][:, :, D:ROW].bitcast(U32)).then_inc(x_read, 1)
                if m.gated:
                    dve.wait_ge(h_ready, t + 1)
                if has(t, 2):
                    dve.wait_ge(act_ready if m.act == "gelu" else h_turned, t - 1)
                if m.gated:
                    dve.tensor_tensor(act_h[w % 2][:, :, :], h[w % 2][:, :, :], pGate[:, :, 0:H],
                                      ALU.mult).then_inc(act_ready, 1)
                    return
                dst = act_h if m.act == "relu" else h
                ready = act_ready if m.act == "relu" else h_ready
                for i in range(2):
                    last = dve.tensor_tensor(dst[w % 2][:, i, :], pUp[w % 2][:, i, 0:H],
                                             b_up[:, bass.ds(e[i], 1), :].rearrange("p o f -> p (o f)"), ALU.add)
                last.then_inc(ready, 1)

            def finish(t, w):
                e = None if m.gated else [experts.of(w, DOWN, i) for i in range(2)]
                weight = [tail[w][:, i, 0:1].bitcast(F32) for i in range(2)]
                if has(t, WAYS):
                    dve.wait_ge(out[w], (t - w) * (32 // WAYS))
                dve.tensor_copy(place[w][:, :], tail[w][:, :, 1])
                dve.wait_ge(down_done, t + 1)
                if m.gated:
                    for i in range(2):
                        last = dve.tensor_scalar(y[w][:, i, :], pY[:, i * D:(i + 1) * D], weight[i], None, ALU.mult)
                    last.then_inc(y_ready, 1)
                    return
                yy, cc = y[w][:, :, :], yc[w % 2][:, :, :]
                chain.start(t)
                for i in range(2):
                    last = dve.tensor_tensor(yc[w % 2][:, i, :], pY[:, i * D:(i + 1) * D],
                                             b_down[:, bass.ds(e[i], 1), :].rearrange("p o f -> p (o f)"), ALU.add)
                last.then_inc(down_read, 1)
                dve.wait_ge(down_read, t + 1)
                dst = y[w] if m.act == "gelu" else yc[w % 2]
                for i in range(2):
                    last = dve.tensor_scalar(dst[:, i, :], yc[w % 2][:, i, :], weight[i], None, ALU.mult)
                if m.act == "gelu":
                    last.then_inc(y_ready, 1)
                    return
                chain.link(last)
                dve.tensor_scalar(yy, cc, 1e4, -1e4, ALU.min, ALU.max)
                dve.tensor_tensor(no_number[w % 2][:, :, :], cc, cc, ALU.not_equal)
                chain.link(dve.scalar_tensor_tensor(finite[w % 2][:, :, :], cc, 0.0, zeros[:, :, :], ALU.mult, ALU.is_equal))
                dve.sem_inc(settled, 1)
                chain.link(dve.copy_predicated(yy, no_number[w % 2][:, :, :], zeros[:, :, :]))
                dve.sem_inc(settled, 1)
                dve.copy_predicated(yy, finite[w % 2][:, :, :], cc).then_inc(y_ready, 1)

            software_pipeline(dve, [None, None, None, activate, None, None, finish, None], NP, WAYS,
                              None if m.gated else experts.turn)

        @block.gpsimd
        def _(pool):
            last_place = pool.to_reg(n_result - 1)

            def send(t, w):
                pool.wait_ge(y_ready, t + 1)
                pool.sem_inc(begun, 1)
                for i in range(2):
                    pool.indirect_dma_start(result, bass.IndirectOffsetOnAxis(ap=place[w][:, i:i + 1], axis=0),
                                            y[w][:, i, :], None, bounds_check=last_place,
                                            oob_is_err=False).then_inc(out[w], 16)

            software_pipeline(pool, [None] * 7 + [send], NP, WAYS)
            for w in range(WAYS):
                pool.wait_ge(out[w], 32 * NP // WAYS)


def combine(nc, m, X, STATS, result, out):
    with ExitStack() as stack:
        sc = Scope(nc, stack, m.name + "5")
        PARTS = 4
        K, n, tiles = m.top_k, NG // 2, 2 * GT
        part = [sc.sb(f"part{u}", [P, K, tiles, D]) for u in range(PARTS)]
        x_done, part_in, carried, x_out = sc.sem("x_done"), sc.sems("part_in", PARTS), sc.sem("carried"), sc.sem("x_out")
        both_ready = sc.sem("both_ready")
        block = stack.enter_context(nc.Block())

        @block.sync
        def _(sp):
            for g in range(n):
                if g >= PARTS:
                    sp.wait_ge(x_done, g - PARTS + 1)
                for k in range(K):
                    src = result[bass.ds(k * TOKENS + g * tiles * P, tiles * P), :]
                    sp.dma_start(part[g % PARTS][:, k, :, :], src.rearrange("(t p) d -> p t d", p=P)).then_inc(part_in[g % PARTS], 16)

        @block.gpsimd
        def _(pool):
            for g in range(n if K == 2 else 0):
                pool.wait_ge(part_in[g % PARTS], 16 * K * (g // PARTS + 1))
                first, second = (part[g % PARTS][:, k, :, :] for k in range(2))
                pool.tensor_tensor(first, first, second, ALU.add).then_inc(both_ready, 1)

        @block.vector
        def _(dve):
            for g in range(n):
                dve.wait_ge(part_in[g % PARTS], 16 * K * (g // PARTS + 1))
                xs = X[:, g * tiles:(g + 1) * tiles, :]
                if K == 2:
                    dve.wait_ge(both_ready, g + 1)
                dve.tensor_tensor(xs, xs, part[g % PARTS][:, 0, :, :], ALU.add).then_inc(x_done, 1)
                dve.wait_ge(x_done, g + 1)
                if out is None:
                    dve.sem_inc(carried, 1)
                    for t in range(g * tiles, (g + 1) * tiles):
                        tile_stats(dve, STATS, X, t)

        @block.scalar
        def _(act):
            if out is not None:
                for g in range(n):
                    act.wait_ge(x_done, g + 1)
                    dst = out[g * tiles * P:(g + 1) * tiles * P, :].rearrange("(t p) d -> p t d", p=P)
                    act.dma_start(dst, X[:, g * tiles:(g + 1) * tiles, :]).then_inc(x_out, 16)
                act.wait_ge(x_out, 16 * n)


def experts_layer(nc, m, g_in, X, STATS, MEAN, R, ident, psum, banks, rows, result, filled, fills, out):
    layer_norm(nc, "ln" + m.name, STATS, MEAN, R, twice=(m.act == "gelu"))
    with ExitStack() as stack:
        sc = Scope(nc, stack, m.name)
        XN = sc.sb("XN", [P, T, D])
        LOG = sc.sb("logits", [P, T, E])
        META = sc.sb("meta", [P, T, m.top_k, 2])
        ROWS = sc.sb("rows", [P, T, m.top_k], U32)
        TILE_E = sc.sb("tile_e", [1, 2, TURNS], I32)
        expert_logits(nc, m, g_in, X, XN, MEAN, R, LOG, ident, banks)
        route(nc, m, g_in, LOG, META, ROWS, TILE_E, banks)
        weights = expert_weights(sc, m, g_in)
        dispatch(nc, m, XN, META, ROWS, rows, filled, fills, weights[2])
        run_experts(nc, m, g_in, TILE_E, rows, result, ident, psum, *weights)
    combine(nc, m, X, STATS, result, out)


def program(nc, g_in, out):
    with ExitStack() as stack:
        sc = Scope(nc, stack, "all")
        X = sc.sb("X", [P, T, D])
        MEAN = sc.sb("MEAN", [P, T])
        R = sc.sb("R", [P, T])
        SHIFT = sc.sb("SHIFT", [P, T])
        STATS = sc.sb("STATS", [P, T, 6])
        adj = sc.sb("adj", [P, T, NODES])
        ident = sc.sb("ident", [P, P])
        psum = stack.enter_context(nc.psum_tensor("psum", [P, 8, 512], F32))
        banks = [psum[:, i, :] for i in range(8)]
        x_in, x_out, const_in, carried = sc.sems("x_in", NCH), sc.sem("x_out"), sc.sem("const_in"), sc.sem("carried")
        adj_in = sc.sem("adj_in")
        out_bias = {name: sc.sb(name, [P, D]) for name in ("L0_gnn_bo", "L1_ffn_bo")}
        scratch = {
            name: (nc.dram_tensor(f"dram_{name}_rows", (m.tiles * P, ROW), F32).ap(),
                   nc.dram_tensor(f"dram_{name}_result", (m.top_k * TOKENS, D), F32).ap())
            for name, m in EXPERTS.items() if name in STAGES
        }

        blank = sc.sb("blank", [P, ROW])
        early = stack.enter_context(ExitStack())
        adj_A = early.enter_context(nc.sbuf_tensor("A_adj", [P, T, NODES], F32))
        weights_A = [early.enter_context(nc.sbuf_tensor(f"A_{name}", [P, cols], F32))
                     for name, cols in (("wq", D), ("wk", D), ("wv", D), ("wo", D), ("head_of", HEADS))]
        with nc.Block() as block:
            @block.sync
            def _(sp):
                for c in range(NCH):
                    src = g_in["x"][c * CH * P:(c + 1) * CH * P, :].rearrange("(t p) d -> p t d", p=P)
                    sp.dma_start(X[:, c * CH:(c + 1) * CH, :], src).then_inc(x_in[c], 16)
                for buf, name in zip(weights_A, ("L0_gnn_Wq", "L0_gnn_Wk", "L0_gnn_Wv", "L0_gnn_Wo", "c_head_of")):
                    sp.dma_start(buf[:, :], g_in[name]).then_inc(const_in, 16)
                sp.dma_start(ident[:, :], g_in["c_ident"]).then_inc(const_in, 16)
                for name, buf in out_bias.items():
                    sp.dma_start(buf[:, :], bcast(g_in[name], [P, D])).then_inc(const_in, 16)
                sp.dma_start(adj[:, :, :], g_in["adj"].rearrange("(t p) j -> p t j", p=P)).then_inc(adj_in, 16)
                sp.wait_ge(const_in, 16 * 8)

            @block.vector
            def _(dve):
                for c in range(NCH):
                    dve.wait_ge(x_in[c], 16)
                    dve.sem_inc(carried, 1)
                    for t in range(c * CH, (c + 1) * CH):
                        tile_stats(dve, STATS, X, t)

        filled, fills = prefill(nc, stack, scratch, blank)
        for stage in STAGES:
            if stage == "A":
                layer_norm(nc, "lnA", STATS, MEAN, R)
                graph_attention(nc, g_in, X, STATS, MEAN, R, ident, banks, out_bias["L0_gnn_bo"], adj, adj_in, adj_A, *weights_A)
                early.close()
            if stage == "B" or (stage == "C" and "B" not in STAGES):
                held_C = stack.enter_context(ExitStack())
                weights_C = load_gcn_weights(nc, Scope(nc, held_C, "C0"), g_in)
            if stage in EXPERTS:
                experts_layer(nc, EXPERTS[stage], g_in, X, STATS, MEAN, R, ident, psum, banks, *scratch[stage], filled, fills,
                              out if stage == STAGES[-1] else None)
            if stage == "C":
                held_D = held_C.enter_context(ExitStack())
                weights_D = RoutedWeights(Scope(nc, held_D, "D0"), g_in)
                layer_norm(nc, "lnC", STATS, MEAN, R, SHIFT=SHIFT)
                group_gcns(nc, g_in, X, STATS, SHIFT, R, ident, banks, weights_C, weights_D.combine)
            if stage == "D":
                layer_norm(nc, "lnD", STATS, MEAN, R)
                routed_mlp(nc, g_in, X, STATS, MEAN, R, ident, banks, out_bias["L1_ffn_bo"], weights_D.w)
                held_C.close()
            if stage == "E":
                layer_norm(nc, "lnE", STATS, MEAN, R, SHIFT=SHIFT)
                edge_attention(nc, g_in, X, STATS, SHIFT, R, ident, banks, adj)
            if stage == "G":
                layer_norm(nc, "lnG", STATS, MEAN, R, SHIFT=SHIFT)
                dense_gcn(nc, g_in, X, STATS, SHIFT, R, ident, banks, adj)

        if STAGES[-1] not in EXPERTS:
            with nc.Block() as block:
                @block.sync
                def _(sp):
                    sp.dma_start(out.rearrange("(t p) d -> p t d", p=P), X[:, :, :]).then_inc(x_out, 16)
                    sp.wait_ge(x_out, 16)


def kernel(**inputs):
    import numpy as np
    import concourse.bacc as bacc
    from concourse.bass_utils import run_bass_kernel_spmd

    a = {n: np.asarray(v) for n, v in inputs.items()}
    slot_adj = np.zeros((128, NODES, NODES), np.float32)
    slot_b2 = np.zeros((P, D), np.float32)
    slot_group = np.zeros((P, len(GROUPS)), np.float32)
    pick = np.zeros((P, P), np.float32)
    for g, nodes in enumerate(GROUPS):
        sl = slice(SLOT0[g], SLOT0[g] + len(nodes))
        slot_adj[:, sl, sl] = a["adj"][:, nodes][:, :, nodes]
        for b in range(2):
            rows = NODES * b + np.arange(sl.start, sl.stop)
            slot_b2[rows] = a["L1_gnn_b2"][g]
            slot_group[rows, g] = 1
            pick[NODES * b + np.array(nodes), rows] = 1
    lay = {
        "x": a["x"].reshape(TOKENS, D),
        "adj": a["adj"].reshape(TOKENS, NODES),
        "adjT": a["adj"].transpose(0, 2, 1).reshape(TOKENS, NODES),
        "nodemask": a["nodemask"].reshape(T, P).T,
        "L3_gnn_W": a["L3_gnn_W"].T,
        "L3_gnn_b": a["L3_gnn_b"].reshape(1, D),
        "L0_gnn_Wq": a["L0_gnn_Wq"].T, "L0_gnn_Wk": a["L0_gnn_Wk"].T, "L0_gnn_Wv": a["L0_gnn_Wv"].T,
        "L0_gnn_Wo": a["L0_gnn_Wo"].T, "L0_gnn_bo": a["L0_gnn_bo"].reshape(1, D),
        "c_head_of": np.repeat(np.eye(HEADS, dtype=np.float32), HD, axis=0),
        "slot_adj": slot_adj.reshape(TOKENS, NODES), "slot_adjT": slot_adj.transpose(0, 2, 1).reshape(TOKENS, NODES),
        "L1_gnn_W1": a["L1_gnn_W1"], "L1_gnn_W2": a["L1_gnn_W2"],
        "L1_gnn_b1": a["L1_gnn_b1"].reshape(len(GROUPS), 2, P).transpose(2, 0, 1),
        "L1_gnn_b2": slot_b2, "L1_gnn_fusion_w": a["L1_gnn_fusion_w"].reshape(1, -1),
        "c_slot_group": slot_group, "c_pick": pick, "c_spread": pick.T,
        "L1_ffn_route_id": a["L1_ffn_route_id"].reshape(1, T),
        "c_hex_digits": (float(ROUTES) ** np.arange(D_WAYS)).astype(np.float32).reshape(1, D_WAYS),
        "L1_ffn_Wr": a["L1_ffn_Wr"].reshape(LAYERS, ROUTES, MID, 2, P).transpose(4, 0, 1, 3, 2),
        "L1_ffn_Ws": a["L1_ffn_Ws"].reshape(LAYERS, MID, 2, P).transpose(3, 0, 2, 1),
        "c_eye2": np.eye(MID, dtype=np.float32).reshape(2, P, MID).transpose(1, 0, 2),
        "L1_ffn_br": a["L1_ffn_br"].reshape(1, -1), "L1_ffn_bs": a["L1_ffn_bs"].reshape(1, -1),
        "L1_ffn_Wi": a["L1_ffn_Wi"].T, "L1_ffn_bi": a["L1_ffn_bi"].reshape(2, P).T,
        "L1_ffn_Wo": a["L1_ffn_Wo"].reshape(D, 2, P).transpose(2, 1, 0), "L1_ffn_bo": a["L1_ffn_bo"].reshape(1, D),
        "L2_gnn_W1": a["L2_gnn_W1"].T, "L2_gnn_W2": a["L2_gnn_W2"].T, "L2_gnn_w3": a["L2_gnn_w3"].reshape(2, P).T,
        "c_ident": np.eye(P, dtype=np.float32),
        "c_tri": np.triu(np.ones((P, P), np.float32)),
        "c_digits": (float(E) ** np.arange(2 * WAYS)).astype(np.float32).reshape(1, 2 * WAYS),
        "c_ones": np.ones((P, P), np.float32),
        "c_steps": (np.arange(T, dtype=np.float32) * P).reshape(1, T),
        "c_tile_no": np.arange(2 * T + SPARE, dtype=np.float32).reshape(1, -1),
        "c_places": (np.arange(P)[:, None, None] + np.arange(T)[None, :, None] * P
                     + np.arange(2)[None, None, :] * TOKENS).astype(np.uint32),
        "L0_ffn_gate": a["L0_ffn_gate_w"],
        "L0_ffn_gate_b": a["L0_ffn_gate_b"].reshape(1, E),
        "L0_ffn_up": a["L0_ffn_w1"],
        "L0_ffn_b_up": a["L0_ffn_b1"].reshape(1, -1),
        "L0_ffn_down": a["L0_ffn_w2"],
        "L0_ffn_b_down": a["L0_ffn_b2"].reshape(1, -1),
        "L2_ffn_gate": a["L2_ffn_router_w"].T,
        "L2_ffn_up": a["L2_ffn_w1"].transpose(0, 2, 1),
        "L2_ffn_up3": a["L2_ffn_w3"].transpose(0, 2, 1),
        "L2_ffn_down": a["L2_ffn_w2"].transpose(0, 2, 1),
        "L3_ffn_gate": a["L3_ffn_Wr"],
        "L3_ffn_gate_b": a["L3_ffn_br"].reshape(1, E),
        "L3_ffn_gamma": a["L3_ffn_gamma"].reshape(1, D),
        "L3_ffn_beta": a["L3_ffn_beta"].reshape(1, D),
        "L3_ffn_up": a["L3_ffn_W1"],
        "L3_ffn_b_up": a["L3_ffn_b1"].reshape(1, -1),
        "L3_ffn_down": a["L3_ffn_W2"],
        "L3_ffn_b_down": a["L3_ffn_b2"].reshape(1, -1),
    }
    nc = bacc.Bacc("TRN2", target_bir_lowering=False, num_devices=1)
    arrays, g_in = {}, {}
    for name, v in lay.items():
        v = np.ascontiguousarray(v)
        arrays[f"in_{name}"] = v
        g_in[name] = nc.dram_tensor(f"in_{name}", v.shape, mybir.dt.from_np(v.dtype), kind="ExternalInput").ap()
    out = nc.dram_tensor("out_x", (TOKENS, D), F32, kind="ExternalOutput").ap()
    program(nc, g_in, out)
    r = run_bass_kernel_spmd(nc, [arrays], core_ids=[0])
    return r.results[0]["out_x"].reshape(128, NODES, D)
```
